# Optimizing a Trainium2 kernel written in Bass

```python
import numpy as np
import jax
import jax.numpy as jnp

def _softmax(x, axis=-1):
    return jax.nn.softmax(x, axis=axis)

def _gelu(x):
    return jax.nn.gelu(x, approximate=True)

def _silu(x):
    return jax.nn.silu(x)

def _sigmoid(x):
    return jax.nn.sigmoid(x)

def _layernorm(x, axis=-1, eps=1e-05):
    m = jnp.mean(x, axis=axis, keepdims=True)
    v = jnp.var(x, axis=axis, keepdims=True)
    return (x - m) / jnp.sqrt(v + eps)

def _scatter_add(tgt, idx, src, axis=0):
    return tgt.at[idx].add(src)

def _segment_sum(src, seg, n):
    return jax.ops.segment_sum(src, seg, n)
kernel_name = 'mk_hybrid_d1_jaxref_r8_ed8d17'

def setup_inputs(seed: int=0):
    np.random.seed(seed)
    _w = jnp.asarray

    def _L0_attn_a_setup():
        import jax, jax.numpy as jnp
        import numpy as np
        B, S, HID = (2, 512, 128)
        NH, HD, W = (16, 64, 128)
        ROPE_THETA = 10000.0

        def _apply_rope(x):
            s, d = (x.shape[2], x.shape[3])
            pos = jnp.arange(s, dtype=jnp.float32)
            inv_freq = 1.0 / ROPE_THETA ** (jnp.arange(0, d, 2, dtype=jnp.float32) / d)
            ang = pos[:, None] * inv_freq[None, :]
            cos = jnp.tile(jnp.cos(ang), (1, 2))[None, None]
            sin = jnp.tile(jnp.sin(ang), (1, 2))[None, None]
            x1, x2 = jnp.split(x, 2, axis=-1)
            rot = jnp.concatenate([-x2, x1], axis=-1)
            return x * cos + rot * sin
        key = jax.random.key(seed)
        ks = jax.random.split(key, 9)
        sc = 0.02
        return {'hidden_states': jax.random.normal(ks[0], (B, S, HID), dtype=jnp.float32), 'Wq': jax.random.normal(ks[1], (NH * HD, HID), dtype=jnp.float32) * sc, 'bq': jnp.zeros((NH * HD,), dtype=jnp.float32), 'Wk': jax.random.normal(ks[2], (NH * HD, HID), dtype=jnp.float32) * sc, 'bk': jnp.zeros((NH * HD,), dtype=jnp.float32), 'Wv': jax.random.normal(ks[3], (NH * HD, HID), dtype=jnp.float32) * sc, 'bv': jnp.zeros((NH * HD,), dtype=jnp.float32), 'Wo': jax.random.normal(ks[4], (HID, NH * HD), dtype=jnp.float32) * sc, 'bo': jnp.zeros((HID,), dtype=jnp.float32)}
    _L0_attn_a_in = _L0_attn_a_setup()

    def _L0_attn_b_setup():
        import jax, jax.numpy as jnp
        import numpy as np
        B, S, D_MODEL, D_K = (4, 256, 128, 1)
        D_QKV = D_MODEL * D_K
        MASK_NEG = -9000000000000000.0

        def _scaled_dot_product_attention(q, k, v):
            d_k = k.shape[-1]
            scores = jnp.einsum('bqd,bkd->bqk', q, k) / jnp.sqrt(jnp.float32(d_k))
            scores = jnp.triu(scores, k=0)
            scores = jnp.where(scores == 0, MASK_NEG, scores)
            attn = jax.nn.softmax(scores, axis=-1)
            return jnp.einsum('bqk,bkd->bqd', attn, v)
        key = jax.random.key(seed)
        kx, kw = jax.random.split(key)
        x = jax.random.normal(kx, (B, S, D_MODEL), dtype=jnp.float32)
        W = jax.random.normal(kw, (D_MODEL, 3 * D_QKV), dtype=jnp.float32) * (1.0 / np.sqrt(D_MODEL))
        return {'x': x, 'W': W}
    _L0_attn_b_in = _L0_attn_b_setup()

    def _L0_ffn_setup():
        import jax, jax.numpy as jnp
        import numpy as np
        EMBED_DIM = 128
        HIDDEN_DIM = 512
        NUM_EXPERTS = 8
        TOP_K = 2
        key = jax.random.key(seed)
        ks = jax.random.split(key, 4)
        std1 = float(np.sqrt(2.0 / EMBED_DIM))
        std2 = float(np.sqrt(2.0 / HIDDEN_DIM))
        x = jax.random.normal(ks[0], (1, 256, EMBED_DIM), dtype=jnp.float32)
        w_router = jax.random.normal(ks[1], (EMBED_DIM, NUM_EXPERTS), dtype=jnp.float32) * 0.02
        w1 = jax.random.normal(ks[2], (NUM_EXPERTS, EMBED_DIM, HIDDEN_DIM), dtype=jnp.float32) * std1
        b1 = jnp.zeros((NUM_EXPERTS, HIDDEN_DIM), dtype=jnp.float32)
        w2 = jax.random.normal(ks[3], (NUM_EXPERTS, HIDDEN_DIM, EMBED_DIM), dtype=jnp.float32) * std2
        b2 = jnp.zeros((NUM_EXPERTS, EMBED_DIM), dtype=jnp.float32)
        return {'x': x, 'w_router': w_router, 'w1': w1, 'b1': b1, 'w2': w2, 'b2': b2}
    _L0_ffn_in = _L0_ffn_setup()
    _d = {'L0_attn_a_hidden_states': _L0_attn_a_in['hidden_states'], 'L0_attn_a_Wq': _L0_attn_a_in['Wq'], 'L0_attn_a_bq': _L0_attn_a_in['bq'], 'L0_attn_a_Wk': _L0_attn_a_in['Wk'], 'L0_attn_a_bk': _L0_attn_a_in['bk'], 'L0_attn_a_Wv': _L0_attn_a_in['Wv'], 'L0_attn_a_bv': _L0_attn_a_in['bv'], 'L0_attn_a_Wo': _L0_attn_a_in['Wo'], 'L0_attn_a_bo': _L0_attn_a_in['bo'], 'L0_attn_b_W': _L0_attn_b_in['W'], 'L0_ffn_w_router': _L0_ffn_in['w_router'], 'L0_ffn_w1': _L0_ffn_in['w1'], 'L0_ffn_b1': _L0_ffn_in['b1'], 'L0_ffn_w2': _L0_ffn_in['w2'], 'L0_ffn_b2': _L0_ffn_in['b2']}
    _x0 = _d['L0_attn_a_hidden_states']
    _d['L0_attn_a_hidden_states'] = jax.random.normal(jax.random.fold_in(jax.random.key(seed), 1), (2, 2048, 128), dtype=_x0.dtype)
    del _x0
    return _d

def reference(L0_attn_a_hidden_states, L0_attn_a_Wq, L0_attn_a_bq, L0_attn_a_Wk, L0_attn_a_bk, L0_attn_a_Wv, L0_attn_a_bv, L0_attn_a_Wo, L0_attn_a_bo, L0_attn_b_W, L0_ffn_w_router, L0_ffn_w1, L0_ffn_b1, L0_ffn_w2, L0_ffn_b2):

    def _L0_attn_a_ref(hidden_states, Wq, bq, Wk, bk, Wv, bv, Wo, bo):
        import jax, jax.numpy as jnp
        import numpy as np
        B, S, HID = (2, 512, 128)
        NH, HD, W = (16, 64, 128)
        ROPE_THETA = 10000.0

        def _apply_rope(x):
            s, d = (x.shape[2], x.shape[3])
            pos = jnp.arange(s, dtype=jnp.float32)
            inv_freq = 1.0 / ROPE_THETA ** (jnp.arange(0, d, 2, dtype=jnp.float32) / d)
            ang = pos[:, None] * inv_freq[None, :]
            cos = jnp.tile(jnp.cos(ang), (1, 2))[None, None]
            sin = jnp.tile(jnp.sin(ang), (1, 2))[None, None]
            x1, x2 = jnp.split(x, 2, axis=-1)
            rot = jnp.concatenate([-x2, x1], axis=-1)
            return x * cos + rot * sin
        b, s, _ = hidden_states.shape

        def proj(Wm, bm):
            y = hidden_states @ Wm.T + bm
            return y.reshape(b, s, NH, HD).transpose(0, 2, 1, 3)
        q = _apply_rope(proj(Wq, bq))
        k = _apply_rope(proj(Wk, bk))
        v = proj(Wv, bv)
        nb = s // W
        qb = q.reshape(b, NH, nb, W, HD)
        kb = k.reshape(b, NH, nb, W, HD)
        vb = v.reshape(b, NH, nb, W, HD)
        zpad = jnp.zeros_like(kb[:, :, :1])
        kcat = jnp.concatenate([jnp.concatenate([zpad, kb[:, :, :-1]], axis=2), kb], axis=3)
        vcat = jnp.concatenate([jnp.concatenate([zpad, vb[:, :, :-1]], axis=2), vb], axis=3)
        scale = 1.0 / jnp.sqrt(jnp.asarray(HD, dtype=q.dtype))
        scores = jnp.einsum('bhnqd,bhnkd->bhnqk', qb, kcat) * scale
        qi = jnp.arange(W)[:, None]
        kj = jnp.arange(2 * W)[None, :]
        band = (kj >= qi) & (kj <= qi + W)
        nidx = jnp.arange(nb)[:, None, None]
        valid = band[None] & ((nidx > 0) | (kj[None] >= W))
        scores = jnp.where(valid[None, None], scores, jnp.asarray(-1e+30, scores.dtype))
        attn = jax.nn.softmax(scores, axis=-1)
        ctx = jnp.einsum('bhnqk,bhnkd->bhnqd', attn, vcat)
        merged = ctx.reshape(b, NH, s, HD).transpose(0, 2, 1, 3).reshape(b, s, NH * HD)
        return merged @ Wo.T + bo

    def _L0_attn_b_ref(x, W):
        import jax, jax.numpy as jnp
        import numpy as np
        B, S, D_MODEL, D_K = (4, 256, 128, 1)
        D_QKV = D_MODEL * D_K
        MASK_NEG = -9000000000000000.0

        def _scaled_dot_product_attention(q, k, v):
            d_k = k.shape[-1]
            scores = jnp.einsum('bqd,bkd->bqk', q, k) / jnp.sqrt(jnp.float32(d_k))
            scores = jnp.triu(scores, k=0)
            scores = jnp.where(scores == 0, MASK_NEG, scores)
            attn = jax.nn.softmax(scores, axis=-1)
            return jnp.einsum('bqk,bkd->bqd', attn, v)
        qkv = jnp.einsum('bsd,df->bsf', x, W)
        q, k, v = jnp.split(qkv, 3, axis=-1)
        return _scaled_dot_product_attention(q, k, v)

    def _L0_ffn_ref(x, w_router, w1, b1, w2, b2):
        import jax, jax.numpy as jnp
        import numpy as np
        EMBED_DIM = 128
        HIDDEN_DIM = 512
        NUM_EXPERTS = 8
        TOP_K = 2
        orig_shape = x.shape
        xf = x.reshape(-1, EMBED_DIM)
        logits = xf @ w_router
        probs = jax.nn.softmax(logits, axis=-1)
        topk_w, topk_idx = jax.lax.top_k(probs, TOP_K)
        mask = jax.nn.one_hot(topk_idx, NUM_EXPERTS, dtype=xf.dtype)
        weights = jnp.sum(topk_w[..., None] * mask, axis=1)
        h = jnp.einsum('te,ieh->tih', xf, w1) + b1
        h = jax.nn.gelu(h)
        out = jnp.einsum('tih,ihe->tie', h, w2) + b2
        out = jnp.sum(out * weights[..., None], axis=1)
        return out.reshape(orig_shape)
    x = L0_attn_a_hidden_states
    x = x + _L0_attn_a_ref(_layernorm(x, axis=-1), L0_attn_a_Wq, L0_attn_a_bq, L0_attn_a_Wk, L0_attn_a_bk, L0_attn_a_Wv, L0_attn_a_bv, L0_attn_a_Wo, L0_attn_a_bo)
    x = x + _L0_ffn_ref(_layernorm(x, axis=-1), L0_ffn_w_router, L0_ffn_w1, L0_ffn_b1, L0_ffn_w2, L0_ffn_b2)
    x = x + _L0_attn_b_ref(_layernorm(x, axis=-1), L0_attn_b_W)
    x = x + _L0_ffn_ref(_layernorm(x, axis=-1), L0_ffn_w_router, L0_ffn_w1, L0_ffn_b1, L0_ffn_w2, L0_ffn_b2)
    return x

_drawn_inputs = setup_inputs


def setup_inputs(seed=0):
    import zlib

    import numpy as np

    out = dict(_drawn_inputs(seed))
    spreads = {'L0_attn_a_bq': (0.0, 0.8),
     'L0_attn_a_bk': (0.0, 0.8),
     'L0_attn_a_bv': (0.0, 0.1),
     'L0_attn_a_bo': (0.0, 0.1),
     'L0_ffn_b1': (0.0, 0.1),
     'L0_ffn_b2': (0.0, 0.1)}
    factors = {'L0_attn_a_Wq': 6.215, 'L0_attn_a_Wk': 5.78}
    for name, (base, spread) in spreads.items():
        noise = np.random.default_rng([zlib.crc32(name.encode()), seed]).standard_normal(out[name].shape)
        drawn = base * np.exp(spread * noise) if base else spread * noise
        out[name] = jnp.asarray(drawn.astype(out[name].dtype))
    for name, factor in factors.items():
        out[name] = (out[name] * factor).astype(out[name].dtype)
    return out
```

```python
from contextlib import ExitStack

import concourse.bass as bass
from concourse import mybir

F32 = mybir.dt.float32
U32 = mybir.dt.uint32
I32 = mybir.dt.int32
ALU = mybir.AluOpType
ACT = mybir.ActivationFunctionType
AX_X = mybir.AxisListType.X

P = 128
BATCH, SEQ, HID = 2, 2048, 128
TILES = BATCH * SEQ // P
SB_TILES = 4
SB = SB_TILES * P
NSB = TILES // SB_TILES
SB_PER_BATCH = NSB // BATCH
EPS = 1e-5

HEADS, HD = 16, 64
CHUNKS = HEADS * HD // P
VCOLS = HD + 1
NEG = -1e30

EXPERTS, FFN, TOPK = 8, 512, 2
HCHUNKS = FFN // P
GROUP = 2 * P
GROUPS = TILES * P * TOPK // GROUP + EXPERTS
ZERO_DMAS = 10

MASKED = 2.0 ** 53
BTILES = SEQ // P


START = 1


class Memory:

    def __init__(self, nc, ctx):
        self.nc, self.ctx = nc, ctx

    def sb(self, name, shape, dt=F32):
        return self.ctx.enter_context(self.nc.sbuf_tensor(name, shape, dt))

    def psum(self, name, shape, dt=F32):
        return self.ctx.enter_context(self.nc.psum_tensor(name, shape, dt))

    def sem(self, name):
        return self.ctx.enter_context(self.nc.semaphore(name))


class Chain:

    def __init__(self, eng, sem):
        self.eng, self.sem, self.base, self.n = eng, sem, 0, 0

    def enter(self, start, i, per):
        self.base, self.n = start + i * per, 0

    def mark(self, ins):
        self.n += 1
        return ins.then_inc(self.sem, 1)

    def wait(self):
        self.eng.wait_ge(self.sem, START + self.base + self.n)

    def link(self, ins):
        self.mark(ins)
        self.wait()


def stand_alone(eng, s):
    eng.sem_inc(s.s_passed, 1)


def set_up(nc, signals):
    with nc.Block() as block:

        @block.sync
        def _(sp):
            for sem in signals.values():
                sp.sem_inc(sem, START)


def norm_stage(nc, sems, tag, s, first=False, router=False):
    with ExitStack() as ctx:
        m = Memory(nc, ctx)
        stats = m.sb(f"stats{tag}", [P, TILES, 6])
        mean = m.sb(f"mean{tag}", [P, TILES])
        rstd = m.sb(f"rstd{tag}", [P, TILES])
        tmp = m.sb(f"tmp{tag}", [P, 5, TILES])
        xn = m.sb(f"xn{tag}", [P, 2, SB_TILES, P])
        tp = m.psum(f"tp{tag}", [P, 2, SB])
        S = {n: sems.sem(f"n_{n}{tag}") for n in ("chain var std xn tp xs lg sh ex both cnt slot keep" if router else "chain var std xn tp xT").split()}
        put = sems.sem(f"n_put{tag}")
        if router:
            xs = m.sb(f"xs{tag}", [P, 2, SB])
            lg = m.psum(f"lg{tag}", [P, TILES, EXPERTS])
            sh = m.sb(f"sh{tag}", [P, TILES, EXPERTS])
            ex = m.sb(f"ex{tag}", [P, TILES, EXPERTS])
            pr = m.sb(f"pr{tag}", [P, TILES, EXPERTS])
            top = m.sb(f"top{tag}", [P, TILES, 8])
            ti = m.sb(f"ti{tag}", [P, TILES, 8], U32)
            tf = m.sb(f"tf{tag}", [P, TILES, 8])
            red = m.sb(f"red{tag}", [P, 3, TILES])
            hot = m.sb(f"hot{tag}", [P, TOPK, TILES, EXPERTS])
            both = m.sb(f"both{tag}", [P, TILES, EXPERTS])
            run = m.sb(f"run{tag}", [P, 2, TILES, EXPERTS])
            place = m.sb(f"place{tag}", [P, TILES, EXPERTS])
            few = m.sb(f"few{tag}", [P, 6, EXPERTS])
            fewi = m.sb(f"fewi{tag}", [P, 2, EXPERTS], I32)
            picked = m.sb(f"picked{tag}", [P, TOPK, TILES, EXPERTS])
            slotf = m.sb(f"slotf{tag}", [P, TOPK, TILES])
            past = m.sb(f"past{tag}", [P, GROUPS, EXPERTS])
            emf = m.sb(f"emf{tag}", [P, 2, GROUPS])
            cnt = m.psum(f"cnt{tag}", [P, 2, SB])
        set_up(nc, S)
        block = ctx.enter_context(nc.Block())

        @block.vector
        def _(dve):
            ch = Chain(dve, S["chain"])
            for t in range(TILES):
                if first and t % SB_TILES == 0:
                    dve.wait_ge(s.s_x[t // SB_TILES], 16)
                ins = nc.vector.bn_stats(stats[:, t, :], s.x[:, t, :])
            ch.link(ins)
            me, mo, ve, vo = stats[:, :, 1], stats[:, :, 4], stats[:, :, 2], stats[:, :, 5]
            ch.mark(nc.vector.tensor_tensor(tmp[:, 0, :], me, mo, ALU.add))
            ch.mark(nc.vector.tensor_tensor(tmp[:, 1, :], me, mo, ALU.subtract))
            ch.link(nc.vector.tensor_tensor(tmp[:, 2, :], ve, vo, ALU.add))
            ch.mark(nc.vector.tensor_scalar(mean[:, :], tmp[:, 0, :], 0.5, None, ALU.mult))
            ch.link(nc.vector.scalar_tensor_tensor(tmp[:, 3, :], tmp[:, 1, :], 0.25, tmp[:, 1, :],
                                                   ALU.mult, ALU.mult))
            ch.link(nc.vector.scalar_tensor_tensor(tmp[:, 4, :], tmp[:, 2, :], 1.0 / HID, tmp[:, 3, :],
                                                   ALU.mult, ALU.add))
            nc.vector.tensor_scalar(tmp[:, 0, :], tmp[:, 4, :], EPS, None, ALU.add).then_inc(S["var"], 1)
            dve.wait_ge(S["std"], START + 1)
            ch.link(nc.vector.reciprocal(rstd[:, :], tmp[:, 1, :]))
            with dve.Fori(0, NSB // 2) as j:
                for k in range(2):
                    i = 2 * j + k
                    dve.wait_ge(S["tp"], START + i)
                    if router:
                        dve.wait_ge(S["keep"], START + i)
                    for t in range(SB_TILES):
                        col = i * SB_TILES + t
                        ins = nc.vector.tensor_scalar(xn[:, k, t, :], s.x[:, col, :], mean[:, bass.ds(col, 1)],
                                                      rstd[:, bass.ds(col, 1)], ALU.subtract, ALU.mult)
                    ins.then_inc(S["xn"], 1)
            if not router:
                return
            dve.wait_ge(S["lg"], START + NSB)
            wide = [P, TILES, EXPERTS]
            ch.link(nc.vector.tensor_reduce(red[:, 0, :], lg[:, :, :], AX_X, ALU.max))
            nc.vector.tensor_tensor(sh[:, :, :], lg[:, :, :], red[:, 0, :].unsqueeze(2).to_broadcast(wide),
                                    ALU.subtract).then_inc(S["sh"], 1)
            dve.wait_ge(S["ex"], START + 1)
            ch.link(nc.vector.tensor_reduce(red[:, 1, :], ex[:, :, :], AX_X, ALU.add))
            ch.link(nc.vector.reciprocal(red[:, 2, :], red[:, 1, :]))
            ch.link(nc.vector.tensor_tensor(pr[:, :, :], ex[:, :, :],
                                            red[:, 2, :].unsqueeze(2).to_broadcast(wide), ALU.mult))
            for t in range(TILES):
                ins = nc.vector.max(top[:, t, :], pr[:, t, :])
            ch.link(ins)
            for t in range(TILES):
                ins = nc.vector.max_index(ti[:, t, :], top[:, t, :], pr[:, t, :])
            ch.link(ins)
            ch.link(nc.vector.tensor_copy(tf[:, :, :], ti[:, :, :]))
            nc_copy = nc.vector.tensor_copy
            for r in range(TOPK):
                ch.mark(nc.vector.tensor_tensor(hot[:, r, :, :], s.iota[:, :].unsqueeze(1).to_broadcast(wide),
                                                tf[:, :, r:r + 1].to_broadcast(wide), ALU.is_equal))
                ch.mark(nc_copy(s.pick[:, :, r:r + 1], top[:, :, r:r + 1]))
            ch.wait()
            nc.vector.tensor_tensor(both[:, :, :], hot[:, 0, :, :], hot[:, 1, :, :], ALU.add).then_inc(S["both"], 1)
            dve.wait_ge(S["cnt"], START + 1)
            before, inside = (cnt[:, r, 0:TILES * EXPERTS].rearrange("p (t e) -> p t e", e=EXPERTS) for r in range(2))
            ch.link(nc_copy(run[:, 0, :, :], inside))
            k, step = 0, 1
            while step < TILES:
                ch.mark(nc_copy(run[:, 1 - k, 0:step, :], run[:, k, 0:step, :]))
                ch.link(nc.vector.tensor_tensor(run[:, 1 - k, step:, :], run[:, k, step:, :],
                                                run[:, k, 0:TILES - step, :], ALU.add))
                k, step = 1 - k, 2 * step
            ch.link(nc.vector.tensor_scalar(fewi[:, 0, :], run[:, k, TILES - 1, :], float(GROUP - 1), None, ALU.add))
            ch.link(nc.vector.tensor_scalar(fewi[:, 1, :], fewi[:, 0, :], GROUP.bit_length() - 1, None,
                                            ALU.logical_shift_right))
            ch.link(nc_copy(few[:, 0, :], fewi[:, 1, :]))
            a, step = 0, 1
            while step < EXPERTS:
                ch.mark(nc_copy(few[:, a + 1, 0:step], few[:, a, 0:step]))
                ch.link(nc.vector.tensor_tensor(few[:, a + 1, step:], few[:, a, step:], few[:, a, 0:EXPERTS - step],
                                                ALU.add))
                a, step = a + 1, 2 * step
            ch.mark(nc.vector.tensor_tensor(few[:, 4, :], few[:, a, :], few[:, 0, :], ALU.subtract))
            tiles = [P, GROUPS, EXPERTS]
            ch.mark(nc.vector.tensor_tensor(past[:, :, :], s.tileno[:, :].unsqueeze(2).to_broadcast(tiles),
                                            few[:, a, :].unsqueeze(1).to_broadcast(tiles), ALU.is_ge))
            ch.link(nc.vector.tensor_tensor(place[:, :, :], run[:, k, :, :], inside, ALU.subtract))
            ch.mark(nc.vector.tensor_scalar(few[:, 5, :], few[:, 4, :], float(GROUP), None, ALU.mult))
            ch.mark(nc.vector.tensor_reduce(emf[:, 0, :], past[:, :, :], AX_X, ALU.add))
            ch.link(nc.vector.tensor_tensor(run[:, 1 - k, :, :], place[:, :, :], before, ALU.add))
            ch.mark(nc.vector.tensor_scalar(emf[:, 1, :], emf[:, 0, :], float(EXPERTS - 1), None, ALU.min))
            ch.link(nc.vector.tensor_tensor(place[:, :, :], run[:, 1 - k, :, :],
                                            few[:, 5, :].unsqueeze(1).to_broadcast(wide), ALU.add))
            ch.mark(nc_copy(s.emap[:, :], emf[:, 1, :]))
            for r in range(TOPK):
                ch.mark(nc.vector.tensor_tensor(picked[:, r, :, :], hot[:, r, :, :], place[:, :, :], ALU.mult))
            ch.wait()
            ch.link(nc.vector.tensor_reduce(slotf[:, :, :], picked[:, :, :, :], AX_X, ALU.add))
            nc_copy(s.slot[:, :, :], slotf[:, :, :]).then_inc(S["slot"], 1)

        @block.scalar
        def _(act):
            act.wait_ge(S["var"], START + 1)
            nc.scalar.activation(tmp[:, 1, :], tmp[:, 0, :], ACT.Sqrt).then_inc(S["std"], 1)
            with act.Fori(0, NSB // 2) as j:
                for k in range(2):
                    i = 2 * j + k
                    act.wait_ge(S["tp"], START + i + 1)
                    if router:
                        act.wait_ge(S["lg"], START + i)
                        nc.scalar.copy(xs[:, k, :], tp[:, k, :]).then_inc(S["xs"], 1)
                    else:
                        nc.scalar.copy(s.xT[:, bass.ts(i, SB)], tp[:, k, :]).then_inc(S["xT"], 1)
            if router:
                act.wait_ge(S["sh"], START + 1)
                nc.scalar.activation(ex[:, :, :], sh[:, :, :], ACT.Exp).then_inc(S["ex"], 1)

        @block.tensor
        def _(pe):
            pe.wait_ge(s.s_const, CONSTS)
            if router:
                pe.wait_ge(s.s_small, 16 * s.n_small)
            with pe.Fori(0, NSB // 2) as j:
                for k in range(2):
                    i = 2 * j + k
                    pe.wait_ge(S["xn"], START + i + 1)
                    pe.wait_ge(S["xs" if router else "xT"], START + i)
                    for t in range(SB_TILES):
                        ins = nc.tensor.transpose(tp[:, k, t * P:(t + 1) * P], xn[:, k, t, :], s.ident[:, :])
                    ins.then_inc(S["tp"], 1)
                    if router:
                        pe.wait_ge(S["xs"], START + i + 1)
                        for t in range(SB_TILES):
                            ins = nc.tensor.matmul(lg[:, i * SB_TILES + t, :], xs[:, k, t * P:(t + 1) * P],
                                                   s.w_router[:, :], start=True, stop=True)
                        ins.then_inc(S["lg"], 1)
            if router:
                pe.wait_ge(S["both"], START + 1)
                marks = both[:, :, :].rearrange("p t e -> p (t e)")
                nc.tensor.matmul(cnt[:, 0, 0:TILES * EXPERTS], s.before[:, :], marks, start=True, stop=True)
                nc.tensor.matmul(cnt[:, 1, 0:TILES * EXPERTS], s.ones[:, :], marks, start=True,
                                 stop=True).then_inc(S["cnt"], 1)

        if router:
            @block.gpsimd
            def _(pool):
                with pool.Fori(0, NSB // 2) as j:
                    for k in range(2):
                        i = 2 * j + k
                        pool.wait_ge(S["xn"], START + i + 1)
                        stand_alone(pool, s)
                        nc.gpsimd.tensor_copy(s.xn[:, bass.ts(i, SB_TILES), :], xn[:, k, :, :]).then_inc(S["keep"], 1)
                pool.wait_ge(S["keep"], START + NSB)
                pool.wait_ge(S["slot"], START + 1)
                pool.wait_ge(s.s_zeroed, 16 * ZERO_DMAS)
                rows = s.xg.rearrange("j p d -> (j p) d")
                for t in range(TILES):
                    for r in range(TOPK):
                        nc.gpsimd.indirect_dma_start(
                            out=rows, out_offset=bass.IndirectOffsetOnAxis(ap=s.slot[:, r, t:t + 1], axis=0),
                            in_=s.xn[:, t, :], in_offset=None).then_inc(put, 16)
                pool.wait_ge(put, 16 * TILES * TOPK)


def window_stage(nc, sems, s):
    with ExitStack() as ctx:
        m = Memory(nc, ctx)
        xs = m.sb("xs", [P, SB])
        Q = m.sb("Q", [P, CHUNKS, SB])
        K = m.sb("K", [P, CHUNKS, P + SB])
        V = m.sb("V", [P, CHUNKS, 1 + SB_TILES, 2, VCOLS])
        lin = m.sb("lin", [P, 2, SB])
        rot = m.sb("rot", [P, 2, SB])
        sc = m.sb("sc", [P, 2, 2, 2 * P])
        mx = m.sb("mx", [P, 2, 2])
        pT = m.sb("pT", [P, 2, 2, 2, P])
        rs = m.sb("rs", [P, 4])
        on = m.sb("on", [P, SB_TILES, P])
        oT = m.sb("oT", [P, SB])
        mask = m.sb("mask", [P, 2 * P])
        masks = m.sb("masks", [P, SB_PER_BATCH, 2 * P])
        mask0 = m.sb("mask0", [P, 2 * P])
        pj = m.psum("pj", [P, SB])
        ps = m.psum("ps", [P, 2, SB])
        pt = m.psum("pt", [P, 2, 2, 2, P])
        po = m.psum("po", [P, 2, SB])
        pout = m.psum("pout", [P, SB_TILES, P])

        names = ("mask xs q_ps k_ps v_ps q_sb k_sb v_sb q_sh k_sh q_cos k_cos q_rdy k_rdy k_prev v_prev "
                 "s max p t pt pv norm oT oT_sb out res mask0 chain pool").split()
        S = {n: sems.sem(f"a_{n}") for n in names}
        swap = [(w + 16) % 32 for w in range(32)]
        set_up(nc, S)
        block = ctx.enter_context(nc.Block())

        def units(sb, c):
            u = CHUNKS * sb + c
            return u, u + 2, (c + 2) % CHUNKS, (sb if c + 2 < CHUNKS else sb + 1)

        def pos(sb):
            return bass.ts(sb % SB_PER_BATCH, SB)

        @block.tensor
        def _(pe):
            def project_q(v, c, head=False):
                pe.wait_ge(S["v_sb"], START + v + CHUNKS)
                if not head:
                    pe.wait_ge(S["oT_sb"], START + v - 2)
                nc.tensor.matmul(pj[:, :], s.wq[:, c, :], xs[:, :], start=True, stop=True).then_inc(S["q_ps"], 1)

            def project_k(v, c):
                pe.wait_ge(S["q_sb"], START + v + 1)
                nc.tensor.matmul(pj[:, :], s.wk[:, c, :], xs[:, :], start=True, stop=True).then_inc(S["k_ps"], 1)

            def project_v(v, c):
                pe.wait_ge(S["k_sb"], START + v + 1)
                for t in range(SB_TILES):
                    ins = nc.tensor.matmul(pj[:, t * P:(t + 1) * P], xs[:, t * P:(t + 1) * P], s.wv[:, c, :],
                                           start=True, stop=True)
                ins.then_inc(S["v_ps"], 1)

            def scores(c, b, u, G, first=False):
                if b == 0:
                    pe.wait_ge(S["q_rdy"], START + u + 1)
                    pe.wait_ge(S["k_rdy"], START + u + 1 + CHUNKS)
                for h in range(2):
                    if not first:
                        pe.wait_ge(S["max"], START + 2 * G - 1 + h)
                    r = slice(h * HD, (h + 1) * HD)
                    ins = nc.tensor.matmul(ps[:, h, 0:2 * P], Q[r, c, b * P:(b + 1) * P], K[r, c, b * P:(b + 2) * P],
                                           start=True, stop=True)
                ins.then_inc(S["s"], 1)

            def transposes(b, G, first=False):
                pe.wait_ge(S["p"], START + 2 * G + 2)
                if not first:
                    pe.wait_ge(S["pt"], START + G - 1)
                for h in range(2):
                    for kb in range(2):
                        ins = nc.tensor.transpose(pt[:, b % 2, h, kb, :], sc[:, b % 2, h, kb * P:(kb + 1) * P],
                                                  s.ident[:, :])
                ins.then_inc(S["t"], 1)

            def values(c, b, u, G):
                pe.wait_ge(S["pt"], START + G + 1)
                if b == 0:
                    pe.wait_ge(S["v_sb"], START + u + 1 + CHUNKS)
                    pe.wait_ge(S["v_prev"], START + u + 1)
                if b == 0:
                    pe.wait_ge(S["norm"], START + 2 * u)
                for h in range(2):
                    for kb in range(2):
                        ins = nc.tensor.matmul(po[:, b // 2, (b % 2 * 2 + h) * VCOLS:(b % 2 * 2 + h + 1) * VCOLS], pT[:, b % 2, h, kb, :], V[:, c, b + kb, h, :],
                                               start=(kb == 0), stop=(kb == 1))
                ins.then_inc(S["pv"], 1)

            def turn_out(u):
                pe.wait_ge(S["norm"], START + 2 * u + 2)
                pe.wait_ge(S["v_sb"], START + u + 3 + CHUNKS)
                for t in range(SB_TILES):
                    ins = nc.tensor.transpose(pj[:, t * P:(t + 1) * P], on[:, t, :], s.ident[:, :])
                ins.then_inc(S["oT"], 1)

            def project_out(u, c, sb):
                if c == 0:
                    pe.wait_ge(S["res"], START + sb)
                    nc.tensor.matmul(pout[:, :, :].rearrange("p a b -> p (a b)"), s.ones[0:1, :], s.bo4[0:1, :],
                                     start=True, stop=False, skip_group_check=True)
                pe.wait_ge(S["oT_sb"], START + u + 1)
                for t in range(SB_TILES):
                    ins = nc.tensor.matmul(pout[:, t, :], oT[:, t * P:(t + 1) * P], s.wo[:, c, :],
                                           start=False, stop=(c == CHUNKS - 1), skip_group_check=True)
                ins.then_inc(S["out"], 1)

            pe.wait_ge(s.s_wqkvo, 64)
            pe.wait_ge(s.s_small, 16 * s.n_small)
            pe.sem_inc(S["oT"], CHUNKS)
            pe.wait_ge(S["xs"], START + 1)
            for v in range(2):
                project_q(v, v, head=True)
                project_k(v, v)
                project_v(v, v)
            scores(0, 0, 0, 0, first=True)
            scores(0, 1, 0, 1)
            transposes(0, 0, first=True)
            with pe.Fori(0, NSB) as sb:
                for c in range(CHUNKS):
                    u, v, vc, vsb = units(sb, c)
                    for b in range(SB_TILES):
                        G = SB_TILES * u + b
                        if b < 2:
                            scores(c, b + 2, u, G + 2)
                        else:
                            scores((c + 1) % CHUNKS, b - 2, u + 1, G + 2)
                        transposes((b + 1) % SB_TILES, G + 1)
                        if b == 0 and c > 0:
                            turn_out(u - 1)
                        if b == 1:
                            if vc == 0:
                                pe.wait_ge(S["xs"], START + vsb + 1)
                            project_q(v, vc)
                        if b == 2 and c > 0:
                            project_out(u - 1, c - 1, sb)
                        if b == 2:
                            project_k(v, vc)
                        if b == 3:
                            project_v(v, vc)
                        values(c, b, u, G)
                turn_out(CHUNKS * sb + CHUNKS - 1)
                project_out(CHUNKS * sb + CHUNKS - 1, CHUNKS - 1, sb)

        @block.scalar
        def _(act):
            def probabilities(b, G):
                act.wait_ge(S["max"], START + 2 * G + 2)
                for h in range(2):
                    nc.scalar.activation(sc[:, b % 2, h, :], sc[:, b % 2, h, :], ACT.Exp, scale=-1.0,
                                         bias=mx[:, b % 2, h:h + 1]).then_inc(S["p"], 1)

            def read_pt(b, G, first=False):
                act.wait_ge(S["t"], START + G + 1)
                if not first:
                    act.wait_ge(S["pv"], START + G - 1)
                nc.scalar.copy(pT[:, b % 2, :, :, :], pt[:, b % 2, :, :, :]).then_inc(S["pt"], 1)

            def read_q(v, c, v0=False):
                act.wait_ge(S["q_ps"], START + v + 1)
                if not v0:
                    act.wait_ge(S["q_rdy"], START + v)
                nc.scalar.activation(lin[:, 0, :], pj[:, :], ACT.Identity, bias=s.bq[:, c:c + 1]).then_inc(S["q_sb"], 1)

            def read_k(v, c, v0=False):
                act.wait_ge(S["k_ps"], START + v + 1)
                if not v0:
                    act.wait_ge(S["k_rdy"], START + v + CHUNKS)
                nc.scalar.activation(lin[:, 1, :], pj[:, :], ACT.Identity, bias=s.bk[:, c:c + 1]).then_inc(S["k_sb"], 1)

            def read_out(u, c):
                act.wait_ge(S["oT"], START + u + 1 + CHUNKS)
                act.wait_ge(S["out"], START + u)
                nc.scalar.activation(oT[:, :], pj[:, :], ACT.Identity, bias=s.bv[:, c:c + 1]).then_inc(S["oT_sb"], 1)

            act.wait_ge(s.s_small, 16 * s.n_small)
            for v in range(2):
                read_q(v, v, v0=(v == 0))
                read_k(v, v, v0=(v == 0))
            probabilities(0, 0)
            probabilities(1, 1)
            read_pt(0, 0, first=True)
            with act.Fori(0, NSB) as sb:
                for c in range(CHUNKS):
                    u, v, vc, vsb = units(sb, c)
                    for b in range(SB_TILES):
                        G = SB_TILES * u + b
                        probabilities((b + 2) % SB_TILES, G + 2)
                        read_pt((b + 1) % SB_TILES, G + 1)
                        if b == 0 and c > 0:
                            read_out(u - 1, c - 1)
                        if b == 1:
                            read_q(v, vc)
                        if b == 2:
                            read_k(v, vc)
                read_out(CHUNKS * sb + CHUNKS - 1, CHUNKS - 1)

        @block.vector
        def _(dve):
            ch = Chain(dve, S["chain"])

            def maxima(c, b, G, first=False):
                dve.wait_ge(S["s"], START + G + 1)
                if not first:
                    dve.wait_ge(S["t"], START + G - 1)
                stand_alone(dve, s)
                for h in range(2):
                    nc.vector.tensor_tensor_reduce(sc[:, b % 2, h, :], ps[:, h, 0:2 * P],
                                                   (mask0 if b == 0 else mask)[:, :], -float(HD) ** -0.5, 3e38,
                                                   ALU.add, ALU.min, mx[:, b % 2, h:h + 1]).then_inc(S["max"], 1)

            def turn(v, sb, which, src, w0):
                dve.wait_ge(S[src], START + v + 1)
                if not w0:
                    dve.wait_ge(S["q_rdy" if which == 0 else "k_rdy"], START + v + (CHUNKS if which else 0))
                stand_alone(dve, s)
                nc.vector.stream_shuffle(rot[:, which, :], lin[:, which, :], swap).then_inc(
                    S["q_sh" if which == 0 else "k_sh"], 1)
                nc.vector.tensor_tensor(lin[:, which, :], lin[:, which, :], s.cos[:, pos(sb)], ALU.mult).then_inc(
                    S["q_cos" if which == 0 else "k_cos"], 1)

            def keep_v(v, c):
                dve.wait_ge(S["v_ps"], START + v + 1)
                dve.wait_ge(S["v_prev"], START + v + 1)
                nc.vector.tensor_copy(V[:, c, 1:, :, 0:HD],
                                      pj[:, :].rearrange("p (t h d) -> p t h d", t=SB_TILES, h=2)).then_inc(S["v_sb"], 1)

            def normalise(u, b, G):
                dve.wait_ge(S["pv"], START + G + 1)
                pair = po[:, b // 2, 0:4 * VCOLS].rearrange("p (a d) -> p a d", a=4)
                ch.link(nc.vector.reciprocal(rs[:, :], pair[:, :, HD]))
                if b == 1:
                    dve.wait_ge(S["oT"], START + u + CHUNKS)
                nc.vector.tensor_tensor(
                    on[:, b - 1:b + 1, :].rearrange("p a (h d) -> p (a h) d", h=2),
                    pair[:, :, 0:HD],
                    rs[:, :].unsqueeze(2).to_broadcast([P, 4, HD]), ALU.mult).then_inc(S["norm"], 1)

            dve.wait_ge(s.s_rope, 32)
            nc.vector.memset(V[:, :, :, :, :], 1.0).then_inc(S["v_sb"], CHUNKS)
            dve.wait_ge(S["v_sb"], START + CHUNKS)
            dve.wait_ge(S["mask"], START + 3)
            ch.link(nc.vector.tensor_copy(mask0[:, :], masks[:, 0, :]))
            for v in range(2):
                turn(v, 0, 0, "q_sb", v == 0)
                turn(v, 0, 1, "k_sb", v == 0)
                keep_v(v, v)
            maxima(0, 0, 0, first=True)
            maxima(0, 1, 1, first=True)
            start = ch.base + ch.n
            with dve.Fori(0, NSB) as sb:
                ch.enter(start, sb, 2 * CHUNKS + 1)
                for c in range(CHUNKS):
                    u, v, vc, vsb = units(sb, c)
                    for b in range(SB_TILES):
                        G = SB_TILES * u + b
                        if b == 2 and c == CHUNKS - 1:
                            ch.link(nc.vector.tensor_copy(mask0[:, :], masks[:, (sb + 1) % SB_PER_BATCH, :]))
                        maxima(c, (b + 2) % SB_TILES, G + 2)
                        if b == 2:
                            turn(v, vsb, 0, "q_sb", False)
                        if b == 3:
                            turn(v, vsb, 1, "k_sb", False)
                            keep_v(v, vc)
                        if b % 2 == 1:
                            normalise(u, b, G)
                dve.wait_ge(S["out"], START + CHUNKS * (sb + 1))
                own = s.x[:, bass.ts(sb, SB_TILES), :]
                nc.vector.tensor_tensor(own, own, pout[:, :, :], ALU.add).then_inc(S["res"], 1)

        @block.sync
        def _(sp):
            sp.wait_ge(s.s_zeroed, 16 * ZERO_DMAS)

        @block.gpsimd
        def _(pool):
            ch = Chain(pool, S["pool"])
            nc.gpsimd.memset(masks[:, :, :], 0.0).then_inc(S["pool"], 1)
            nc.gpsimd.memset(K[:, :, :], 0.0).then_inc(S["k_rdy"], CHUNKS)
            pool.wait_ge(S["pool"], START + 1)
            nc.gpsimd.affine_select(out=masks[:, :, 0:P], in_=masks[:, :, 0:P], compare_op=ALU.is_ge, fill=NEG,
                                    base=0, pattern=[[0, SB_PER_BATCH], [1, P]], channel_multiplier=-1).then_inc(S["pool"], 1)
            nc.gpsimd.affine_select(out=masks[:, :, P:], in_=masks[:, :, P:], compare_op=ALU.is_ge, fill=NEG,
                                    base=0, pattern=[[0, SB_PER_BATCH], [-1, P]], channel_multiplier=1).then_inc(S["mask"], 1)
            pool.wait_ge(S["pool"], START + 2)
            pool.wait_ge(S["mask"], START + 1)
            nc.gpsimd.tensor_copy(mask[:, :], masks[:, 1, :]).then_inc(S["mask"], 1)
            nc.gpsimd.memset(masks[:, 0, 0:P], NEG).then_inc(S["mask"], 1)
            pool.wait_ge(s.s_rope, 32)
            nc.gpsimd.tensor_copy(xs[:, :], s.xT[:, 0:SB]).then_inc(S["xs"], 1)

            def rotate(v, c, sb, which):
                pool.wait_ge(S["q_sh" if which == 0 else "k_sh"], START + v + 1)
                stand_alone(pool, s)
                nc.gpsimd.tensor_tensor(rot[:, which, :], rot[:, which, :], s.sin[:, pos(sb)], ALU.mult).then_inc(S["pool"], 1)
                ch.n += 1
                ch.wait()
                pool.wait_ge(S["q_cos" if which == 0 else "k_cos"], START + v + 1)
                to = Q[:, c, :] if which == 0 else K[:, c, P:]
                nc.gpsimd.tensor_tensor(to, lin[:, which, :], rot[:, which, :], ALU.add).then_inc(
                    S["q_rdy" if which == 0 else "k_rdy"], 1)

            def unit(v, c, sb):
                pool.wait_ge(S["oT"], START + v + 1)
                pool.wait_ge(S["k_rdy"], START + v + CHUNKS)
                stand_alone(pool, s)
                nc.gpsimd.tensor_copy(K[:, c, 0:P], K[:, c, SB:]).then_inc(S["k_prev"], 1)
                pool.wait_ge(S["v_sb"], START + v + CHUNKS)
                stand_alone(pool, s)
                nc.gpsimd.tensor_copy(V[:, c, 0, :, :], V[:, c, SB_TILES, :, :]).then_inc(S["v_prev"], 1)
                rotate(v, c, sb, 0)
                pool.wait_ge(S["k_prev"], START + v + 1)
                rotate(v, c, sb, 1)

            ch.base = 2
            ch.n = 0
            for v in range(2):
                unit(v, v, 0)
            start = ch.base + ch.n
            with pool.Fori(0, NSB) as sb:
                ch.enter(start, sb, 2 * CHUNKS)
                for c in range(CHUNKS):
                    u, v, vc, vsb = units(sb, c)
                    if vc == 0:
                        pool.wait_ge(S["v_ps"], START + CHUNKS * (sb + 1))
                        stand_alone(pool, s)
                        nc.gpsimd.tensor_copy(xs[:, :], s.xT[:, bass.ts((sb + 1) % NSB, SB)]).then_inc(S["xs"], 1)
                    unit(v, vc, vsb)


def expert_stage(nc, sems, tag, s):
    with ExitStack() as ctx:
        m = Memory(nc, ctx)
        xt = m.sb(f"xt{tag}", [P, 4, GROUP // P, P])
        xgT = m.sb(f"xgT{tag}", [P, 2, GROUP])
        w1s = m.sb(f"w1s{tag}", [P, 2, FFN])
        w2s = m.sb(f"w2s{tag}", [P, 2, HCHUNKS, P])
        hT = m.sb(f"hT{tag}", [P, 2, HCHUNKS, GROUP])
        yT = m.sb(f"yT{tag}", [P, 2, GROUP])
        yo = m.sb(f"yo{tag}", [P, 2, GROUP // P, P])
        got = m.sb(f"got{tag}", [P, TILES, TOPK, P])
        px = m.psum(f"px{tag}", [P, SB])
        ph = m.psum(f"ph{tag}", [P, 2, HCHUNKS, GROUP])
        py = m.psum(f"py{tag}", [P, 2, SB])
        pz = m.psum(f"pz{tag}", [P, SB])
        S = {n: sems.sem(f"e_{n}{tag}") for n in "t xT w1 w2 h gelu y yT z yo chain".split()}
        PARTS = 4
        load = [sems.sem(f"e_load{k}{tag}") for k in range(4)]
        stored = [sems.sem(f"e_stored{k}{tag}") for k in range(2)]
        gathered = [sems.sem(f"e_got{g}{tag}") for g in range(PARTS)]
        set_up(nc, S)
        block = ctx.enter_context(nc.Block())
        STEP = 4
        ROUNDS = GROUPS // STEP

        def steps(eng, body, ahead=None):
            def turn(jj):
                es = []
                if ahead is not None:
                    es = [expert(eng, STEP * jj + a) for a in range(STEP + ahead)
                          if not isinstance(jj, int) or STEP * jj + a < GROUPS]
                for k in range(STEP):
                    body(jj, k, *([es[k:]] if es else []))

            turn(0)
            with eng.Fori(0, ROUNDS - 2) as i:
                turn(i + 1)
            turn(ROUNDS - 1)

        def outside(jj, k, ahead):
            return isinstance(jj, int) and not 0 <= STEP * jj + k + ahead < GROUPS

        def expert(eng, j):
            return eng.value_load(s.emap[0:1, bass.ds(j, 1)], min_val=0, max_val=EXPERTS - 1)

        def rows(dram, j):
            return dram[j, :, :].rearrange("(p r) d -> p r d", r=GROUP // P)

        @block.sync
        def _(sp):
            def fetch(j, k):
                sp.dma_start(xt[:, k, :, :], rows(s.xg, j)).then_inc(load[k], 16)

            def store(j, k):
                sp.wait_ge(S["yo"], START + j + 1)
                sp.dma_start(rows(s.yg, j), yo[:, k % 2, :, :]).then_inc(stored[k % 2], 16)

            def body(jj, k):
                j = STEP * jj + k
                if not outside(jj, k, STEP):
                    sp.wait_ge(S["t"], START + j + 1)
                    fetch(j + STEP, k)
                if not outside(jj, k, -1):
                    store(j - 1, k + 1)

            for k in range(STEP):
                fetch(k, k)
            steps(sp, body)
            store(GROUPS - 1, GROUPS - 1)
            for k in range(2):
                sp.wait_ge(stored[k], 16 * (GROUPS // 2))

        @block.tensor
        def _(pe):
            def turn(j, k, nth):
                pe.wait_ge(load[k % STEP], 16 * nth)
                for r in range(GROUP // P):
                    ins = nc.tensor.transpose(px[:, r * P:(r + 1) * P], xt[:, k % STEP, r, :], s.ident[:, :])
                ins.then_inc(S["t"], 1)

            def hidden(j, k):
                pe.wait_ge(S["xT"], START + j + 1)
                pe.wait_ge(S["w1"], START + j + 1)
                for i in range(HCHUNKS):
                    ins = nc.tensor.matmul(ph[:, k % 2, i, :], w1s[:, k % 2, i * P:(i + 1) * P], xgT[:, k % 2, :],
                                           start=True, stop=True)
                ins.then_inc(S["h"], 1)

            def turn_back(j, k):
                pe.wait_ge(S["yT"], START + j + 1)
                for r in range(GROUP // P):
                    ins = nc.tensor.transpose(pz[:, r * P:(r + 1) * P], yT[:, k % 2, r * P:(r + 1) * P], s.ident[:, :])
                ins.then_inc(S["z"], 1)

            def body(jj, k):
                j = STEP * jj + k
                if not outside(jj, k, 2):
                    pe.wait_ge(S["xT"], START + j + 2)
                    turn(j + 2, k + 2, jj + 1 + (k + 2) // STEP)
                if not outside(jj, k, 1):
                    if not outside(jj, k, -1):
                        pe.wait_ge(S["gelu"], START + HCHUNKS * j)
                    hidden(j + 1, k + 1)
                if not outside(jj, k, -1):
                    if not outside(jj, k, -2):
                        pe.wait_ge(S["yo"], START + j - 1)
                    turn_back(j - 1, k + 1)
                pe.wait_ge(S["gelu"], START + HCHUNKS * (j + 1))
                pe.wait_ge(S["w2"], START + j + 1)
                if not outside(jj, k, -2):
                    pe.wait_ge(S["yT"], START + j - 1)
                for i in range(HCHUNKS):
                    ins = nc.tensor.matmul(py[:, k % 2, 0:GROUP], w2s[:, k % 2, i, :], hT[:, k % 2, i, :],
                                           start=(i == 0), stop=(i == HCHUNKS - 1))
                ins.then_inc(S["y"], 1)

            turn(0, 0, 1)
            pe.wait_ge(S["xT"], START + 1)
            turn(1, 1, 1)
            hidden(0, 0)
            steps(pe, body)
            pe.wait_ge(S["yo"], START + GROUPS - 1)
            turn_back(GROUPS - 1, GROUPS - 1)

        @block.scalar
        def _(act):
            def read(j, k):
                act.wait_ge(S["t"], START + j + 1)
                nc.scalar.copy(xgT[:, k % 2, :], px[:, 0:GROUP]).then_inc(S["xT"], 1)

            def gelu(j, k, e):
                act.wait_ge(S["h"], START + j + 1)
                for i in range(HCHUNKS):
                    nc.scalar.activation(hT[:, k % 2, i, :], ph[:, k % 2, i, :], ACT.Gelu_apprx_tanh,
                                         bias=s.b1[:, bass.ds(e * HCHUNKS + i, 1)]).then_inc(S["gelu"], 1)

            def body(jj, k, es):
                j = STEP * jj + k
                if not outside(jj, k, 2):
                    act.wait_ge(S["h"], START + j + 1)
                    read(j + 2, k + 2)
                if not outside(jj, k, 1):
                    if not outside(jj, k, -1):
                        act.wait_ge(S["y"], START + j)
                    gelu(j + 1, k + 1, es[1])
                if not outside(jj, k, -2):
                    act.wait_ge(S["z"], START + j - 1)
                act.wait_ge(S["y"], START + j + 1)
                nc.scalar.activation(yT[:, k % 2, :], py[:, k % 2, 0:GROUP], ACT.Identity,
                                     bias=s.b2[:, bass.ds(es[0], 1)]).then_inc(S["yT"], 1)

            e = expert(act, 0)
            read(0, 0)
            read(1, 1)
            gelu(0, 0, e)
            steps(act, body, 1)

        @block.vector
        def _(dve):
            def first_weights(j, k, e):
                nc.vector.tensor_copy(w1s[:, k % 2, :], s.w1[:, e, :]).then_inc(S["w1"], 1)

            def second_weights(j, k, e):
                nc.vector.tensor_copy(w2s[:, k % 2, :, :], s.w2[:, e, :, :]).then_inc(S["w2"], 1)

            def keep(j, k):
                dve.wait_ge(S["z"], START + j + 1)
                nc.vector.tensor_copy(yo[:, k % 2, :, :], pz[:, 0:GROUP].rearrange("p (r d) -> p r d", d=P)).then_inc(
                    S["yo"], 1)

            def body(jj, k, es):
                j = STEP * jj + k
                if not outside(jj, k, 2):
                    dve.wait_ge(S["h"], START + j + 1)
                    first_weights(j + 2, k + 2, es[2])
                if not outside(jj, k, 1):
                    if not outside(jj, k, -1):
                        dve.wait_ge(S["y"], START + j)
                    second_weights(j + 1, k + 1, es[1])
                if not outside(jj, k, -1):
                    if not outside(jj, k, -3):
                        dve.wait_ge(stored[(k + 1) % 2], 16 * (2 * jj + (k - 1) // 2))
                    keep(j - 1, k + 1)

            dve.wait_ge(s.s_w1, 16)
            dve.wait_ge(s.s_w2, 16)
            e0, e1 = expert(dve, 0), expert(dve, 1)
            first_weights(0, 0, e0)
            first_weights(1, 1, e1)
            second_weights(0, 0, e0)
            steps(dve, body, 2)
            dve.wait_ge(stored[1], 16 * (GROUPS // 2 - 1))
            keep(GROUPS - 1, GROUPS - 1)
            ch = Chain(dve, S["chain"])
            for g in range(PARTS):
                dve.wait_ge(gathered[g], 16 * TOPK * TILES // PARTS)
                for r in range(TOPK):
                    for t in range(g * TILES // PARTS, (g + 1) * TILES // PARTS):
                        ins = nc.vector.scalar_tensor_tensor(s.x[:, t, :], got[:, t, r, :], s.pick[:, t, r:r + 1],
                                                             s.x[:, t, :], ALU.mult, ALU.add)
                    ch.link(ins)

        @block.gpsimd
        def _(pool):
            for k in range(2):
                pool.wait_ge(stored[k], 16 * (GROUPS // 2))
            outputs = s.yg.rearrange("j p d -> (j p) d")
            for t in range(TILES):
                for r in range(TOPK):
                    nc.gpsimd.indirect_dma_start(
                        out=got[:, t, r, :], out_offset=None, in_=outputs,
                        in_offset=bass.IndirectOffsetOnAxis(ap=s.slot[:, r, t:t + 1], axis=0)).then_inc(
                            gathered[t * PARTS // TILES], 16)


def full_stage(nc, sems, s):
    with ExitStack() as ctx:
        m = Memory(nc, ctx)
        xs = m.sb("bxs", [P, SEQ])
        qT = m.sb("qT", [P, SEQ])
        kT = m.sb("kT", [P, SEQ])
        V = m.sb("bV", [P, BTILES, HID + 1])
        U = m.sb("U", [P, 2, SEQ])
        tri = m.sb("tri", [P, P])
        st = m.sb("st", [P, 2, 4])
        pT = m.sb("bpT", [P, 2, 4, P])
        pre = m.sb("pre", [P, HID + 1])
        oo = m.sb("oo", [P, HID + 1])
        pp = m.psum("pp", [P, 2, SB])
        ps = m.psum("bps", [P, 2, SB])
        pt = m.psum("bpt", [P, 2, 4, P])
        po = m.psum("bpo", [P, 2, SB])
        S = {n: sems.sem(f"f_{n}") for n in
             "xs proj qk v ones s copy u bias p w0 t pt pv pre pre_sb o chain end tri".split()}
        set_up(nc, S)
        block = ctx.enter_context(nc.Block())
        chunks = [[(k, min(4, BTILES - k)) for k in range(i, BTILES, 4)] for i in range(BTILES)]
        first = [sum(len(c) for c in chunks[:i]) for i in range(BTILES + 1)]
        NCH = first[-1]
        MARKS = 4 * BTILES

        @block.tensor
        def _(pe):
            pe.wait_ge(s.s_wb, 16)
            with pe.Fori(0, BATCH) as b:
                pe.wait_ge(S["xs"], START + b + 1)
                for a in range(12):
                    if a >= 2:
                        k = min(a - 1, 8)
                        pe.wait_ge(S["qk"], START + 8 * b + k)
                        if a - 1 > 8:
                            pe.wait_ge(S["v"], START + 4 * b + a - 9)
                    if a < 2:
                        pe.wait_ge(S["pre_sb"], START + (BTILES - 1) * b)
                    sl = slice(a % 4 * SB, (a % 4 + 1) * SB)
                    if a < 8:
                        w = s.wb[:, HID:2 * HID] if a < 4 else s.wb[:, 0:HID]
                        ins = nc.tensor.matmul(pp[:, a % 2, :], w, xs[:, sl], start=True, stop=True)
                    else:
                        for t in range(SB_TILES):
                            g = a % 4 * SB_TILES + t
                            ins = nc.tensor.matmul(pp[:, a % 2, t * P:(t + 1) * P], xs[:, g * P:(g + 1) * P],
                                                   s.wb[:, 2 * HID:], start=True, stop=True)
                    ins.then_inc(S["proj"], 1)
                pe.wait_ge(S["qk"], START + 8 * (b + 1))

                def scores(i, c):
                    g = first[i] + c
                    k0, n = chunks[i][c]
                    pe.wait_ge(S["copy"], START + NCH * b + max(g - 1, 0))
                    nc.tensor.matmul(ps[:, g % 2, 0:n * P], qT[:, i * P:(i + 1) * P], kT[:, k0 * P:(k0 + n) * P],
                                     start=True, stop=True).then_inc(S["s"], 1)

                def turn(i, c):
                    g = first[i] + c
                    k0, n = chunks[i][c]
                    pe.wait_ge(S["p"], START + NCH * b + g + 1)
                    pe.wait_ge(S["pt"], START + NCH * b + max(g - 1, 0))
                    for t in range(n):
                        off = (k0 - i + t) * P
                        ins = nc.tensor.transpose(pt[:, g % 2, t, :], U[:, i % 2, off:off + P], s.ident[:, :])
                    ins.then_inc(S["t"], 1)

                def values(i, c):
                    g = first[i] + c
                    k0, n = chunks[i][c]
                    pe.wait_ge(S["pt"], START + NCH * b + g + 1)
                    if c == 0:
                        pe.wait_ge(S["o"], START + BTILES * b + max(i - 1, 0))
                    for t in range(n):
                        ins = nc.tensor.matmul(po[:, i % 2, 0:HID + 1], pT[:, g % 2, t, :], V[:, k0 + t, :],
                                               start=(c == 0 and t == 0), stop=(k0 + t == BTILES - 1))
                    ins.then_inc(S["pv"], 1)

                for c in range(len(chunks[0])):
                    scores(0, c)
                pe.wait_ge(S["v"], START + 4 * (b + 1))
                for i in range(BTILES):
                    ahead = len(chunks[i + 1]) if i + 1 < BTILES else 0
                    if i > 0:
                        pe.wait_ge(S["pre_sb"], START + (BTILES - 1) * b + max(i - 2, 0))
                        nc.tensor.matmul(pp[:, i % 2, 0:HID + 1], s.ones[:, :], V[:, i - 1, :], start=True,
                                         stop=True).then_inc(S["pre"], 1)
                    for c in range(max(len(chunks[i]), ahead)):
                        if c < ahead:
                            scores(i + 1, c)
                        if c < len(chunks[i]):
                            turn(i, c)
                            if c > 0:
                                values(i, c - 1)
                    values(i, len(chunks[i]) - 1)

        def read(act, b, i, c):
            g = first[i] + c
            n = chunks[i][c][1]
            act.wait_ge(S["t"], START + NCH * b + g + 1)
            act.wait_ge(S["pv"], START + NCH * b + max(g - 1, 0))
            nc.scalar.copy(pT[:, g % 2, 0:n, :], pt[:, g % 2, 0:n, :]).then_inc(S["pt"], 1)

        @block.scalar
        def _(act):
            with act.Fori(0, BATCH) as b:
                for a in range(8):
                    act.wait_ge(S["proj"], START + 12 * b + a + 1)
                    if a == 0:
                        act.wait_ge(S["pv"], START + NCH * b)
                    sl = slice(a % 4 * SB, (a % 4 + 1) * SB)
                    if a < 4:
                        ins = nc.scalar.copy(kT[:, sl], pp[:, a % 2, :])
                    else:
                        ins = nc.scalar.mul(qT[:, sl], pp[:, a % 2, :], float(HID) ** -0.5 / MASKED)
                    ins.then_inc(S["qk"], 1)

                def take(i, c):
                    g = first[i] + c
                    k0, n = chunks[i][c]
                    act.wait_ge(S["s"], START + NCH * b + g + 1)
                    if c == 0:
                        act.wait_ge(S["t"], START + NCH * b + (first[i - 1] if i > 0 else 0))
                    nc.scalar.copy(U[:, i % 2, (k0 - i) * P:(k0 - i + n) * P], ps[:, g % 2, 0:n * P]).then_inc(S["copy"], 1)

                for c in range(len(chunks[0])):
                    take(0, c)
                for i in range(BTILES):
                    bias = st[:, i % 2, 1:2]
                    ahead = len(chunks[i + 1]) if i + 1 < BTILES else 0
                    for c in range(max(len(chunks[i]), ahead)):
                        if c < ahead:
                            take(i + 1, c)
                        if c == 0:
                            act.wait_ge(S["bias"], START + BTILES * b + i + 1)
                            nc.scalar.activation(st[:, i % 2, 2:3], s.ones[:, 0:1], ACT.Exp, scale=-MASKED,
                                                 bias=bias).then_inc(S["w0"], 1)
                        if c < len(chunks[i]):
                            k0, n = chunks[i][c]
                            sl = U[:, i % 2, (k0 - i) * P:(k0 - i + n) * P]
                            nc.scalar.activation(sl, sl, ACT.Exp, scale=-MASKED, bias=bias).then_inc(S["p"], 1)
                            if c > 0:
                                read(act, b, i, c - 1)
                    read(act, b, i, len(chunks[i]) - 1)

        @block.vector
        def _(dve):
            ch = Chain(dve, S["chain"])
            nc.vector.memset(V[:, :, HID:], 1.0).then_inc(S["ones"], 1)
            dve.wait_ge(S["tri"], START + 2)
            with dve.Fori(0, BATCH) as b:
                ch.enter(0, b, MARKS)
                dve.wait_ge(S["proj"], START + 12 * b)
                nc.vector.tensor_copy(xs[:, :], s.xT[:, bass.ts(b, SEQ)]).then_inc(S["xs"], 1)
                for a in range(8, 12):
                    dve.wait_ge(S["proj"], START + 12 * b + a + 1)
                    if a == 8:
                        dve.wait_ge(S["pv"], START + NCH * b)
                        dve.wait_ge(S["pre"], START + (BTILES - 1) * b)
                    g = a % 4 * SB_TILES
                    nc.vector.tensor_copy(V[:, g:g + SB_TILES, 0:HID],
                                          pp[:, a % 2, :].rearrange("p (t d) -> p t d", t=SB_TILES)).then_inc(S["v"], 1)

                def take(i):
                    dve.wait_ge(S["w0"], START + BTILES * b + max(i - 1, 0))
                    for c, (k0, n) in enumerate(chunks[i]):
                        g = first[i] + c
                        dve.wait_ge(S["copy"], START + NCH * b + g + 1)
                        to = U[:, i % 2, (k0 - i) * P:(k0 - i + n) * P]
                        if c == 0:
                            ch.link(nc.vector.tensor_tensor(to[:, 0:P], to[:, 0:P], tri[:, :], ALU.mult))
                        nc.vector.scalar_tensor_tensor(to, to, 0.0, to, ALU.is_equal, ALU.subtract).then_inc(S["u"], 1)
                    dve.wait_ge(S["u"], START + NCH * b + first[i + 1])
                    ch.link(nc.vector.tensor_reduce(st[:, i % 2, 0:1], U[:, i % 2, 0:(BTILES - i) * P], AX_X, ALU.min))
                    nc.vector.tensor_scalar(st[:, i % 2, 1:2], st[:, i % 2, 0:1], MASKED, None,
                                            ALU.mult).then_inc(S["bias"], 1)

                def finish(i):
                    if i > 0:
                        dve.wait_ge(S["pre"], START + (BTILES - 1) * b + i)
                        if i == 1:
                            nc.vector.tensor_copy(pre[:, :], pp[:, i % 2, 0:HID + 1]).then_inc(S["pre_sb"], 1)
                        else:
                            nc.vector.tensor_tensor(pre[:, :], pre[:, :], pp[:, i % 2, 0:HID + 1],
                                                    ALU.add).then_inc(S["pre_sb"], 1)
                        dve.wait_ge(S["pre_sb"], START + (BTILES - 1) * b + i)
                    dve.wait_ge(S["pv"], START + NCH * b + first[i + 1])
                    if i > 0:
                        dve.wait_ge(S["w0"], START + BTILES * b + i + 1)
                        ins = nc.vector.scalar_tensor_tensor(oo[:, :], pre[:, :], st[:, i % 2, 2:3],
                                                             po[:, i % 2, 0:HID + 1], ALU.mult, ALU.add)
                    else:
                        ins = nc.vector.tensor_copy(oo[:, :], po[:, 0, 0:HID + 1])
                    ins.then_inc(S["o"], 1)
                    dve.wait_ge(S["o"], START + BTILES * b + i + 1)
                    ch.link(nc.vector.reciprocal(st[:, i % 2, 3:4], oo[:, HID:]))
                    own = s.x[:, b * BTILES + i, :]
                    ch.mark(nc.vector.scalar_tensor_tensor(own, oo[:, 0:HID], st[:, i % 2, 3:4], own,
                                                           ALU.mult, ALU.add))

                take(0)
                for i in range(BTILES):
                    if i + 1 < BTILES:
                        take(i + 1)
                    finish(i)
                assert ch.n == 4 * BTILES

        @block.gpsimd
        def _(pool):
            nc.gpsimd.memset(tri[:, :], 1.0).then_inc(S["tri"], 1)
            pool.wait_ge(S["tri"], START + 1)
            nc.gpsimd.affine_select(out=tri[:, :], in_=tri[:, :], compare_op=ALU.is_ge, fill=0.0, base=0,
                                    pattern=[[1, P]], channel_multiplier=-1).then_inc(S["tri"], 1)



CONSTS = 2


class Shared:
    pass


def bass_hybrid(nc, hidden, wq, wk, wv, wo, bq, bk, bv, bo4, wb, w_router, w1, b1, w2, b2, cos, sin, out, stages=5):
    with ExitStack() as ctx:
        m = Memory(nc, ctx)
        s = Shared()
        s.x = m.sb("x", [P, TILES, HID])
        s.xT = m.sb("xT", [P, TILES * P])
        s.xn = s.xT[:, :].rearrange("p (t d) -> p t d", d=HID)
        s.pick = m.sb("pick", [P, TILES, TOPK])
        s.slot = m.sb("slot", [P, TOPK, TILES], U32)
        s.emap = m.sb("emap", [P, GROUPS], I32)
        s.tileno = m.sb("tileno", [P, GROUPS])
        s.before = m.sb("before", [P, P])
        s.xg = nc.dram_tensor("xg", [GROUPS, GROUP, HID], F32, kind="Internal").ap()
        s.yg = nc.dram_tensor("yg", [GROUPS, GROUP, HID], F32, kind="Internal").ap()
        s.w1 = m.sb("w1", [P, EXPERTS, FFN])
        s.w2 = m.sb("w2", [P, EXPERTS, HCHUNKS, HID])
        s.b1 = m.sb("b1", [P, EXPERTS * HCHUNKS])
        s.b2 = m.sb("b2", [P, EXPERTS])
        s.w_router = m.sb("w_router", [P, EXPERTS])
        s.wb = m.sb("wb", [P, 3 * HID])
        s.ident = m.sb("ident", [P, P])
        s.ones = m.sb("ones", [P, P])
        s.zero = m.sb("zero", [P, 1])
        s.iota = m.sb("iota", [P, EXPERTS])
        s.bq, s.bk, s.bv = (m.sb(n, [P, CHUNKS]) for n in ("bq", "bk", "bv"))
        s.bo4 = m.sb("bo4", [1, SB])
        s.s_x = [m.sem(f"s_x{i}") for i in range(NSB)]
        s.s_const, s.s_small, s.s_wqkvo, s.s_rope, s.s_w1, s.s_w2, s.s_wb, s_out = (
            m.sem(n) for n in "s_const s_small s_wqkvo s_rope s_w1 s_w2 s_wb s_out".split())
        s.s_passed = m.sem("s_passed")
        small = [(s.bq, bq), (s.bk, bk), (s.bv, bv), (s.bo4, bo4), (s.b1, b1), (s.b2, b2), (s.w_router, w_router)]
        s.n_small = len(small)
        s.s_zero, s.s_zeroed, s.s_count = (m.sem(n) for n in ("s_zero", "s_zeroed", "s_count"))

        with ExitStack() as actx:
            a = Memory(nc, actx)
            s.wq, s.wk, s.wv, s.wo = (a.sb(n, [P, CHUNKS, P]) for n in ("wq", "wk", "wv", "wo"))
            zeros = a.sb("zeros", [P, GROUPS // ZERO_DMAS * GROUP // P * HID])
            number = a.sb("number", [P, GROUPS], I32)
            s.cos, s.sin = (a.sb(n, [P, SEQ]) for n in ("cos", "sin"))
            tokens = hidden.rearrange("b (t p) d -> p (b t) d", p=P)
            with nc.Block() as block:

                @block.sync
                def _(sp):
                    for i in range(NSB):
                        r = slice(i * SB_TILES, (i + 1) * SB_TILES)
                        sp.dma_start(s.x[:, r, :], tokens[:, r, :]).then_inc(s.s_x[i], 16)
                    for to, of in ((s.wq, wq), (s.wk, wk), (s.wv, wv), (s.wo, wo)):
                        sp.dma_start(to[:, :, :], of).then_inc(s.s_wqkvo, 16)
                    for to, of in small:
                        sp.dma_start(to[:, :], of).then_inc(s.s_small, 16)
                    for to, of in ((s.cos, cos), (s.sin, sin)):
                        sp.dma_start(to[:, :], of).then_inc(s.s_rope, 16)
                    sp.dma_start(s.w1[:, :, :], w1.rearrange("e p f -> p e f")).then_inc(s.s_w1, 16)
                    sp.dma_start(s.w2[:, :, :, :], w2.rearrange("e (c p) d -> p e c d", p=P)).then_inc(s.s_w2, 16)
                    sp.dma_start(s.wb[:, :], wb).then_inc(s.s_wb, 16)
                    sp.wait_ge(s.s_zero, 1)
                    part = s.xg.rearrange("(n j) (r p) d -> n p (j r) d", n=ZERO_DMAS, p=P)
                    for n in range(ZERO_DMAS):
                        sp.dma_start(part[n], zeros[:, :].rearrange("p (j d) -> p j d", d=HID)).then_inc(s.s_zeroed, 16)

                @block.gpsimd
                def _(pool):
                    nc.gpsimd.memset(s.ident[:, :], 0.0).then_inc(s.s_const, 1)
                    pool.wait_ge(s.s_const, 1)
                    nc.gpsimd.affine_select(out=s.ident[:, :], in_=s.ident[:, :], compare_op=ALU.not_equal,
                                            fill=1.0, base=0, pattern=[[-1, P]],
                                            channel_multiplier=1).then_inc(s.s_const, 1)
                    nc.gpsimd.memset(s.before[:, :], 1.0).then_inc(s.s_count, 1)
                    nc.gpsimd.iota(number[:, :], pattern=[[1, GROUPS]], base=0, channel_multiplier=0).then_inc(s.s_count, 1)
                    pool.wait_ge(s.s_count, 2)
                    nc.gpsimd.affine_select(out=s.before[:, :], in_=s.before[:, :], compare_op=ALU.is_gt, fill=0.0,
                                            base=0, pattern=[[1, P]], channel_multiplier=-1)
                    nc.gpsimd.tensor_copy(s.tileno[:, :], number[:, :])

                @block.vector
                def _(dve):
                    nc.vector.memset(zeros[:, :], 0.0).then_inc(s.s_zero, 1)
                    nc.vector.memset(s.ones[:, :], 1.0)
                    nc.vector.memset(s.zero[:, :], 0.0)
                    for e in range(EXPERTS):
                        nc.vector.memset(s.iota[:, e:e + 1], float(e))
            norm_stage(nc, m, 0, s, first=True)
            window_stage(nc, m, s)
        if stages > 1:
            norm_stage(nc, m, 1, s, router=True)
            expert_stage(nc, m, 1, s)
        if stages > 2:
            norm_stage(nc, m, 2, s)
            full_stage(nc, m, s)
        if stages > 3:
            norm_stage(nc, m, 3, s, router=True)
            expert_stage(nc, m, 3, s)
        with nc.Block() as block:

            @block.sync
            def _(sp):
                sp.dma_start(out.rearrange("b (t p) d -> p (b t) d", p=P), s.x[:, :, :]).then_inc(s_out, 16)
                sp.wait_ge(s_out, 16)


STAGES = 4


def kernel(**inputs):
    import numpy as _np
    import concourse.bacc as _bacc
    from concourse import mybir as _mybir
    from concourse.bass_utils import run_bass_kernel_spmd as _run

    a = {k.removeprefix("L0_"): _np.asarray(v) for k, v in inputs.items()}
    w = _np.arange(P)
    feature = (w // HD) * HD + (w % HD) // 32 * 16 + _np.where(w % 32 < 16, w % 16, HD // 2 + w % 16)
    rows = (_np.arange(CHUNKS)[:, None] * P + feature[None, :]).reshape(-1)

    def transposed(x):
        return x.T.reshape(HID, CHUNKS, P)

    inv = (_np.float32(1.0) / _np.float32(10000.0) ** (_np.arange(0, HD, 2, dtype=_np.float32) / _np.float32(HD)))
    angle = (_np.arange(SEQ, dtype=_np.float32)[None, :] * inv.astype(_np.float32)[feature % 32][:, None])
    sign = _np.where(w % 32 < 16, -1.0, 1.0)[:, None]
    arrays = {
        "hidden": a["attn_a_hidden_states"],
        "wq": transposed(a["attn_a_Wq"][rows]), "wk": transposed(a["attn_a_Wk"][rows]),
        "wv": transposed(a["attn_a_Wv"]), "wo": a["attn_a_Wo"].T.reshape(CHUNKS, P, HID).transpose(1, 0, 2),
        "bq": a["attn_a_bq"][rows].reshape(CHUNKS, P).T, "bk": a["attn_a_bk"][rows].reshape(CHUNKS, P).T,
        "bv": a["attn_a_bv"].reshape(CHUNKS, P).T, "bo4": _np.tile(a["attn_a_bo"], SB_TILES)[None, :],
        "wb": a["attn_b_W"], "w_router": a["ffn_w_router"], "w1": a["ffn_w1"],
        "b1": a["ffn_b1"].reshape(EXPERTS * HCHUNKS, P).T, "w2": a["ffn_w2"], "b2": a["ffn_b2"].T,
        "cos": _np.cos(angle.astype(_np.float64)).astype(_np.float32),
        "sin": (sign * _np.sin(angle.astype(_np.float64))).astype(_np.float32),
    }
    arrays = {f"in_{k}": _np.ascontiguousarray(v) for k, v in arrays.items()}
    nc = _bacc.Bacc("TRN2", target_bir_lowering=False, num_devices=1)
    args = [nc.dram_tensor(k, v.shape, _mybir.dt.from_np(v.dtype), kind="ExternalInput").ap() for k, v in arrays.items()]
    out = nc.dram_tensor("out_x", (BATCH, SEQ, HID), F32, kind="ExternalOutput").ap()
    bass_hybrid(nc, *args, out, stages=STAGES)
    r = _run(nc, [arrays], core_ids=[0])
    return r.results[0]["out_x"]
```

```python
from contextlib import ExitStack

import concourse.bass as bass
from concourse import mybir

F32 = mybir.dt.float32
U32 = mybir.dt.uint32
I32 = mybir.dt.int32
ALU = mybir.AluOpType
ACT = mybir.ActivationFunctionType
AX_X = mybir.AxisListType.X

P = 128
BATCH, SEQ, HID = 2, 2048, 128
TILES = BATCH * SEQ // P
SB_TILES = 4
SB = SB_TILES * P
NSB = TILES // SB_TILES
SB_PER_BATCH = NSB // BATCH
EPS = 1e-5

HEADS, HD = 16, 64
CHUNKS = HEADS * HD // P
VCOLS = HD + 1
NEG = -1e30

EXPERTS, FFN, TOPK = 8, 512, 2
HCHUNKS = FFN // P
GROUP = 2 * P
GROUPS = TILES * P * TOPK // GROUP + EXPERTS
BLOCKS = TILES * P // GROUP
XBLOCKS = (EXPERTS - 1) * BLOCKS + GROUPS
PART = 8
ZERO_DMAS = XBLOCKS // 4

MASKED = 2.0 ** 53
BTILES = SEQ // P


START = 1


class Memory:

    def __init__(self, nc, ctx):
        self.nc, self.ctx = nc, ctx

    def sb(self, name, shape, dt=F32):
        return self.ctx.enter_context(self.nc.sbuf_tensor(name, shape, dt))

    def psum(self, name, shape, dt=F32):
        return self.ctx.enter_context(self.nc.psum_tensor(name, shape, dt))

    def sem(self, name):
        return self.ctx.enter_context(self.nc.semaphore(name))


class Chain:

    def __init__(self, eng, sem):
        self.eng, self.sem, self.base, self.n = eng, sem, 0, 0

    def enter(self, start, i, per):
        self.base, self.n = start + i * per, 0

    def mark(self, ins):
        self.n += 1
        return ins.then_inc(self.sem, 1)

    def wait(self):
        self.eng.wait_ge(self.sem, START + self.base + self.n)

    def link(self, ins):
        self.mark(ins)
        self.wait()


def stand_alone(eng, s):
    eng.sem_inc(s.s_passed, 1)


def set_up(nc, signals):
    with nc.Block() as block:

        @block.sync
        def _(sp):
            for sem in signals.values():
                sp.sem_inc(sem, START)


def gather(nc, pool, s, got, gathered):
    rows = s.yg.rearrange("j p d -> (j p) d")
    for t in range(TILES):
        for r in range(TOPK):
            nc.gpsimd.indirect_dma_start(
                out=got[:, t, r, :], out_offset=None, in_=rows,
                in_offset=bass.IndirectOffsetOnAxis(ap=s.yslot[:, r, t:t + 1], axis=0)).then_inc(
                    gathered[t // PART], 16)


def combine(nc, ch, s, got, gathered, i):
    ch.eng.wait_ge(gathered[i * SB_TILES // PART], 16 * TOPK * PART)
    for r in range(TOPK):
        for t in range(i * SB_TILES, (i + 1) * SB_TILES):
            ins = nc.vector.scalar_tensor_tensor(s.x[:, t, :], got[:, t, r, :], s.pick[:, t, r:r + 1],
                                                 s.x[:, t, :], ALU.mult, ALU.add)
        ch.link(ins)


def norm_stage(nc, sems, tag, s, first=False, router=False, collect=False):
    with ExitStack() as ctx:
        m = Memory(nc, ctx)
        stats = m.sb(f"stats{tag}", [P, TILES, 6])
        mean = m.sb(f"mean{tag}", [P, TILES])
        rstd = m.sb(f"rstd{tag}", [P, TILES])
        tmp = m.sb(f"tmp{tag}", [P, 6, TILES])
        tp = m.psum(f"tp{tag}", [P, 2, SB])
        S = {n: sems.sem(f"n_{n}{tag}") for n in
             ("chain var std xn tp xs lg sh ex both cnt slot total" if router else "chain var std xn tp xT").split()}
        if router:
            xs = m.sb(f"xs{tag}", [P, 2, SB])
            sh, ex, pr, top, tf, both, place = (m.sb(f"{n}{tag}", [P, TILES, EXPERTS])
                                                for n in "sh ex pr top tf both place".split())
            ti = m.sb(f"ti{tag}", [P, TILES, 8], U32)
            red = m.sb(f"red{tag}", [P, 3, TILES])
            hot, picked = (m.sb(f"{n}{tag}", [P, TOPK, TILES, EXPERTS]) for n in ("hot", "picked"))
            acc = m.sb(f"acc{tag}", [P, TILES + 1, EXPERTS])
            slotf = m.sb(f"slotf{tag}", [P, TOPK, TILES])
            yslotf = m.sb(f"yslotf{tag}", [P, TOPK, TILES])
            few = m.sb(f"few{tag}", [P, 7, EXPERTS])
            fewi = m.sb(f"fewi{tag}", [P, 2, EXPERTS], I32)
            past, skip = (m.sb(f"{n}{tag}", [P, GROUPS, EXPERTS]) for n in ("past", "skip"))
            emf = m.sb(f"emf{tag}", [P, 3, GROUPS])
            lg = m.psum(f"lg{tag}", [P, 2, SB])
            cnt = m.psum(f"cnt{tag}", [P, 2, SB])
            put = sems.sem(f"n_put{tag}")
        else:
            xn = m.sb(f"xn{tag}", [P, 2, SB_TILES, P])
        if collect:
            got = m.sb(f"got{tag}", [P, TILES, TOPK, P])
            gathered = [sems.sem(f"n_got{i}{tag}") for i in range(TILES // PART)]
        set_up(nc, S)
        block = ctx.enter_context(nc.Block())
        SMALL = SB_TILES * EXPERTS

        def tiles(i):
            return slice(i * SB_TILES, (i + 1) * SB_TILES)

        def normalised(i):
            return s.xn[:, tiles(i), :] if router else xn[:, i % 2, :, :]

        @block.vector
        def _(dve):
            ch = Chain(dve, S["chain"])
            wide = [P, SB_TILES, EXPERTS]
            copy = nc.vector.tensor_copy

            def statistics(i):
                r = tiles(i)
                if first:
                    dve.wait_ge(s.s_x[i], 16)
                if collect:
                    combine(nc, ch, s, got, gathered, i)
                for t in range(r.start, r.stop):
                    ins = nc.vector.bn_stats(stats[:, t, :], s.x[:, t, :])
                ch.link(ins)
                me, mo, ve, vo = (stats[:, r, k] for k in (1, 4, 2, 5))
                ch.mark(nc.vector.tensor_tensor(tmp[:, 0, r], me, mo, ALU.add))
                ch.mark(nc.vector.tensor_tensor(tmp[:, 1, r], me, mo, ALU.subtract))
                ch.link(nc.vector.tensor_tensor(tmp[:, 2, r], ve, vo, ALU.add))
                ch.mark(nc.vector.tensor_scalar(mean[:, r], tmp[:, 0, r], 0.5, None, ALU.mult))
                ch.link(nc.vector.scalar_tensor_tensor(tmp[:, 3, r], tmp[:, 1, r], 0.25, tmp[:, 1, r],
                                                       ALU.mult, ALU.mult))
                ch.link(nc.vector.scalar_tensor_tensor(tmp[:, 4, r], tmp[:, 2, r], 1.0 / HID, tmp[:, 3, r],
                                                       ALU.mult, ALU.add))
                nc.vector.tensor_scalar(tmp[:, 5, r], tmp[:, 4, r], EPS, None, ALU.add).then_inc(S["var"], 1)

            def normalise(i):
                r = tiles(i)
                dve.wait_ge(S["std"], START + i + 1)
                ch.link(nc.vector.reciprocal(rstd[:, r], tmp[:, 0, r]))
                if not router and i >= 2:
                    dve.wait_ge(S["tp"], START + i - 1)
                for k in range(SB_TILES):
                    t = i * SB_TILES + k
                    ins = nc.vector.tensor_scalar(normalised(i)[:, k, :], s.x[:, t, :], mean[:, t:t + 1],
                                                  rstd[:, t:t + 1], ALU.subtract, ALU.mult)
                ins.then_inc(S["xn"], 1)

            def shift(i):
                r = tiles(i)
                dve.wait_ge(S["lg"], START + i + 1)
                logits = lg[:, i % 2, 0:SMALL].rearrange("p (t e) -> p t e", e=EXPERTS)
                ch.link(nc.vector.tensor_reduce(red[:, 0, r], logits, AX_X, ALU.max))
                nc.vector.tensor_tensor(sh[:, r, :], logits, red[:, 0, r].unsqueeze(2).to_broadcast(wide),
                                        ALU.subtract).then_inc(S["sh"], 1)

            def choose(i):
                r = tiles(i)
                dve.wait_ge(S["ex"], START + i + 1)
                ch.link(nc.vector.tensor_reduce(red[:, 1, r], ex[:, r, :], AX_X, ALU.add))
                ch.link(nc.vector.reciprocal(red[:, 2, r], red[:, 1, r]))
                ch.link(nc.vector.tensor_tensor(pr[:, r, :], ex[:, r, :],
                                                red[:, 2, r].unsqueeze(2).to_broadcast(wide), ALU.mult))
                for t in range(r.start, r.stop):
                    ins = nc.vector.max(top[:, t, :], pr[:, t, :])
                ch.link(ins)
                for t in range(r.start, r.stop):
                    ins = nc.vector.max_index(ti[:, t, :], top[:, t, :], pr[:, t, :])
                ch.mark(ins)
                ch.link(copy(s.pick[:, r, :], top[:, r, 0:TOPK]))
                ch.link(copy(tf[:, r, :], ti[:, r, :]))
                for k in range(TOPK):
                    ch.mark(nc.vector.tensor_tensor(hot[:, k, r, :], s.iota[:, :].unsqueeze(1).to_broadcast(wide),
                                                    tf[:, r, k:k + 1].to_broadcast(wide), ALU.is_equal))
                ch.wait()
                ch.link(nc.vector.tensor_tensor(both[:, r, :], hot[:, 0, r, :], hot[:, 1, r, :], ALU.add))
                for t in range(r.start, r.stop):
                    ch.link(nc.vector.tensor_tensor(acc[:, t + 1, :], acc[:, t, :], both[:, t, :], ALU.add))
                dve.sem_inc(S["both"], 1)

            def assign(i):
                r = tiles(i)
                dve.wait_ge(S["cnt"], START + i + 1)
                before = cnt[:, i % 2, 0:SMALL].rearrange("p (t e) -> p t e", e=EXPERTS)
                ch.link(nc.vector.tensor_tensor(place[:, r, :], before,
                                                s.base[:, :].unsqueeze(1).to_broadcast(wide), ALU.add))
                for k in range(TOPK):
                    ch.mark(nc.vector.tensor_tensor(picked[:, k, r, :], hot[:, k, r, :], place[:, r, :], ALU.mult))
                ch.wait()
                ch.link(nc.vector.tensor_reduce(slotf[:, :, r], picked[:, :, r, :], AX_X, ALU.add))
                copy(s.slot[:, :, r], slotf[:, :, r]).then_inc(S["slot"], 1)

            def groups():
                dve.wait_ge(S["total"], START + 1)
                ch.link(nc.vector.tensor_scalar(fewi[:, 0, :], cnt[:, 0, 0:EXPERTS], float(GROUP - 1), None, ALU.add))
                ch.link(nc.vector.tensor_scalar(fewi[:, 1, :], fewi[:, 0, :], GROUP.bit_length() - 1, None,
                                                ALU.logical_shift_right))
                ch.link(copy(few[:, 0, :], fewi[:, 1, :]))
                a, step = 0, 1
                while step < EXPERTS:
                    ch.mark(copy(few[:, a + 1, 0:step], few[:, a, 0:step]))
                    ch.link(nc.vector.tensor_tensor(few[:, a + 1, step:], few[:, a, step:],
                                                    few[:, a, 0:EXPERTS - step], ALU.add))
                    a, step = a + 1, 2 * step
                shape = [P, GROUPS, EXPERTS]
                ch.mark(nc.vector.tensor_scalar(few[:, 4, :], few[:, 0, :], -1.0, float(BLOCKS), ALU.mult, ALU.add))
                ch.link(nc.vector.tensor_tensor(past[:, :, :], s.groupno[:, :].unsqueeze(2).to_broadcast(shape),
                                                few[:, a, :].unsqueeze(1).to_broadcast(shape), ALU.is_ge))
                ch.mark(nc.vector.tensor_reduce(emf[:, 0, :], past[:, :, 0:EXPERTS - 1], AX_X, ALU.add))
                ch.link(nc.vector.tensor_tensor(skip[:, :, :], past[:, :, :],
                                                few[:, 4, :].unsqueeze(1).to_broadcast(shape), ALU.mult))
                ch.link(nc.vector.tensor_reduce(emf[:, 1, :], skip[:, :, 0:EXPERTS - 1], AX_X, ALU.add))
                ch.link(nc.vector.tensor_tensor(emf[:, 2, :], emf[:, 1, :], s.groupno[:, :], ALU.add))
                ch.mark(copy(s.emap[:, :], emf[:, 0, :]))
                ch.mark(copy(s.gmap[:, :], emf[:, 2, :]))
                ch.link(nc.vector.tensor_tensor(few[:, 5, :], few[:, a, :], few[:, 0, :], ALU.subtract))
                ch.link(nc.vector.scalar_tensor_tensor(few[:, 6, :], few[:, 5, :], float(GROUP), s.base[:, :],
                                                       ALU.mult, ALU.subtract))
                ch.link(nc.vector.tensor_tensor(
                    picked[:, :, :, :].rearrange("p k t e -> p (k t) e"), hot[:, :, :, :].rearrange("p k t e -> p (k t) e"),
                    few[:, 6, :].unsqueeze(1).to_broadcast([P, TOPK * TILES, EXPERTS]), ALU.mult))
                ch.link(nc.vector.tensor_reduce(yslotf[:, :, :], picked[:, :, :, :], AX_X, ALU.add))
                ch.link(nc.vector.tensor_tensor(yslotf[:, :, :], yslotf[:, :, :], slotf[:, :, :], ALU.add))
                ch.mark(copy(s.yslot[:, :, :], yslotf[:, :, :]))

            if router:
                ch.link(nc.vector.memset(acc[:, 0, :], 0.0))
            for i in range(NSB + 3):
                if router and 0 <= i - 2 < NSB:
                    shift(i - 2)
                if i < NSB:
                    statistics(i)
                if 0 <= i - 1 < NSB:
                    normalise(i - 1)
                if router and 0 <= i - 3 < NSB:
                    assign(i - 3)
                if router and 0 <= i - 2 < NSB:
                    choose(i - 2)
            if router:
                groups()

        @block.scalar
        def _(act):
            for i in range(NSB + 2):
                if router and 0 <= i - 2 < NSB:
                    r = tiles(i - 2)
                    act.wait_ge(S["sh"], START + i - 1)
                    nc.scalar.activation(ex[:, r, :], sh[:, r, :], ACT.Exp).then_inc(S["ex"], 1)
                if i < NSB:
                    act.wait_ge(S["var"], START + i + 1)
                    nc.scalar.activation(tmp[:, 0, tiles(i)], tmp[:, 5, tiles(i)], ACT.Sqrt).then_inc(S["std"], 1)
                if 0 <= i - 1 < NSB:
                    act.wait_ge(S["tp"], START + i)
                    if router:
                        if i >= 3:
                            act.wait_ge(S["lg"], START + i - 2)
                        nc.scalar.copy(xs[:, (i - 1) % 2, :], tp[:, (i - 1) % 2, :]).then_inc(S["xs"], 1)
                    else:
                        nc.scalar.copy(s.xT[:, (i - 1) * SB:i * SB], tp[:, (i - 1) % 2, :]).then_inc(S["xT"], 1)

        @block.tensor
        def _(pe):
            pe.wait_ge(s.s_const, CONSTS)
            if router:
                pe.wait_ge(s.s_small, 16 * s.n_small)

            def count(i):
                pe.wait_ge(S["both"], START + i + 1)
                if i >= 2:
                    pe.wait_ge(S["slot"], START + i - 1)
                to = cnt[:, i % 2, 0:SMALL]
                nc.tensor.matmul(to, s.before[:, :], both[:, tiles(i), :].rearrange("p t e -> p (t e)"),
                                 start=True, stop=False)
                nc.tensor.matmul(to, s.ones[:, :], acc[:, tiles(i), :].rearrange("p t e -> p (t e)"),
                                 start=False, stop=True).then_inc(S["cnt"], 1)

            for i in range(NSB + 1):
                if i < NSB:
                    pe.wait_ge(S["xn"], START + i + 1)
                    if i >= 2:
                        pe.wait_ge(S["xs" if router else "xT"], START + i - 1)
                    for t in range(SB_TILES):
                        ins = nc.tensor.transpose(tp[:, i % 2, t * P:(t + 1) * P], normalised(i)[:, t, :],
                                                  s.ident[:, :])
                    ins.then_inc(S["tp"], 1)
                    if router:
                        pe.wait_ge(S["xs"], START + i + 1)
                        if i >= 2:
                            pe.wait_ge(S["sh"], START + i - 1)
                        for t in range(SB_TILES):
                            ins = nc.tensor.matmul(lg[:, i % 2, t * EXPERTS:(t + 1) * EXPERTS],
                                                   xs[:, i % 2, t * P:(t + 1) * P], s.w_router[:, :],
                                                   start=True, stop=True)
                        ins.then_inc(S["lg"], 1)
                if router and i > 0:
                    count(i - 1)
            if router:
                pe.wait_ge(S["slot"], START + NSB - 1)
                nc.tensor.matmul(cnt[:, 0, 0:EXPERTS], s.ones[:, :], acc[:, TILES, :], start=True,
                                 stop=True).then_inc(S["total"], 1)

        if router or collect:
            @block.gpsimd
            def _(pool):
                if collect:
                    gather(nc, pool, s, got, gathered)
                    return
                pool.wait_ge(s.s_zeroed, 16 * ZERO_DMAS)
                rows = s.xg.rearrange("j p d -> (j p) d")
                for t in range(TILES):
                    if t % SB_TILES == 0:
                        pool.wait_ge(S["slot"], START + t // SB_TILES + 1)
                    for r in range(TOPK):
                        nc.gpsimd.indirect_dma_start(
                            out=rows, out_offset=bass.IndirectOffsetOnAxis(ap=s.slot[:, r, t:t + 1], axis=0),
                            in_=s.xn[:, t, :], in_offset=None).then_inc(put, 16)
                pool.wait_ge(put, 16 * TILES * TOPK)


def window_stage(nc, sems, s):
    with ExitStack() as ctx:
        m = Memory(nc, ctx)
        xs = m.sb("xs", [P, SB])
        Q = m.sb("Q", [P, CHUNKS, SB])
        K = m.sb("K", [P, CHUNKS, P + SB])
        V = m.sb("V", [P, CHUNKS, 1 + SB_TILES, 2, VCOLS])
        lin = m.sb("lin", [P, 2, SB])
        rot = m.sb("rot", [P, 2, SB])
        sc = m.sb("sc", [P, 2, 2, 2 * P])
        mx = m.sb("mx", [P, 2, 2])
        pT = m.sb("pT", [P, 2, 2, 2, P])
        rs = m.sb("rs", [P, 4])
        on = m.sb("on", [P, SB_TILES, P])
        oT = m.sb("oT", [P, SB])
        mask = m.sb("mask", [P, 2 * P])
        masks = m.sb("masks", [P, SB_PER_BATCH, 2 * P])
        mask0 = m.sb("mask0", [P, 2 * P])
        pj = m.psum("pj", [P, SB])
        ps = m.psum("ps", [P, 2, SB])
        pt = m.psum("pt", [P, 2, 2, 2, P])
        po = m.psum("po", [P, 2, SB])
        pout = m.psum("pout", [P, SB_TILES, P])

        names = ("mask xs q_ps k_ps v_ps q_sb k_sb v_sb q_sh k_sh q_cos k_cos q_rdy k_rdy k_prev v_prev "
                 "s max p t pt pv norm oT oT_sb out res mask0 chain pool").split()
        S = {n: sems.sem(f"a_{n}") for n in names}
        swap = [(w + 16) % 32 for w in range(32)]
        set_up(nc, S)
        block = ctx.enter_context(nc.Block())

        def units(sb, c):
            u = CHUNKS * sb + c
            return u, u + 2, (c + 2) % CHUNKS, (sb if c + 2 < CHUNKS else sb + 1)

        def pos(sb):
            return bass.ts(sb % SB_PER_BATCH, SB)

        @block.tensor
        def _(pe):
            def project_q(v, c, head=False):
                pe.wait_ge(S["v_sb"], START + v + CHUNKS)
                if not head:
                    pe.wait_ge(S["oT_sb"], START + v - 2)
                nc.tensor.matmul(pj[:, :], s.wq[:, c, :], xs[:, :], start=True, stop=True).then_inc(S["q_ps"], 1)

            def project_k(v, c):
                pe.wait_ge(S["q_sb"], START + v + 1)
                nc.tensor.matmul(pj[:, :], s.wk[:, c, :], xs[:, :], start=True, stop=True).then_inc(S["k_ps"], 1)

            def project_v(v, c):
                pe.wait_ge(S["k_sb"], START + v + 1)
                for t in range(SB_TILES):
                    ins = nc.tensor.matmul(pj[:, t * P:(t + 1) * P], xs[:, t * P:(t + 1) * P], s.wv[:, c, :],
                                           start=True, stop=True)
                ins.then_inc(S["v_ps"], 1)

            def scores(c, b, u, G, first=False):
                if b == 0:
                    pe.wait_ge(S["q_rdy"], START + u + 1)
                    pe.wait_ge(S["k_rdy"], START + u + 1 + CHUNKS)
                for h in range(2):
                    if not first:
                        pe.wait_ge(S["max"], START + 2 * G - 1 + h)
                    r = slice(h * HD, (h + 1) * HD)
                    ins = nc.tensor.matmul(ps[:, h, 0:2 * P], Q[r, c, b * P:(b + 1) * P], K[r, c, b * P:(b + 2) * P],
                                           start=True, stop=True)
                ins.then_inc(S["s"], 1)

            def transposes(b, G, first=False):
                pe.wait_ge(S["p"], START + 2 * G + 2)
                if not first:
                    pe.wait_ge(S["pt"], START + G - 1)
                for h in range(2):
                    for kb in range(2):
                        ins = nc.tensor.transpose(pt[:, b % 2, h, kb, :], sc[:, b % 2, h, kb * P:(kb + 1) * P],
                                                  s.ident[:, :])
                ins.then_inc(S["t"], 1)

            def values(c, b, u, G):
                pe.wait_ge(S["pt"], START + G + 1)
                if b == 0:
                    pe.wait_ge(S["v_sb"], START + u + 1 + CHUNKS)
                    pe.wait_ge(S["v_prev"], START + u + 1)
                if b == 0:
                    pe.wait_ge(S["norm"], START + 2 * u)
                for h in range(2):
                    for kb in range(2):
                        ins = nc.tensor.matmul(po[:, b // 2, (b % 2 * 2 + h) * VCOLS:(b % 2 * 2 + h + 1) * VCOLS], pT[:, b % 2, h, kb, :], V[:, c, b + kb, h, :],
                                               start=(kb == 0), stop=(kb == 1))
                ins.then_inc(S["pv"], 1)

            def turn_out(u):
                pe.wait_ge(S["norm"], START + 2 * u + 2)
                pe.wait_ge(S["v_sb"], START + u + 3 + CHUNKS)
                for t in range(SB_TILES):
                    ins = nc.tensor.transpose(pj[:, t * P:(t + 1) * P], on[:, t, :], s.ident[:, :])
                ins.then_inc(S["oT"], 1)

            def project_out(u, c, sb):
                if c == 0:
                    pe.wait_ge(S["res"], START + sb)
                    nc.tensor.matmul(pout[:, :, :].rearrange("p a b -> p (a b)"), s.ones[0:1, :], s.bo4[0:1, :],
                                     start=True, stop=False, skip_group_check=True)
                pe.wait_ge(S["oT_sb"], START + u + 1)
                for t in range(SB_TILES):
                    ins = nc.tensor.matmul(pout[:, t, :], oT[:, t * P:(t + 1) * P], s.wo[:, c, :],
                                           start=False, stop=(c == CHUNKS - 1), skip_group_check=True)
                ins.then_inc(S["out"], 1)

            pe.wait_ge(s.s_wqkvo, 64)
            pe.wait_ge(s.s_small, 16 * s.n_small)
            pe.sem_inc(S["oT"], CHUNKS)
            pe.wait_ge(S["xs"], START + 1)
            for v in range(2):
                project_q(v, v, head=True)
                project_k(v, v)
                project_v(v, v)
            scores(0, 0, 0, 0, first=True)
            scores(0, 1, 0, 1)
            transposes(0, 0, first=True)
            with pe.Fori(0, NSB) as sb:
                for c in range(CHUNKS):
                    u, v, vc, vsb = units(sb, c)
                    for b in range(SB_TILES):
                        G = SB_TILES * u + b
                        if b < 2:
                            scores(c, b + 2, u, G + 2)
                        else:
                            scores((c + 1) % CHUNKS, b - 2, u + 1, G + 2)
                        transposes((b + 1) % SB_TILES, G + 1)
                        if b == 0 and c > 0:
                            turn_out(u - 1)
                        if b == 1:
                            if vc == 0:
                                pe.wait_ge(S["xs"], START + vsb + 1)
                            project_q(v, vc)
                        if b == 2 and c > 0:
                            project_out(u - 1, c - 1, sb)
                        if b == 2:
                            project_k(v, vc)
                        if b == 3:
                            project_v(v, vc)
                        values(c, b, u, G)
                turn_out(CHUNKS * sb + CHUNKS - 1)
                project_out(CHUNKS * sb + CHUNKS - 1, CHUNKS - 1, sb)

        @block.scalar
        def _(act):
            def probabilities(b, G):
                act.wait_ge(S["max"], START + 2 * G + 2)
                for h in range(2):
                    nc.scalar.activation(sc[:, b % 2, h, :], sc[:, b % 2, h, :], ACT.Exp, scale=-1.0,
                                         bias=mx[:, b % 2, h:h + 1]).then_inc(S["p"], 1)

            def read_pt(b, G, first=False):
                act.wait_ge(S["t"], START + G + 1)
                if not first:
                    act.wait_ge(S["pv"], START + G - 1)
                nc.scalar.copy(pT[:, b % 2, :, :, :], pt[:, b % 2, :, :, :]).then_inc(S["pt"], 1)

            def read_q(v, c, v0=False):
                act.wait_ge(S["q_ps"], START + v + 1)
                if not v0:
                    act.wait_ge(S["q_rdy"], START + v)
                nc.scalar.activation(lin[:, 0, :], pj[:, :], ACT.Identity, bias=s.bq[:, c:c + 1]).then_inc(S["q_sb"], 1)

            def read_k(v, c, v0=False):
                act.wait_ge(S["k_ps"], START + v + 1)
                if not v0:
                    act.wait_ge(S["k_rdy"], START + v + CHUNKS)
                nc.scalar.activation(lin[:, 1, :], pj[:, :], ACT.Identity, bias=s.bk[:, c:c + 1]).then_inc(S["k_sb"], 1)

            def read_out(u, c):
                act.wait_ge(S["oT"], START + u + 1 + CHUNKS)
                act.wait_ge(S["out"], START + u)
                nc.scalar.activation(oT[:, :], pj[:, :], ACT.Identity, bias=s.bv[:, c:c + 1]).then_inc(S["oT_sb"], 1)

            act.wait_ge(s.s_small, 16 * s.n_small)
            for v in range(2):
                read_q(v, v, v0=(v == 0))
                read_k(v, v, v0=(v == 0))
            probabilities(0, 0)
            probabilities(1, 1)
            read_pt(0, 0, first=True)
            with act.Fori(0, NSB) as sb:
                for c in range(CHUNKS):
                    u, v, vc, vsb = units(sb, c)
                    for b in range(SB_TILES):
                        G = SB_TILES * u + b
                        probabilities((b + 2) % SB_TILES, G + 2)
                        read_pt((b + 1) % SB_TILES, G + 1)
                        if b == 0 and c > 0:
                            read_out(u - 1, c - 1)
                        if b == 1:
                            read_q(v, vc)
                        if b == 2:
                            read_k(v, vc)
                read_out(CHUNKS * sb + CHUNKS - 1, CHUNKS - 1)

        @block.vector
        def _(dve):
            ch = Chain(dve, S["chain"])

            def maxima(c, b, G, first=False):
                dve.wait_ge(S["s"], START + G + 1)
                if not first:
                    dve.wait_ge(S["t"], START + G - 1)
                stand_alone(dve, s)
                for h in range(2):
                    nc.vector.tensor_tensor_reduce(sc[:, b % 2, h, :], ps[:, h, 0:2 * P],
                                                   (mask0 if b == 0 else mask)[:, :], -float(HD) ** -0.5, 3e38,
                                                   ALU.add, ALU.min, mx[:, b % 2, h:h + 1]).then_inc(S["max"], 1)

            def turn(v, sb, which, src, w0):
                dve.wait_ge(S[src], START + v + 1)
                if not w0:
                    dve.wait_ge(S["q_rdy" if which == 0 else "k_rdy"], START + v + (CHUNKS if which else 0))
                stand_alone(dve, s)
                nc.vector.stream_shuffle(rot[:, which, :], lin[:, which, :], swap).then_inc(
                    S["q_sh" if which == 0 else "k_sh"], 1)
                nc.vector.tensor_tensor(lin[:, which, :], lin[:, which, :], s.cos[:, pos(sb)], ALU.mult).then_inc(
                    S["q_cos" if which == 0 else "k_cos"], 1)

            def keep_v(v, c):
                dve.wait_ge(S["v_ps"], START + v + 1)
                dve.wait_ge(S["v_prev"], START + v + 1)
                nc.vector.tensor_copy(V[:, c, 1:, :, 0:HD],
                                      pj[:, :].rearrange("p (t h d) -> p t h d", t=SB_TILES, h=2)).then_inc(S["v_sb"], 1)

            def normalise(u, b, G):
                dve.wait_ge(S["pv"], START + G + 1)
                pair = po[:, b // 2, 0:4 * VCOLS].rearrange("p (a d) -> p a d", a=4)
                ch.link(nc.vector.reciprocal(rs[:, :], pair[:, :, HD]))
                if b == 1:
                    dve.wait_ge(S["oT"], START + u + CHUNKS)
                nc.vector.tensor_tensor(
                    on[:, b - 1:b + 1, :].rearrange("p a (h d) -> p (a h) d", h=2),
                    pair[:, :, 0:HD],
                    rs[:, :].unsqueeze(2).to_broadcast([P, 4, HD]), ALU.mult).then_inc(S["norm"], 1)

            dve.wait_ge(s.s_rope, 32)
            nc.vector.memset(V[:, :, :, :, :], 1.0).then_inc(S["v_sb"], CHUNKS)
            dve.wait_ge(S["v_sb"], START + CHUNKS)
            dve.wait_ge(S["mask"], START + 3)
            ch.link(nc.vector.tensor_copy(mask0[:, :], masks[:, 0, :]))
            for v in range(2):
                turn(v, 0, 0, "q_sb", v == 0)
                turn(v, 0, 1, "k_sb", v == 0)
                keep_v(v, v)
            maxima(0, 0, 0, first=True)
            maxima(0, 1, 1, first=True)
            start = ch.base + ch.n
            with dve.Fori(0, NSB) as sb:
                ch.enter(start, sb, 2 * CHUNKS + 1)
                for c in range(CHUNKS):
                    u, v, vc, vsb = units(sb, c)
                    for b in range(SB_TILES):
                        G = SB_TILES * u + b
                        if b == 2 and c == CHUNKS - 1:
                            ch.link(nc.vector.tensor_copy(mask0[:, :], masks[:, (sb + 1) % SB_PER_BATCH, :]))
                        maxima(c, (b + 2) % SB_TILES, G + 2)
                        if b == 2:
                            turn(v, vsb, 0, "q_sb", False)
                        if b == 3:
                            turn(v, vsb, 1, "k_sb", False)
                            keep_v(v, vc)
                        if b % 2 == 1:
                            normalise(u, b, G)
                dve.wait_ge(S["out"], START + CHUNKS * (sb + 1))
                own = s.x[:, bass.ts(sb, SB_TILES), :]
                nc.vector.tensor_tensor(own, own, pout[:, :, :], ALU.add).then_inc(S["res"], 1)

        @block.sync
        def _(sp):
            sp.wait_ge(s.s_zeroed, 16 * ZERO_DMAS)

        @block.gpsimd
        def _(pool):
            ch = Chain(pool, S["pool"])
            nc.gpsimd.memset(masks[:, :, :], 0.0).then_inc(S["pool"], 1)
            nc.gpsimd.memset(K[:, :, :], 0.0).then_inc(S["k_rdy"], CHUNKS)
            pool.wait_ge(S["pool"], START + 1)
            nc.gpsimd.affine_select(out=masks[:, :, 0:P], in_=masks[:, :, 0:P], compare_op=ALU.is_ge, fill=NEG,
                                    base=0, pattern=[[0, SB_PER_BATCH], [1, P]], channel_multiplier=-1).then_inc(S["pool"], 1)
            nc.gpsimd.affine_select(out=masks[:, :, P:], in_=masks[:, :, P:], compare_op=ALU.is_ge, fill=NEG,
                                    base=0, pattern=[[0, SB_PER_BATCH], [-1, P]], channel_multiplier=1).then_inc(S["mask"], 1)
            pool.wait_ge(S["pool"], START + 2)
            pool.wait_ge(S["mask"], START + 1)
            nc.gpsimd.tensor_copy(mask[:, :], masks[:, 1, :]).then_inc(S["mask"], 1)
            nc.gpsimd.memset(masks[:, 0, 0:P], NEG).then_inc(S["mask"], 1)
            pool.wait_ge(s.s_rope, 32)
            nc.gpsimd.tensor_copy(xs[:, :], s.xT[:, 0:SB]).then_inc(S["xs"], 1)

            def rotate(v, c, sb, which):
                pool.wait_ge(S["q_sh" if which == 0 else "k_sh"], START + v + 1)
                stand_alone(pool, s)
                nc.gpsimd.tensor_tensor(rot[:, which, :], rot[:, which, :], s.sin[:, pos(sb)], ALU.mult).then_inc(S["pool"], 1)
                ch.n += 1
                ch.wait()
                pool.wait_ge(S["q_cos" if which == 0 else "k_cos"], START + v + 1)
                to = Q[:, c, :] if which == 0 else K[:, c, P:]
                nc.gpsimd.tensor_tensor(to, lin[:, which, :], rot[:, which, :], ALU.add).then_inc(
                    S["q_rdy" if which == 0 else "k_rdy"], 1)

            def unit(v, c, sb):
                pool.wait_ge(S["oT"], START + v + 1)
                pool.wait_ge(S["k_rdy"], START + v + CHUNKS)
                stand_alone(pool, s)
                nc.gpsimd.tensor_copy(K[:, c, 0:P], K[:, c, SB:]).then_inc(S["k_prev"], 1)
                pool.wait_ge(S["v_sb"], START + v + CHUNKS)
                stand_alone(pool, s)
                nc.gpsimd.tensor_copy(V[:, c, 0, :, :], V[:, c, SB_TILES, :, :]).then_inc(S["v_prev"], 1)
                rotate(v, c, sb, 0)
                pool.wait_ge(S["k_prev"], START + v + 1)
                rotate(v, c, sb, 1)

            ch.base = 2
            ch.n = 0
            for v in range(2):
                unit(v, v, 0)
            start = ch.base + ch.n
            with pool.Fori(0, NSB) as sb:
                ch.enter(start, sb, 2 * CHUNKS)
                for c in range(CHUNKS):
                    u, v, vc, vsb = units(sb, c)
                    if vc == 0:
                        pool.wait_ge(S["v_ps"], START + CHUNKS * (sb + 1))
                        stand_alone(pool, s)
                        nc.gpsimd.tensor_copy(xs[:, :], s.xT[:, bass.ts((sb + 1) % NSB, SB)]).then_inc(S["xs"], 1)
                    unit(v, vc, vsb)


def expert_stage(nc, sems, tag, s):
    with ExitStack() as ctx:
        m = Memory(nc, ctx)
        xt = m.sb(f"xt{tag}", [P, 4, GROUP // P, P])
        xgT = m.sb(f"xgT{tag}", [P, 2, GROUP])
        w1s = m.sb(f"w1s{tag}", [P, 2, FFN])
        w2s = m.sb(f"w2s{tag}", [P, 2, HCHUNKS, P])
        hT = m.sb(f"hT{tag}", [P, 2, HCHUNKS, GROUP])
        yT = m.sb(f"yT{tag}", [P, 2, GROUP])
        yo = m.sb(f"yo{tag}", [P, 2, GROUP // P, P])
        px = m.psum(f"px{tag}", [P, SB])
        ph = m.psum(f"ph{tag}", [P, 2, HCHUNKS, GROUP])
        py = m.psum(f"py{tag}", [P, 2, SB])
        pz = m.psum(f"pz{tag}", [P, SB])
        S = {n: sems.sem(f"e_{n}{tag}") for n in "t xT w1 w2 h gelu y yT z yo".split()}
        load = [sems.sem(f"e_load{k}{tag}") for k in range(4)]
        stored = [sems.sem(f"e_stored{k}{tag}") for k in range(2)]
        set_up(nc, S)
        block = ctx.enter_context(nc.Block())
        STEP = 4
        ROUNDS = GROUPS // STEP

        def steps(eng, body, ahead=None):
            def turn(jj):
                es = []
                if ahead is not None:
                    es = [expert(eng, STEP * jj + a) for a in range(STEP + ahead)
                          if not isinstance(jj, int) or STEP * jj + a < GROUPS]
                for k in range(STEP):
                    body(jj, k, *([es[k:]] if es else []))

            rounds(eng, turn)

        def rounds(eng, turn):
            turn(0)
            with eng.Fori(0, ROUNDS - 2) as i:
                turn(i + 1)
            turn(ROUNDS - 1)

        def turns(eng, body):
            def turn(jj):
                gs = [place(eng, STEP * jj + a) if not isinstance(jj, int) or 0 <= STEP * jj + a < GROUPS else None
                      for a in range(2 * STEP)]
                for k in range(STEP):
                    body(jj, k, gs[k:])

            rounds(eng, turn)

        def outside(jj, k, ahead):
            return isinstance(jj, int) and not 0 <= STEP * jj + k + ahead < GROUPS

        def expert(eng, j):
            return eng.value_load(s.emap[0:1, bass.ds(j, 1)], min_val=0, max_val=EXPERTS - 1)

        def place(eng, j):
            return eng.value_load(s.gmap[0:1, bass.ds(j, 1)], min_val=0, max_val=XBLOCKS - 1)

        def rows(dram, j):
            return dram[bass.ds(j, 1), :, :].rearrange("o (p r) d -> p (o r) d", r=GROUP // P)

        @block.sync
        def _(sp):
            def fetch(g, k):
                sp.dma_start(xt[:, k, :, :], rows(s.xg, g)).then_inc(load[k], 16)

            def body(jj, k, gs):
                j = STEP * jj + k
                if not outside(jj, k, STEP):
                    sp.wait_ge(S["t"], START + j + 1)
                    fetch(gs[STEP], k)
                if not outside(jj, k, -1):
                    sp.wait_ge(S["yo"], START + j)
                    store(j - 1, k + 1)

            def store(j, k):
                sp.dma_start(rows(s.yg, j), yo[:, k % 2, :, :]).then_inc(stored[k % 2], 16)

            for k in range(STEP):
                fetch(place(sp, k), k)
            turns(sp, body)
            sp.wait_ge(S["yo"], START + GROUPS)
            store(GROUPS - 1, GROUPS - 1)
            for k in range(2):
                sp.wait_ge(stored[k], 16 * (GROUPS // 2))

        @block.tensor
        def _(pe):
            def turn(j, k, nth):
                pe.wait_ge(load[k % STEP], 16 * nth)
                for r in range(GROUP // P):
                    ins = nc.tensor.transpose(px[:, r * P:(r + 1) * P], xt[:, k % STEP, r, :], s.ident[:, :])
                ins.then_inc(S["t"], 1)

            def hidden(j, k):
                pe.wait_ge(S["xT"], START + j + 1)
                pe.wait_ge(S["w1"], START + j + 1)
                for i in range(HCHUNKS):
                    ins = nc.tensor.matmul(ph[:, k % 2, i, :], w1s[:, k % 2, i * P:(i + 1) * P], xgT[:, k % 2, :],
                                           start=True, stop=True)
                ins.then_inc(S["h"], 1)

            def turn_back(j, k):
                pe.wait_ge(S["yT"], START + j + 1)
                for r in range(GROUP // P):
                    ins = nc.tensor.transpose(pz[:, r * P:(r + 1) * P], yT[:, k % 2, r * P:(r + 1) * P], s.ident[:, :])
                ins.then_inc(S["z"], 1)

            def body(jj, k):
                j = STEP * jj + k
                if not outside(jj, k, 2):
                    pe.wait_ge(S["xT"], START + j + 2)
                    turn(j + 2, k + 2, jj + 1 + (k + 2) // STEP)
                if not outside(jj, k, 1):
                    if not outside(jj, k, -1):
                        pe.wait_ge(S["gelu"], START + HCHUNKS * j)
                    hidden(j + 1, k + 1)
                if not outside(jj, k, -1):
                    if not outside(jj, k, -2):
                        pe.wait_ge(S["yo"], START + j - 1)
                    turn_back(j - 1, k + 1)
                pe.wait_ge(S["gelu"], START + HCHUNKS * (j + 1))
                pe.wait_ge(S["w2"], START + j + 1)
                if not outside(jj, k, -2):
                    pe.wait_ge(S["yT"], START + j - 1)
                for i in range(HCHUNKS):
                    ins = nc.tensor.matmul(py[:, k % 2, 0:GROUP], w2s[:, k % 2, i, :], hT[:, k % 2, i, :],
                                           start=(i == 0), stop=(i == HCHUNKS - 1))
                ins.then_inc(S["y"], 1)

            turn(0, 0, 1)
            pe.wait_ge(S["xT"], START + 1)
            turn(1, 1, 1)
            hidden(0, 0)
            steps(pe, body)
            pe.wait_ge(S["yo"], START + GROUPS - 1)
            turn_back(GROUPS - 1, GROUPS - 1)

        @block.scalar
        def _(act):
            def read(j, k):
                act.wait_ge(S["t"], START + j + 1)
                nc.scalar.copy(xgT[:, k % 2, :], px[:, 0:GROUP]).then_inc(S["xT"], 1)

            def gelu(j, k, e):
                act.wait_ge(S["h"], START + j + 1)
                for i in range(HCHUNKS):
                    nc.scalar.activation(hT[:, k % 2, i, :], ph[:, k % 2, i, :], ACT.Gelu_apprx_tanh,
                                         bias=s.b1[:, bass.ds(e * HCHUNKS + i, 1)]).then_inc(S["gelu"], 1)

            def body(jj, k, es):
                j = STEP * jj + k
                if not outside(jj, k, 2):
                    act.wait_ge(S["h"], START + j + 1)
                    read(j + 2, k + 2)
                if not outside(jj, k, 1):
                    if not outside(jj, k, -1):
                        act.wait_ge(S["y"], START + j)
                    gelu(j + 1, k + 1, es[1])
                if not outside(jj, k, -2):
                    act.wait_ge(S["z"], START + j - 1)
                act.wait_ge(S["y"], START + j + 1)
                nc.scalar.activation(yT[:, k % 2, :], py[:, k % 2, 0:GROUP], ACT.Identity,
                                     bias=s.b2[:, bass.ds(es[0], 1)]).then_inc(S["yT"], 1)

            e = expert(act, 0)
            read(0, 0)
            read(1, 1)
            gelu(0, 0, e)
            steps(act, body, 1)

        @block.vector
        def _(dve):
            def first_weights(j, k, e):
                nc.vector.tensor_copy(w1s[:, k % 2, :], s.w1[:, e, :]).then_inc(S["w1"], 1)

            def second_weights(j, k, e):
                nc.vector.tensor_copy(w2s[:, k % 2, :, :], s.w2[:, e, :, :]).then_inc(S["w2"], 1)

            def keep(j, k):
                dve.wait_ge(S["z"], START + j + 1)
                nc.vector.tensor_copy(yo[:, k % 2, :, :], pz[:, 0:GROUP].rearrange("p (r d) -> p r d", d=P)).then_inc(
                    S["yo"], 1)

            def body(jj, k, es):
                j = STEP * jj + k
                if not outside(jj, k, 2):
                    dve.wait_ge(S["h"], START + j + 1)
                    first_weights(j + 2, k + 2, es[2])
                if not outside(jj, k, 1):
                    if not outside(jj, k, -1):
                        dve.wait_ge(S["y"], START + j)
                    second_weights(j + 1, k + 1, es[1])
                if not outside(jj, k, -1):
                    if not outside(jj, k, -3):
                        dve.wait_ge(stored[(k + 1) % 2], 16 * (2 * jj + (k - 1) // 2))
                    keep(j - 1, k + 1)

            dve.wait_ge(s.s_w1, 16)
            dve.wait_ge(s.s_w2, 16)
            e0, e1 = expert(dve, 0), expert(dve, 1)
            first_weights(0, 0, e0)
            first_weights(1, 1, e1)
            second_weights(0, 0, e0)
            steps(dve, body, 2)
            dve.wait_ge(stored[1], 16 * (GROUPS // 2 - 1))
            keep(GROUPS - 1, GROUPS - 1)


def full_stage(nc, sems, s):
    AHEAD = 7
    UBUF = AHEAD + 3
    with ExitStack() as ctx:
        m = Memory(nc, ctx)
        xs = m.sb("bxs", [P, SEQ])
        qT = m.sb("qT", [P, SEQ])
        kT = m.sb("kT", [P, SEQ])
        V = m.sb("bV", [P, BTILES, HID + 1])
        U = m.sb("U", [P, UBUF, SB])
        tri = m.sb("tri", [P, P])
        mn = m.sb("mn", [P, UBUF, BTILES // 4])
        st = m.sb("st", [P, UBUF, 4])
        pT = m.sb("bpT", [P, 2, 4, P])
        pre = m.sb("pre", [P, HID + 1])
        oo = m.sb("oo", [P, HID + 1])
        pp = m.psum("pp", [P, 2, SB])
        ps = m.psum("bps", [P, 2, SB])
        pt = m.psum("bpt", [P, 2, 4, P])
        po = m.psum("bpo", [P, 2, SB])
        S = {n: sems.sem(f"f_{n}") for n in
             "xs proj qk v ones s copy u bias p w0 t pt pv pre pre_sb o chain end tri".split()}
        set_up(nc, S)
        block = ctx.enter_context(nc.Block())
        chunks = [[(k, min(4, BTILES - k)) for k in range(i, BTILES, 4)] for i in range(BTILES)]
        first = [sum(len(c) for c in chunks[:i]) for i in range(BTILES + 1)]
        NCH = first[-1]
        MARKS = 4 * BTILES + NCH
        chunk = [(i, c, k0, n) for i in range(BTILES) for c, (k0, n) in enumerate(chunks[i])]

        @block.tensor
        def _(pe):
            pe.wait_ge(s.s_wb, 16)
            with pe.Fori(0, BATCH) as b:
                pe.wait_ge(S["xs"], START + b + 1)
                for a in range(12):
                    if a >= 2:
                        k = min(a - 1, 8)
                        pe.wait_ge(S["qk"], START + 8 * b + k)
                        if a - 1 > 8:
                            pe.wait_ge(S["v"], START + 4 * b + a - 9)
                    if a < 2:
                        pe.wait_ge(S["pre_sb"], START + (BTILES - 1) * b)
                    sl = slice(a % 4 * SB, (a % 4 + 1) * SB)
                    if a < 8:
                        w = s.wb[:, HID:2 * HID] if a < 4 else s.wb[:, 0:HID]
                        ins = nc.tensor.matmul(pp[:, a % 2, :], w, xs[:, sl], start=True, stop=True)
                    else:
                        for t in range(SB_TILES):
                            g = a % 4 * SB_TILES + t
                            ins = nc.tensor.matmul(pp[:, a % 2, t * P:(t + 1) * P], xs[:, g * P:(g + 1) * P],
                                                   s.wb[:, 2 * HID:], start=True, stop=True)
                    ins.then_inc(S["proj"], 1)
                pe.wait_ge(S["qk"], START + 8 * (b + 1))

                def scores(g):
                    i, c, k0, n = chunk[g]
                    if g >= 2:
                        pe.wait_ge(S["copy"], START + NCH * b + g - 1)
                    nc.tensor.matmul(ps[:, g % 2, 0:n * P], qT[:, i * P:(i + 1) * P], kT[:, k0 * P:(k0 + n) * P],
                                     start=True, stop=True).then_inc(S["s"], 1)

                def turn(g):
                    i, c, k0, n = chunk[g]
                    pe.wait_ge(S["p"], START + NCH * b + g + 1)
                    pe.wait_ge(S["pt"], START + NCH * b + max(g - 1, 0))
                    for t in range(n):
                        ins = nc.tensor.transpose(pt[:, g % 2, t, :], U[:, g % UBUF, t * P:(t + 1) * P], s.ident[:, :])
                    ins.then_inc(S["t"], 1)

                def values(g):
                    i, c, k0, n = chunk[g]
                    pe.wait_ge(S["pt"], START + NCH * b + g + 1)
                    if c == 0:
                        pe.wait_ge(S["o"], START + BTILES * b + max(i - 1, 0))
                    for t in range(n):
                        ins = nc.tensor.matmul(po[:, i % 2, 0:HID + 1], pT[:, g % 2, t, :], V[:, k0 + t, :],
                                               start=(c == 0 and t == 0), stop=(k0 + t == BTILES - 1))
                    ins.then_inc(S["pv"], 1)

                for g in range(AHEAD):
                    scores(g)
                pe.wait_ge(S["v"], START + 4 * (b + 1))
                for g in range(NCH):
                    turn(g)
                    if g + AHEAD < NCH:
                        scores(g + AHEAD)
                    if g > 0:
                        values(g - 1)
                    i, c, _, _ = chunk[g]
                    if c == 0 and i > 0:
                        pe.wait_ge(S["pre_sb"], START + (BTILES - 1) * b + max(i - 2, 0))
                        nc.tensor.matmul(pp[:, i % 2, 0:HID + 1], s.ones[:, :], V[:, i - 1, :], start=True,
                                         stop=True).then_inc(S["pre"], 1)
                values(NCH - 1)

        @block.scalar
        def _(act):
            with act.Fori(0, BATCH) as b:
                for a in range(8):
                    act.wait_ge(S["proj"], START + 12 * b + a + 1)
                    if a == 0:
                        act.wait_ge(S["pv"], START + NCH * b)
                    sl = slice(a % 4 * SB, (a % 4 + 1) * SB)
                    if a < 4:
                        ins = nc.scalar.copy(kT[:, sl], pp[:, a % 2, :])
                    else:
                        ins = nc.scalar.mul(qT[:, sl], pp[:, a % 2, :], float(HID) ** -0.5 / MASKED)
                    ins.then_inc(S["qk"], 1)

                def copy(g):
                    i, c, k0, n = chunk[g]
                    act.wait_ge(S["s"], START + NCH * b + g + 1)
                    if g >= UBUF:
                        act.wait_ge(S["t"], START + NCH * b + g - UBUF + 1)
                    nc.scalar.copy(U[:, g % UBUF, 0:n * P], ps[:, g % 2, 0:n * P]).then_inc(S["copy"], 1)

                def exponentials(g):
                    i, c, k0, n = chunk[g]
                    bias = st[:, i % UBUF, 1:2]
                    if c == 0:
                        act.wait_ge(S["bias"], START + BTILES * b + i + 1)
                        nc.scalar.activation(st[:, i % UBUF, 2:3], s.ones[:, 0:1], ACT.Exp, scale=-MASKED,
                                             bias=bias).then_inc(S["w0"], 1)
                    sl = U[:, g % UBUF, 0:n * P]
                    nc.scalar.activation(sl, sl, ACT.Exp, scale=-MASKED, bias=bias).then_inc(S["p"], 1)

                def read(g):
                    n = chunk[g][3]
                    act.wait_ge(S["t"], START + NCH * b + g + 1)
                    if g >= 2:
                        act.wait_ge(S["pv"], START + NCH * b + g - 1)
                    nc.scalar.copy(pT[:, g % 2, 0:n, :], pt[:, g % 2, 0:n, :]).then_inc(S["pt"], 1)

                for g in range(AHEAD - 1):
                    copy(g)
                exponentials(0)
                for g in range(NCH):
                    if g + AHEAD - 1 < NCH:
                        copy(g + AHEAD - 1)
                    if g + 1 < NCH:
                        exponentials(g + 1)
                    read(g)

        @block.vector
        def _(dve):
            ch = Chain(dve, S["chain"])
            nc.vector.memset(V[:, :, HID:], 1.0).then_inc(S["ones"], 1)
            dve.wait_ge(S["tri"], START + 2)
            with dve.Fori(0, BATCH) as b:
                ch.enter(0, b, MARKS)
                dve.wait_ge(S["proj"], START + 12 * b)
                nc.vector.tensor_copy(xs[:, :], s.xT[:, bass.ts(b, SEQ)]).then_inc(S["xs"], 1)
                for a in range(8, 12):
                    dve.wait_ge(S["proj"], START + 12 * b + a + 1)
                    if a == 8:
                        dve.wait_ge(S["pv"], START + NCH * b)
                        dve.wait_ge(S["pre"], START + (BTILES - 1) * b)
                    g = a % 4 * SB_TILES
                    nc.vector.tensor_copy(V[:, g:g + SB_TILES, 0:HID],
                                          pp[:, a % 2, :].rearrange("p (t d) -> p t d", t=SB_TILES)).then_inc(S["v"], 1)

                def take(g):
                    i, c, k0, n = chunk[g]
                    if c == 0 and i >= UBUF:
                        dve.wait_ge(S["p"], START + NCH * b + first[i - UBUF + 1])
                    dve.wait_ge(S["copy"], START + NCH * b + g + 1)
                    to = U[:, g % UBUF, 0:n * P]
                    if c == 0:
                        ch.link(nc.vector.tensor_tensor(to[:, 0:P], to[:, 0:P], tri[:, :], ALU.mult))
                    nc.vector.scalar_tensor_tensor(to, to, 0.0, to, ALU.is_equal, ALU.subtract).then_inc(S["u"], 1)
                    dve.wait_ge(S["u"], START + NCH * b + g + 1)
                    ch.mark(nc.vector.tensor_reduce(mn[:, i % UBUF, c:c + 1], to, AX_X, ALU.min))
                    if c == len(chunks[i]) - 1:
                        ch.wait()
                        ch.link(nc.vector.tensor_reduce(st[:, i % UBUF, 0:1], mn[:, i % UBUF, 0:c + 1], AX_X, ALU.min))
                        nc.vector.tensor_scalar(st[:, i % UBUF, 1:2], st[:, i % UBUF, 0:1], MASKED, None,
                                                ALU.mult).then_inc(S["bias"], 1)

                def finish(i):
                    if i > 0:
                        dve.wait_ge(S["pre"], START + (BTILES - 1) * b + i)
                        if i == 1:
                            nc.vector.tensor_copy(pre[:, :], pp[:, i % 2, 0:HID + 1]).then_inc(S["pre_sb"], 1)
                        else:
                            nc.vector.tensor_tensor(pre[:, :], pre[:, :], pp[:, i % 2, 0:HID + 1],
                                                    ALU.add).then_inc(S["pre_sb"], 1)
                        dve.wait_ge(S["pre_sb"], START + (BTILES - 1) * b + i)
                    dve.wait_ge(S["pv"], START + NCH * b + first[i + 1])
                    if i > 0:
                        dve.wait_ge(S["w0"], START + BTILES * b + i + 1)
                        ins = nc.vector.scalar_tensor_tensor(oo[:, :], pre[:, :], st[:, i % UBUF, 2:3],
                                                             po[:, i % 2, 0:HID + 1], ALU.mult, ALU.add)
                    else:
                        ins = nc.vector.tensor_copy(oo[:, :], po[:, 0, 0:HID + 1])
                    ins.then_inc(S["o"], 1)
                    dve.wait_ge(S["o"], START + BTILES * b + i + 1)
                    ch.link(nc.vector.reciprocal(st[:, i % UBUF, 3:4], oo[:, HID:]))
                    own = s.x[:, b * BTILES + i, :]
                    ch.mark(nc.vector.scalar_tensor_tensor(own, oo[:, 0:HID], st[:, i % UBUF, 3:4], own,
                                                           ALU.mult, ALU.add))

                for g in range(AHEAD - 1):
                    take(g)
                for g in range(NCH):
                    if g + AHEAD - 1 < NCH:
                        take(g + AHEAD - 1)
                    if g >= 2 and chunk[g - 2][0] != chunk[g - 1][0]:
                        finish(chunk[g - 2][0])
                for i in range(chunk[NCH - 2][0], BTILES):
                    finish(i)
                assert ch.n == MARKS

        @block.gpsimd
        def _(pool):
            nc.gpsimd.memset(tri[:, :], 1.0).then_inc(S["tri"], 1)
            pool.wait_ge(S["tri"], START + 1)
            nc.gpsimd.affine_select(out=tri[:, :], in_=tri[:, :], compare_op=ALU.is_ge, fill=0.0, base=0,
                                    pattern=[[1, P]], channel_multiplier=-1).then_inc(S["tri"], 1)



CONSTS = 2


class Shared:
    pass


def bass_hybrid(nc, hidden, wq, wk, wv, wo, bq, bk, bv, bo4, wb, w_router, w1, b1, w2, b2, cos, sin, out, stages=5):
    with ExitStack() as ctx:
        m = Memory(nc, ctx)
        s = Shared()
        s.x = m.sb("x", [P, TILES, HID])
        s.xT = m.sb("xT", [P, TILES * P])
        s.xn = s.xT[:, :].rearrange("p (t d) -> p t d", d=HID)
        s.pick = m.sb("pick", [P, TILES, TOPK])
        s.slot = m.sb("slot", [P, TOPK, TILES], U32)
        s.yslot = m.sb("yslot", [P, TOPK, TILES], U32)
        s.emap = m.sb("emap", [P, GROUPS], I32)
        s.gmap = m.sb("gmap", [P, GROUPS], I32)
        s.groupno = m.sb("groupno", [P, GROUPS])
        s.base = m.sb("base", [P, EXPERTS])
        s.before = m.sb("before", [P, P])
        s.xg = nc.dram_tensor("xg", [XBLOCKS, GROUP, HID], F32, kind="Internal").ap()
        s.yg = nc.dram_tensor("yg", [GROUPS, GROUP, HID], F32, kind="Internal").ap()
        s.w1 = m.sb("w1", [P, EXPERTS, FFN])
        s.w2 = m.sb("w2", [P, EXPERTS, HCHUNKS, HID])
        s.b1 = m.sb("b1", [P, EXPERTS * HCHUNKS])
        s.b2 = m.sb("b2", [P, EXPERTS])
        s.w_router = m.sb("w_router", [P, EXPERTS])
        s.wb = m.sb("wb", [P, 3 * HID])
        s.ident = m.sb("ident", [P, P])
        s.ones = m.sb("ones", [P, P])
        s.zero = m.sb("zero", [P, 1])
        s.iota = m.sb("iota", [P, EXPERTS])
        s.bq, s.bk, s.bv = (m.sb(n, [P, CHUNKS]) for n in ("bq", "bk", "bv"))
        s.bo4 = m.sb("bo4", [1, SB])
        s.s_x = [m.sem(f"s_x{i}") for i in range(NSB)]
        s.s_const, s.s_small, s.s_wqkvo, s.s_rope, s.s_w1, s.s_w2, s.s_wb, s_out = (
            m.sem(n) for n in "s_const s_small s_wqkvo s_rope s_w1 s_w2 s_wb s_out".split())
        s.s_passed = m.sem("s_passed")
        small = [(s.bq, bq), (s.bk, bk), (s.bv, bv), (s.bo4, bo4), (s.b1, b1), (s.b2, b2), (s.w_router, w_router)]
        s.n_small = len(small)
        s.s_zero, s.s_zeroed, s.s_count = (m.sem(n) for n in ("s_zero", "s_zeroed", "s_count"))

        with ExitStack() as actx:
            a = Memory(nc, actx)
            s.wq, s.wk, s.wv, s.wo = (a.sb(n, [P, CHUNKS, P]) for n in ("wq", "wk", "wv", "wo"))
            zeros = a.sb("zeros", [P, XBLOCKS // ZERO_DMAS * GROUP // P * HID])
            number = a.sb("number", [P, GROUPS], I32)
            s.cos, s.sin = (a.sb(n, [P, SEQ]) for n in ("cos", "sin"))
            tokens = hidden.rearrange("b (t p) d -> p (b t) d", p=P)
            with nc.Block() as block:

                @block.sync
                def _(sp):
                    for i in range(NSB):
                        r = slice(i * SB_TILES, (i + 1) * SB_TILES)
                        sp.dma_start(s.x[:, r, :], tokens[:, r, :]).then_inc(s.s_x[i], 16)
                    for to, of in ((s.wq, wq), (s.wk, wk), (s.wv, wv), (s.wo, wo)):
                        sp.dma_start(to[:, :, :], of).then_inc(s.s_wqkvo, 16)
                    for to, of in small:
                        sp.dma_start(to[:, :], of).then_inc(s.s_small, 16)
                    for to, of in ((s.cos, cos), (s.sin, sin)):
                        sp.dma_start(to[:, :], of).then_inc(s.s_rope, 16)
                    sp.dma_start(s.w1[:, :, :], w1.rearrange("e p f -> p e f")).then_inc(s.s_w1, 16)
                    sp.dma_start(s.w2[:, :, :, :], w2.rearrange("e (c p) d -> p e c d", p=P)).then_inc(s.s_w2, 16)
                    sp.dma_start(s.wb[:, :], wb).then_inc(s.s_wb, 16)
                    sp.wait_ge(s.s_zero, 1)
                    part = s.xg.rearrange("(n j) (r p) d -> n p (j r) d", n=ZERO_DMAS, p=P)
                    for n in range(ZERO_DMAS):
                        sp.dma_start(part[n], zeros[:, :].rearrange("p (j d) -> p j d", d=HID)).then_inc(s.s_zeroed, 16)

                @block.gpsimd
                def _(pool):
                    nc.gpsimd.memset(s.ident[:, :], 0.0).then_inc(s.s_const, 1)
                    pool.wait_ge(s.s_const, 1)
                    nc.gpsimd.affine_select(out=s.ident[:, :], in_=s.ident[:, :], compare_op=ALU.not_equal,
                                            fill=1.0, base=0, pattern=[[-1, P]],
                                            channel_multiplier=1).then_inc(s.s_const, 1)
                    nc.gpsimd.memset(s.before[:, :], 1.0).then_inc(s.s_count, 1)
                    nc.gpsimd.iota(number[:, :], pattern=[[1, GROUPS]], base=0, channel_multiplier=0).then_inc(s.s_count, 1)
                    pool.wait_ge(s.s_count, 2)
                    nc.gpsimd.affine_select(out=s.before[:, :], in_=s.before[:, :], compare_op=ALU.is_gt, fill=0.0,
                                            base=0, pattern=[[1, P]], channel_multiplier=-1)
                    nc.gpsimd.tensor_copy(s.groupno[:, :], number[:, :])

                @block.vector
                def _(dve):
                    nc.vector.memset(zeros[:, :], 0.0).then_inc(s.s_zero, 1)
                    nc.vector.memset(s.ones[:, :], 1.0)
                    nc.vector.memset(s.zero[:, :], 0.0)
                    for e in range(EXPERTS):
                        nc.vector.memset(s.iota[:, e:e + 1], float(e))
                        nc.vector.memset(s.base[:, e:e + 1], float(e * BLOCKS * GROUP))
            norm_stage(nc, m, 0, s, first=True)
            window_stage(nc, m, s)
        if stages > 1:
            norm_stage(nc, m, 1, s, router=True)
            expert_stage(nc, m, 1, s)
        if stages > 2:
            norm_stage(nc, m, 2, s, collect=True)
            full_stage(nc, m, s)
        if stages > 3:
            norm_stage(nc, m, 3, s, router=True)
            expert_stage(nc, m, 3, s)
        last_stage(nc, m, s, out, s_out)


def last_stage(nc, sems, s, out, s_out):
    with ExitStack() as ctx:
        m = Memory(nc, ctx)
        got = m.sb("got", [P, TILES, TOPK, P])
        gathered = [sems.sem(f"l_got{i}") for i in range(TILES // PART)]
        S = {n: sems.sem(f"l_{n}") for n in ("chain", "sum")}
        set_up(nc, S)
        tokens = out.rearrange("b (t p) d -> p (b t) d", p=P)
        block = ctx.enter_context(nc.Block())

        @block.gpsimd
        def _(pool):
            gather(nc, pool, s, got, gathered)

        @block.vector
        def _(dve):
            ch = Chain(dve, S["chain"])
            for i in range(NSB):
                combine(nc, ch, s, got, gathered, i)
                dve.sem_inc(S["sum"], 1)

        @block.sync
        def _(sp):
            for i in range(NSB):
                sp.wait_ge(S["sum"], START + i + 1)
                r = slice(i * SB_TILES, (i + 1) * SB_TILES)
                sp.dma_start(tokens[:, r, :], s.x[:, r, :]).then_inc(s_out, 16)
            sp.wait_ge(s_out, 16 * NSB)


STAGES = 4


def kernel(**inputs):
    import numpy as _np
    import concourse.bacc as _bacc
    from concourse import mybir as _mybir
    from concourse.bass_utils import run_bass_kernel_spmd as _run

    a = {k.removeprefix("L0_"): _np.asarray(v) for k, v in inputs.items()}
    w = _np.arange(P)
    feature = (w // HD) * HD + (w % HD) // 32 * 16 + _np.where(w % 32 < 16, w % 16, HD // 2 + w % 16)
    rows = (_np.arange(CHUNKS)[:, None] * P + feature[None, :]).reshape(-1)

    def transposed(x):
        return x.T.reshape(HID, CHUNKS, P)

    inv = (_np.float32(1.0) / _np.float32(10000.0) ** (_np.arange(0, HD, 2, dtype=_np.float32) / _np.float32(HD)))
    angle = (_np.arange(SEQ, dtype=_np.float32)[None, :] * inv.astype(_np.float32)[feature % 32][:, None])
    sign = _np.where(w % 32 < 16, -1.0, 1.0)[:, None]
    arrays = {
        "hidden": a["attn_a_hidden_states"],
        "wq": transposed(a["attn_a_Wq"][rows]), "wk": transposed(a["attn_a_Wk"][rows]),
        "wv": transposed(a["attn_a_Wv"]), "wo": a["attn_a_Wo"].T.reshape(CHUNKS, P, HID).transpose(1, 0, 2),
        "bq": a["attn_a_bq"][rows].reshape(CHUNKS, P).T, "bk": a["attn_a_bk"][rows].reshape(CHUNKS, P).T,
        "bv": a["attn_a_bv"].reshape(CHUNKS, P).T, "bo4": _np.tile(a["attn_a_bo"], SB_TILES)[None, :],
        "wb": a["attn_b_W"], "w_router": a["ffn_w_router"], "w1": a["ffn_w1"],
        "b1": a["ffn_b1"].reshape(EXPERTS * HCHUNKS, P).T, "w2": a["ffn_w2"], "b2": a["ffn_b2"].T,
        "cos": _np.cos(angle.astype(_np.float64)).astype(_np.float32),
        "sin": (sign * _np.sin(angle.astype(_np.float64))).astype(_np.float32),
    }
    arrays = {f"in_{k}": _np.ascontiguousarray(v) for k, v in arrays.items()}
    nc = _bacc.Bacc("TRN2", target_bir_lowering=False, num_devices=1)
    args = [nc.dram_tensor(k, v.shape, _mybir.dt.from_np(v.dtype), kind="ExternalInput").ap() for k, v in arrays.items()]
    out = nc.dram_tensor("out_x", (BATCH, SEQ, HID), F32, kind="ExternalOutput").ap()
    bass_hybrid(nc, *args, out, stages=STAGES)
    r = _run(nc, [arrays], core_ids=[0])
    return r.results[0]["out_x"]
```

```python
from contextlib import ExitStack

import concourse.bass as bass
from concourse import mybir

F32 = mybir.dt.float32
U32 = mybir.dt.uint32
I32 = mybir.dt.int32
F32R = mybir.dt.float32r
ALU = mybir.AluOpType
ACT = mybir.ActivationFunctionType
AX_X = mybir.AxisListType.X

P = 128
BATCH, SEQ, HID = 2, 2048, 128
TILES = BATCH * SEQ // P
SB_TILES = 4
SB = SB_TILES * P
NSB = TILES // SB_TILES
SB_PER_BATCH = NSB // BATCH
EPS = 1e-5

HEADS, HD = 16, 64
CHUNKS = HEADS * HD // P
QBUF = 4
VCOLS = HD + 1
NEG = -1e30

EXPERTS, FFN, TOPK = 8, 512, 2
HCHUNKS = FFN // P
GROUP = 2 * P
GROUPS = TILES * P * TOPK // GROUP + EXPERTS
BLOCKS = TILES * P // GROUP
XBLOCKS = (EXPERTS - 1) * BLOCKS + GROUPS
PART = 8
ZERO_DMAS = XBLOCKS // 4

MASKED = 2.0 ** 53
BTILES = SEQ // P


START = 1


class Memory:

    def __init__(self, nc, ctx):
        self.nc, self.ctx = nc, ctx

    def sb(self, name, shape, dt=F32):
        return self.ctx.enter_context(self.nc.sbuf_tensor(name, shape, dt))

    def psum(self, name, shape, dt=F32):
        return self.ctx.enter_context(self.nc.psum_tensor(name, shape, dt))

    def sem(self, name):
        return self.ctx.enter_context(self.nc.semaphore(name))


class Chain:

    def __init__(self, eng, sem):
        self.eng, self.sem, self.base, self.n = eng, sem, 0, 0

    def enter(self, start, i, per):
        self.base, self.n = start + i * per, 0

    def mark(self, ins):
        self.n += 1
        return ins.then_inc(self.sem, 1)

    def wait(self):
        self.eng.wait_ge(self.sem, START + self.base + self.n)

    def link(self, ins):
        self.mark(ins)
        self.wait()


def stand_alone(eng, s):
    eng.sem_inc(s.s_passed, 1)


NORM = "chain var std xn tp"
ROUTE = NORM + " xs lg sh ex both cnt slot total"
EXPERT = "t xT xl w1 w2 h gelu y yT z yo"
SIGNALS = {
    "norm0": NORM + " xT high",
    "window": "xs xh xl q_ps k_ps v_ps q_sb k_sb v_sb q_sh k_sh q_cos k_cos q_sum k_sum q_high k_high q_rdy k_rdy "
              "k_prev v_prev s max p t pt pv norm oT oT_sb out res chain pool",
    "norm1": ROUTE + " high", "experts1": EXPERT,
    "norm2": NORM + " xT", "full": "xs proj qk v s copy u bias p w0 t pt pv pre pre_sb o chain tri",
    "norm3": ROUTE, "experts3": EXPERT,
    "last": "chain sum",
}


def window_constants(nc, pool, s):
    nc.gpsimd.memset(s.masks[:, :, :], 0.0).then_inc(s.s_mask, 1)
    pool.wait_ge(s.s_mask, 1)
    nc.gpsimd.affine_select(out=s.masks[:, :, 0:P], in_=s.masks[:, :, 0:P], compare_op=ALU.is_ge, fill=NEG,
                            base=0, pattern=[[0, SB_PER_BATCH], [1, P]], channel_multiplier=-1)
    nc.gpsimd.affine_select(out=s.masks[:, :, P:], in_=s.masks[:, :, P:], compare_op=ALU.is_ge, fill=NEG,
                            base=0, pattern=[[0, SB_PER_BATCH], [-1, P]], channel_multiplier=1).then_inc(s.s_mask, 1)
    pool.wait_ge(s.s_mask, 2)
    nc.gpsimd.tensor_copy(s.mask[:, :], s.masks[:, 1, :]).then_inc(s.s_mask, 1)
    pool.wait_ge(s.s_mask, 3)
    nc.gpsimd.memset(s.masks[:, 0, 0:P], NEG)
    for part in s.K:
        nc.gpsimd.memset(part[:, :, :].bitcast(F32), 0.0)
    nc.gpsimd.memset(s.V[:, :, :, :, :], 1.0)


def gather(nc, pool, s, got, gathered):
    rows = s.yg.rearrange("j p d -> (j p) d")
    for t in range(TILES):
        for r in range(TOPK):
            nc.gpsimd.indirect_dma_start(
                out=got[:, t, r, :], out_offset=None, in_=rows,
                in_offset=bass.IndirectOffsetOnAxis(ap=s.yslot[:, r, t:t + 1], axis=0)).then_inc(
                    gathered[t // PART], 16)


def combine(nc, ch, s, got, gathered, i):
    ch.eng.wait_ge(gathered[i * SB_TILES // PART], 16 * TOPK * PART)
    for r in range(TOPK):
        for t in range(i * SB_TILES, (i + 1) * SB_TILES):
            ins = nc.vector.scalar_tensor_tensor(s.x[:, t, :], got[:, t, r, :], s.pick[:, t, r:r + 1],
                                                 s.x[:, t, :], ALU.mult, ALU.add)
        ch.link(ins)


def norm_stage(nc, sems, tag, s, first=False, router=False, collect=False):
    split = router and not s.split
    with ExitStack() as ctx:
        m = Memory(nc, ctx)
        stats = m.sb(f"stats{tag}", [P, TILES, 6])
        mean = m.sb(f"mean{tag}", [P, TILES])
        rstd = m.sb(f"rstd{tag}", [P, TILES])
        tmp = m.sb(f"tmp{tag}", [P, 6, TILES])
        tp = m.psum(f"tp{tag}", [P, 2, SB])
        S = s.signals[f"norm{tag}"]
        if router:
            xs = m.sb(f"xs{tag}", [P, 2, SB])
            sh, ex, pr, top, tf, both, place = (m.sb(f"{n}{tag}", [P, TILES, EXPERTS])
                                                for n in "sh ex pr top tf both place".split())
            ti = m.sb(f"ti{tag}", [P, TILES, 8], U32)
            red = m.sb(f"red{tag}", [P, 3, TILES])
            hot, picked = (m.sb(f"{n}{tag}", [P, TOPK, TILES, EXPERTS]) for n in ("hot", "picked"))
            acc = m.sb(f"acc{tag}", [P, TILES + 1, EXPERTS])
            slotf = m.sb(f"slotf{tag}", [P, TOPK, TILES])
            yslotf = m.sb(f"yslotf{tag}", [P, TOPK, TILES])
            few = m.sb(f"few{tag}", [P, 7, EXPERTS])
            fewi = m.sb(f"fewi{tag}", [P, 2, EXPERTS], I32)
            past, skip = (m.sb(f"{n}{tag}", [P, GROUPS, EXPERTS]) for n in ("past", "skip"))
            emf = m.sb(f"emf{tag}", [P, 3, GROUPS])
            lg = m.psum(f"lg{tag}", [P, 2, SB])
            cnt = m.psum(f"cnt{tag}", [P, 2, SB])
            put = sems.sem(f"n_put{tag}")
        else:
            xn = m.sb(f"xn{tag}", [P, 2, SB_TILES, P])
        if collect:
            got = m.sb(f"got{tag}", [P, TILES, TOPK, P])
            gathered = [sems.sem(f"n_got{i}{tag}") for i in range(TILES // PART)]
        block = ctx.enter_context(nc.Block())
        SMALL = SB_TILES * EXPERTS

        def tiles(i):
            return slice(i * SB_TILES, (i + 1) * SB_TILES)

        def normalised(i):
            return s.xn[:, tiles(i), :] if router else xn[:, i % 2, :, :]

        if split:
            @block.sync
            def _(sp):
                for to, of in s.late:
                    sp.dma_start(to, of).then_inc(s.s_late, 16)

        @block.vector
        def _(dve):
            ch = Chain(dve, S["chain"])
            wide = [P, SB_TILES, EXPERTS]
            copy = nc.vector.tensor_copy

            def statistics(i):
                r = tiles(i)
                if first:
                    dve.wait_ge(s.s_x[i // 2], 32)
                if collect:
                    combine(nc, ch, s, got, gathered, i)
                for t in range(r.start, r.stop):
                    ins = nc.vector.bn_stats(stats[:, t, :], s.x[:, t, :])
                ch.link(ins)
                me, mo, ve, vo = (stats[:, r, k] for k in (1, 4, 2, 5))
                ch.mark(nc.vector.tensor_tensor(tmp[:, 0, r], me, mo, ALU.add))
                ch.mark(nc.vector.tensor_tensor(tmp[:, 1, r], me, mo, ALU.subtract))
                ch.link(nc.vector.tensor_tensor(tmp[:, 2, r], ve, vo, ALU.add))
                ch.mark(nc.vector.tensor_scalar(mean[:, r], tmp[:, 0, r], 0.5, None, ALU.mult))
                ch.link(nc.vector.scalar_tensor_tensor(tmp[:, 3, r], tmp[:, 1, r], 0.25, tmp[:, 1, r],
                                                       ALU.mult, ALU.mult))
                ch.link(nc.vector.scalar_tensor_tensor(tmp[:, 4, r], tmp[:, 2, r], 1.0 / HID, tmp[:, 3, r],
                                                       ALU.mult, ALU.add))
                nc.vector.tensor_scalar(tmp[:, 5, r], tmp[:, 4, r], EPS, None, ALU.add).then_inc(S["var"], 1)

            def normalise(i):
                r = tiles(i)
                dve.wait_ge(S["std"], START + i + 1)
                ch.link(nc.vector.reciprocal(rstd[:, r], tmp[:, 0, r]))
                if not router and i >= 2:
                    dve.wait_ge(S["tp"], START + i - 1)
                for k in range(SB_TILES):
                    t = i * SB_TILES + k
                    ins = nc.vector.tensor_scalar(normalised(i)[:, k, :], s.x[:, t, :], mean[:, t:t + 1],
                                                  rstd[:, t:t + 1], ALU.subtract, ALU.mult)
                ins.then_inc(S["xn"], 1)

            def shift(i):
                r = tiles(i)
                dve.wait_ge(S["lg"], START + i + 1)
                logits = lg[:, i % 2, 0:SMALL].rearrange("p (t e) -> p t e", e=EXPERTS)
                ch.link(nc.vector.tensor_reduce(red[:, 0, r], logits, AX_X, ALU.max))
                nc.vector.tensor_tensor(sh[:, r, :], logits, red[:, 0, r].unsqueeze(2).to_broadcast(wide),
                                        ALU.subtract).then_inc(S["sh"], 1)

            def choose(i):
                r = tiles(i)
                dve.wait_ge(S["ex"], START + i + 1)
                ch.link(nc.vector.tensor_reduce(red[:, 1, r], ex[:, r, :], AX_X, ALU.add))
                ch.link(nc.vector.reciprocal(red[:, 2, r], red[:, 1, r]))
                ch.link(nc.vector.tensor_tensor(pr[:, r, :], ex[:, r, :],
                                                red[:, 2, r].unsqueeze(2).to_broadcast(wide), ALU.mult))
                for t in range(r.start, r.stop):
                    ins = nc.vector.max(top[:, t, :], pr[:, t, :])
                ch.link(ins)
                for t in range(r.start, r.stop):
                    ins = nc.vector.max_index(ti[:, t, :], top[:, t, :], pr[:, t, :])
                ch.mark(ins)
                ch.link(copy(s.pick[:, r, :], top[:, r, 0:TOPK]))
                ch.link(copy(tf[:, r, :], ti[:, r, :]))
                for k in range(TOPK):
                    ch.mark(nc.vector.tensor_tensor(hot[:, k, r, :], s.iota[:, :].unsqueeze(1).to_broadcast(wide),
                                                    tf[:, r, k:k + 1].to_broadcast(wide), ALU.is_equal))
                ch.wait()
                ch.link(nc.vector.tensor_tensor(both[:, r, :], hot[:, 0, r, :], hot[:, 1, r, :], ALU.add))
                for t in range(r.start, r.stop):
                    ch.link(nc.vector.tensor_tensor(acc[:, t + 1, :], acc[:, t, :], both[:, t, :], ALU.add))
                dve.sem_inc(S["both"], 1)

            def assign(i):
                r = tiles(i)
                dve.wait_ge(S["cnt"], START + i + 1)
                before = cnt[:, i % 2, 0:SMALL].rearrange("p (t e) -> p t e", e=EXPERTS)
                ch.link(nc.vector.tensor_tensor(place[:, r, :], before,
                                                s.base[:, :].unsqueeze(1).to_broadcast(wide), ALU.add))
                for k in range(TOPK):
                    ch.mark(nc.vector.tensor_tensor(picked[:, k, r, :], hot[:, k, r, :], place[:, r, :], ALU.mult))
                ch.wait()
                ch.link(nc.vector.tensor_reduce(slotf[:, :, r], picked[:, :, r, :], AX_X, ALU.add))
                copy(s.slot[:, :, r], slotf[:, :, r]).then_inc(S["slot"], 1)

            def groups():
                dve.wait_ge(S["total"], START + 1)
                ch.link(nc.vector.tensor_scalar(fewi[:, 0, :], cnt[:, 0, 0:EXPERTS], float(GROUP - 1), None, ALU.add))
                ch.link(nc.vector.tensor_scalar(fewi[:, 1, :], fewi[:, 0, :], GROUP.bit_length() - 1, None,
                                                ALU.logical_shift_right))
                ch.link(copy(few[:, 0, :], fewi[:, 1, :]))
                a, step = 0, 1
                while step < EXPERTS:
                    ch.mark(copy(few[:, a + 1, 0:step], few[:, a, 0:step]))
                    ch.link(nc.vector.tensor_tensor(few[:, a + 1, step:], few[:, a, step:],
                                                    few[:, a, 0:EXPERTS - step], ALU.add))
                    a, step = a + 1, 2 * step
                shape = [P, GROUPS, EXPERTS]
                ch.mark(nc.vector.tensor_scalar(few[:, 4, :], few[:, 0, :], -1.0, float(BLOCKS), ALU.mult, ALU.add))
                ch.link(nc.vector.tensor_tensor(past[:, :, :], s.groupno[:, :].unsqueeze(2).to_broadcast(shape),
                                                few[:, a, :].unsqueeze(1).to_broadcast(shape), ALU.is_ge))
                ch.mark(nc.vector.tensor_reduce(emf[:, 0, :], past[:, :, 0:EXPERTS - 1], AX_X, ALU.add))
                ch.link(nc.vector.tensor_tensor(skip[:, :, :], past[:, :, :],
                                                few[:, 4, :].unsqueeze(1).to_broadcast(shape), ALU.mult))
                ch.link(nc.vector.tensor_reduce(emf[:, 1, :], skip[:, :, 0:EXPERTS - 1], AX_X, ALU.add))
                ch.link(nc.vector.tensor_tensor(emf[:, 2, :], emf[:, 1, :], s.groupno[:, :], ALU.add))
                ch.mark(copy(s.emap[:, :], emf[:, 0, :]))
                ch.mark(copy(s.gmap[:, :], emf[:, 2, :]))
                ch.link(nc.vector.tensor_tensor(few[:, 5, :], few[:, a, :], few[:, 0, :], ALU.subtract))
                ch.link(nc.vector.scalar_tensor_tensor(few[:, 6, :], few[:, 5, :], float(GROUP), s.base[:, :],
                                                       ALU.mult, ALU.subtract))
                ch.link(nc.vector.tensor_tensor(
                    picked[:, :, :, :].rearrange("p k t e -> p (k t) e"), hot[:, :, :, :].rearrange("p k t e -> p (k t) e"),
                    few[:, 6, :].unsqueeze(1).to_broadcast([P, TOPK * TILES, EXPERTS]), ALU.mult))
                ch.link(nc.vector.tensor_reduce(yslotf[:, :, :], picked[:, :, :, :], AX_X, ALU.add))
                ch.link(nc.vector.tensor_tensor(yslotf[:, :, :], yslotf[:, :, :], slotf[:, :, :], ALU.add))
                ch.mark(copy(s.yslot[:, :, :], yslotf[:, :, :]))

            if router:
                ch.link(nc.vector.memset(acc[:, 0, :], 0.0))
            for i in range(NSB + 2):
                if router and 0 <= i - 2 < NSB:
                    shift(i - 2)
                if i < NSB:
                    statistics(i)
                if 0 <= i - 1 < NSB:
                    normalise(i - 1)
                if router and 0 <= i - 2 < NSB:
                    choose(i - 2)
                    assign(i - 2)
            if router:
                groups()
            if split:
                for e in range(EXPERTS):
                    dve.wait_ge(S["high"], START + e + 1)
                    nc.vector.tensor_tensor(s.w1[:, e, :].bitcast(F32R), s.w1[:, e, :], s.w1h[:, e, :].bitcast(F32),
                                            ALU.subtract)

        @block.scalar
        def _(act):
            if first:
                act.wait_ge(s.s_wqkvo, 64)
                for w, high in ((s.wq, s.wqh), (s.wk, s.wkh)):
                    nc.scalar.copy(high[:, :, :], w[:, :, :]).then_inc(S["high"], 1)
            for i in range(NSB + 2):
                if router and 0 <= i - 2 < NSB:
                    r = tiles(i - 2)
                    act.wait_ge(S["sh"], START + i - 1)
                    nc.scalar.activation(ex[:, r, :], sh[:, r, :], ACT.Exp).then_inc(S["ex"], 1)
                if i < NSB:
                    act.wait_ge(S["var"], START + i + 1)
                    nc.scalar.activation(tmp[:, 0, tiles(i)], tmp[:, 5, tiles(i)], ACT.Sqrt).then_inc(S["std"], 1)
                if 0 <= i - 1 < NSB:
                    act.wait_ge(S["tp"], START + i)
                    if router:
                        if i >= 3:
                            act.wait_ge(S["lg"], START + i - 2)
                        nc.scalar.copy(xs[:, (i - 1) % 2, :], tp[:, (i - 1) % 2, :]).then_inc(S["xs"], 1)
                    else:
                        nc.scalar.copy(s.xT[:, (i - 1) * SB:i * SB], tp[:, (i - 1) % 2, :]).then_inc(S["xT"], 1)
            if split:
                act.wait_ge(s.s_late, 48)
                for e in range(EXPERTS):
                    nc.scalar.copy(s.w1h[:, e, :], s.w1[:, e, :]).then_inc(S["high"], 1)

        @block.tensor
        def _(pe):
            pe.wait_ge(s.s_const, CONSTS)
            if router:
                pe.wait_ge(s.s_small, 16 * s.n_small)

            def count(i):
                pe.wait_ge(S["both"], START + i + 1)
                if i >= 2:
                    pe.wait_ge(S["slot"], START + i - 1)
                to = cnt[:, i % 2, 0:SMALL]
                nc.tensor.matmul(to, s.before[:, :], both[:, tiles(i), :].rearrange("p t e -> p (t e)"),
                                 start=True, stop=False)
                nc.tensor.matmul(to, s.ones[:, :], acc[:, tiles(i), :].rearrange("p t e -> p (t e)"),
                                 start=False, stop=True).then_inc(S["cnt"], 1)

            for i in range(NSB + 1):
                if i < NSB:
                    pe.wait_ge(S["xn"], START + i + 1)
                    if i >= 2:
                        pe.wait_ge(S["xs" if router else "xT"], START + i - 1)
                    for t in range(SB_TILES):
                        ins = nc.tensor.transpose(tp[:, i % 2, t * P:(t + 1) * P], normalised(i)[:, t, :],
                                                  s.ident[:, :])
                    ins.then_inc(S["tp"], 1)
                    if router:
                        pe.wait_ge(S["xs"], START + i + 1)
                        if i >= 2:
                            pe.wait_ge(S["sh"], START + i - 1)
                        for t in range(SB_TILES):
                            ins = nc.tensor.matmul(lg[:, i % 2, t * EXPERTS:(t + 1) * EXPERTS],
                                                   xs[:, i % 2, t * P:(t + 1) * P], s.w_router[:, :],
                                                   start=True, stop=True)
                        ins.then_inc(S["lg"], 1)
                if router and i > 0:
                    count(i - 1)
            if router:
                pe.wait_ge(S["slot"], START + NSB - 1)
                nc.tensor.matmul(cnt[:, 0, 0:EXPERTS], s.ones[:, :], acc[:, TILES, :], start=True,
                                 stop=True).then_inc(S["total"], 1)

        if first or router or collect:
            @block.gpsimd
            def _(pool):
                if first:
                    window_constants(nc, pool, s)
                    for n, (w, high, low) in enumerate(((s.wq, s.wqh, s.wql), (s.wk, s.wkh, s.wkl))):
                        pool.wait_ge(S["high"], START + n + 1)
                        nc.gpsimd.tensor_tensor(low[:, :, :], w[:, :, :], high[:, :, :].bitcast(F32),
                                                ALU.subtract)
                    return
                if collect:
                    gather(nc, pool, s, got, gathered)
                    return
                pool.wait_ge(s.s_zeroed, 16 * ZERO_DMAS)
                rows = s.xg.rearrange("j p d -> (j p) d")
                for t in range(TILES):
                    if t % SB_TILES == 0:
                        pool.wait_ge(S["slot"], START + t // SB_TILES + 1)
                    for r in range(TOPK):
                        nc.gpsimd.indirect_dma_start(
                            out=rows, out_offset=bass.IndirectOffsetOnAxis(ap=s.slot[:, r, t:t + 1], axis=0),
                            in_=s.xn[:, t, :], in_offset=None).then_inc(put, 16)
                pool.wait_ge(put, 16 * TILES * TOPK)


def window_stage(nc, sems, s):
    with ExitStack() as ctx:
        m = Memory(nc, ctx)
        xs = m.sb("xs", [P, SB])
        xh, xl = (m.sb(n, [P, 2, SB], F32R) for n in ("xh", "xl"))
        Q = [m.sb(n, [P, QBUF, SB], F32R) for n in ("Qh", "Ql")]
        sums = m.sb("sums", [P, 2, SB])
        K, V, masks, mask = s.K, s.V, s.masks, s.mask
        lin, rot = s.lin, s.rot
        sc = m.sb("sc", [P, 2, 2, 2 * P])
        mx = m.sb("mx", [P, 2, 2])
        pT = m.sb("pT", [P, 2, 2, 2, P])
        rs = m.sb("rs", [P, 4])
        on = m.sb("on", [P, SB_TILES, P])
        oT = m.sb("oT", [P, SB])
        mask0 = m.sb("mask0", [P, 2 * P])
        pj = m.psum("pj", [P, SB])
        ps = m.psum("ps", [P, 2, SB])
        pt = m.psum("pt", [P, 2, 2, 2, P])
        po = m.psum("po", [P, 2, SB])
        pout = m.psum("pout", [P, SB_TILES, P])

        S = s.signals["window"]
        swap = [(w + 16) % 32 for w in range(32)]
        block = ctx.enter_context(nc.Block())

        def units(sb, c):
            u = CHUNKS * sb + c
            return u, u + 2, (c + 2) % CHUNKS, (sb if c + 2 < CHUNKS else sb + 1)

        def pos(sb):
            return bass.ts(sb % SB_PER_BATCH, SB)

        @block.tensor
        def _(pe):
            def project(high, low, c, sb):
                for n, (w, x) in enumerate(((high, xh), (high, xl), (low, xh))):
                    ins = nc.tensor.matmul(pj[:, :], w[:, c, :], x[:, bass.ds(sb % 2, 1), :].rearrange("p o t -> p (o t)"),
                                           start=(n == 0), stop=(n == 2))
                return ins

            def project_q(v, c, sb, head=False):
                pe.wait_ge(S["v_sb"], START + v + CHUNKS)
                if not head:
                    pe.wait_ge(S["oT_sb"], START + v - 1)
                project(s.wqh, s.wql, c, sb).then_inc(S["q_ps"], 1)

            def project_k(v, c, sb):
                pe.wait_ge(S["q_sb"], START + v + 1)
                project(s.wkh, s.wkl, c, sb).then_inc(S["k_ps"], 1)

            def project_v(v, c):
                pe.wait_ge(S["k_sb"], START + v + 1)
                for t in range(SB_TILES):
                    ins = nc.tensor.matmul(pj[:, t * P:(t + 1) * P], xs[:, t * P:(t + 1) * P], s.wv[:, c, :],
                                           start=True, stop=True)
                ins.then_inc(S["v_ps"], 1)

            def scores(c, b, u, G, first=False):
                if b == 0:
                    pe.wait_ge(S["q_rdy"], START + u + 1)
                    pe.wait_ge(S["k_rdy"], START + u + 1 + CHUNKS)
                for h in range(2):
                    if not first:
                        pe.wait_ge(S["max"], START + 2 * G - 1 + h)
                    r = slice(h * HD, (h + 1) * HD)
                    for n, (i, j) in enumerate(((0, 0), (0, 1), (1, 0))):
                        ins = nc.tensor.matmul(ps[:, h, 0:2 * P], Q[i][r, c % QBUF, b * P:(b + 1) * P],
                                               K[j][r, c, b * P:(b + 2) * P], start=(n == 0), stop=(n == 2))
                ins.then_inc(S["s"], 1)

            def transposes(b, G, first=False):
                pe.wait_ge(S["p"], START + 2 * G + 2)
                if not first:
                    pe.wait_ge(S["pt"], START + G - 1)
                for h in range(2):
                    for kb in range(2):
                        ins = nc.tensor.transpose(pt[:, b % 2, h, kb, :], sc[:, b % 2, h, kb * P:(kb + 1) * P],
                                                  s.ident[:, :])
                ins.then_inc(S["t"], 1)

            def values(c, b, u, G):
                pe.wait_ge(S["pt"], START + G + 1)
                if b == 0:
                    pe.wait_ge(S["v_sb"], START + u + 1 + CHUNKS)
                    pe.wait_ge(S["v_prev"], START + u + 1)
                if b == 0:
                    pe.wait_ge(S["norm"], START + 2 * u)
                for h in range(2):
                    for kb in range(2):
                        ins = nc.tensor.matmul(po[:, b // 2, (b % 2 * 2 + h) * VCOLS:(b % 2 * 2 + h + 1) * VCOLS], pT[:, b % 2, h, kb, :], V[:, c, b + kb, h, :],
                                               start=(kb == 0), stop=(kb == 1))
                ins.then_inc(S["pv"], 1)

            def turn_out(u):
                pe.wait_ge(S["norm"], START + 2 * u + 2)
                pe.wait_ge(S["v_sb"], START + u + 3 + CHUNKS)
                for t in range(SB_TILES):
                    ins = nc.tensor.transpose(pj[:, t * P:(t + 1) * P], on[:, t, :], s.ident[:, :])
                ins.then_inc(S["oT"], 1)

            def start_out():
                nc.tensor.matmul(pout[:, :, :].rearrange("p a b -> p (a b)"), s.ones[0:1, :], s.bo4[0:1, :],
                                 start=True, stop=False, skip_group_check=True)

            def project_out(u, c, sb):
                if c == 0:
                    pe.wait_ge(S["res"], START + sb + 1)
                    start_out()
                pe.wait_ge(S["oT_sb"], START + u + 2)
                for t in range(SB_TILES):
                    ins = nc.tensor.matmul(pout[:, t, :], oT[:, t * P:(t + 1) * P], s.wo[:, c, :],
                                           start=False, stop=(c == CHUNKS - 1), skip_group_check=True)
                ins.then_inc(S["out"], 1)

            pe.wait_ge(s.s_wqkvo, 64)
            pe.wait_ge(s.s_small, 16 * s.n_small)
            pe.sem_inc(S["oT"], CHUNKS - 1)
            start_out()
            pe.wait_ge(S["xs"], START + 1)
            pe.wait_ge(S["xl"], START + 1)
            for v in range(2):
                project_q(v, v, 0, head=True)
                project_k(v, v, 0)
                project_v(v, v)
            scores(0, 0, 0, 0, first=True)
            scores(0, 1, 0, 1)
            transposes(0, 0, first=True)
            with pe.Fori(0, NSB) as sb:
                for c in range(CHUNKS):
                    u, v, vc, vsb = units(sb, c)
                    for b in range(SB_TILES):
                        G = SB_TILES * u + b
                        if b < 2:
                            scores(c, b + 2, u, G + 2)
                        else:
                            scores((c + 1) % CHUNKS, b - 2, u + 1, G + 2)
                        transposes((b + 1) % SB_TILES, G + 1)
                        if b == 0:
                            turn_out(u - 1)
                        if b == 2:
                            project_out(u - 1, (c - 1) % CHUNKS, sb)
                            project_k(v, vc, vsb)
                        if b == 3:
                            project_v(v, vc)
                        values(c, b, u, G)
                        if b == 1:
                            if vc == 0:
                                pe.wait_ge(S["xs"], START + vsb + 1)
                                pe.wait_ge(S["xl"], START + vsb + 1)
                            project_q(v, vc, vsb)
            turn_out(CHUNKS * NSB - 1)
            project_out(CHUNKS * NSB - 1, CHUNKS - 1, NSB - 1)

        @block.scalar
        def _(act):
            def probabilities(b, G):
                act.wait_ge(S["max"], START + 2 * G + 2)
                for h in range(2):
                    nc.scalar.activation(sc[:, b % 2, h, :], sc[:, b % 2, h, :], ACT.Exp, scale=-1.0,
                                         bias=mx[:, b % 2, h:h + 1]).then_inc(S["p"], 1)

            def read_pt(b, G, first=False):
                act.wait_ge(S["t"], START + G + 1)
                if not first:
                    act.wait_ge(S["pv"], START + G - 1)
                nc.scalar.copy(pT[:, b % 2, :, :, :], pt[:, b % 2, :, :, :]).then_inc(S["pt"], 1)

            def read_q(v, c, v0=False):
                act.wait_ge(S["q_ps"], START + v + 1)
                if not v0:
                    act.wait_ge(S["q_sum"], START + v)
                nc.scalar.activation(lin[:, 0, :], pj[:, :], ACT.Identity, bias=s.bq[:, c:c + 1]).then_inc(S["q_sb"], 1)

            def read_k(v, c, v0=False):
                act.wait_ge(S["k_ps"], START + v + 1)
                if not v0:
                    act.wait_ge(S["k_sum"], START + v)
                nc.scalar.activation(lin[:, 1, :], pj[:, :], ACT.Identity, bias=s.bk[:, c:c + 1]).then_inc(S["k_sb"], 1)

            def high(v, c, which):
                act.wait_ge(S["k_sum" if which else "q_sum"], START + v + 1)
                if which:
                    act.wait_ge(S["k_prev"], START + v + 1)
                to = K[0][:, c, P:] if which else Q[0][:, c % QBUF, :]
                nc.scalar.copy(to, sums[:, which, :]).then_inc(S["k_high" if which else "q_high"], 1)

            def high_x(sb):
                nc.scalar.copy(xh[:, bass.ds(sb % 2, 1), :].rearrange("p o t -> p (o t)"),
                               s.xT[:, bass.ts(sb % NSB, SB)]).then_inc(S["xh"], 1)

            def read_out(u, c):
                act.wait_ge(S["oT"], START + u + 1 + CHUNKS)
                act.wait_ge(S["out"], START + u + 1)
                nc.scalar.activation(oT[:, :], pj[:, :], ACT.Identity, bias=s.bv[:, c:c + 1]).then_inc(S["oT_sb"], 1)

            act.wait_ge(s.s_small, 16 * s.n_small)
            high_x(0)
            for v in range(2):
                read_q(v, v, v0=(v == 0))
                read_k(v, v, v0=(v == 0))
                high(v, v, 0)
                if v == 0:
                    high(0, 0, 1)
            probabilities(0, 0)
            probabilities(1, 1)
            read_pt(0, 0, first=True)
            with act.Fori(0, NSB) as sb:
                for c in range(CHUNKS):
                    u, v, vc, vsb = units(sb, c)
                    for b in range(SB_TILES):
                        G = SB_TILES * u + b
                        probabilities((b + 2) % SB_TILES, G + 2)
                        read_pt((b + 1) % SB_TILES, G + 1)
                        if b == 0:
                            high(u + 1, (c + 1) % CHUNKS, 1)
                        if b == 0:
                            read_out(u - 1, (c - 1) % CHUNKS)
                        if b == 1:
                            read_q(v, vc)
                        if b == 3:
                            high(v, vc, 0)
                        if b == 3 and c == 2:
                            act.wait_ge(S["k_ps"], START + CHUNKS * sb)
                            high_x(sb + 1)
                        if b == 2:
                            read_k(v, vc)
            read_out(CHUNKS * NSB - 1, CHUNKS - 1)

        @block.vector
        def _(dve):
            ch = Chain(dve, S["chain"])

            def maxima(c, b, G, first=False):
                dve.wait_ge(S["s"], START + G + 1)
                if not first:
                    dve.wait_ge(S["t"], START + G - 1)
                stand_alone(dve, s)
                for h in range(2):
                    nc.vector.tensor_tensor_reduce(sc[:, b % 2, h, :], ps[:, h, 0:2 * P],
                                                   (mask0 if b == 0 else mask)[:, :], -float(HD) ** -0.5, 3e38,
                                                   ALU.add, ALU.min, mx[:, b % 2, h:h + 1]).then_inc(S["max"], 1)

            def turn(v, sb, which, src, w0):
                dve.wait_ge(S[src], START + v + 1)
                if not w0:
                    dve.wait_ge(S["k_sum" if which else "q_sum"], START + v)
                stand_alone(dve, s)
                nc.vector.stream_shuffle(rot[:, which, :], lin[:, which, :], swap).then_inc(
                    S["q_sh" if which == 0 else "k_sh"], 1)
                nc.vector.tensor_tensor(lin[:, which, :], lin[:, which, :], s.cos[:, pos(sb)], ALU.mult).then_inc(
                    S["q_cos" if which == 0 else "k_cos"], 1)

            def low(v, c, which):
                dve.wait_ge(S["k_high" if which else "q_high"], START + v + 1)
                to, high = (x[:, c, P:] if which else x[:, c % QBUF, :] for x in ((K if which else Q)[1], (K if which else Q)[0]))
                nc.vector.tensor_tensor(to, sums[:, which, :], high.bitcast(F32), ALU.subtract).then_inc(
                    S["k_rdy" if which else "q_rdy"], 1)

            def keep_v(v, c):
                dve.wait_ge(S["v_ps"], START + v + 1)
                dve.wait_ge(S["v_prev"], START + v + 1)
                nc.vector.tensor_copy(V[:, c, 1:, :, 0:HD],
                                      pj[:, :].rearrange("p (t h d) -> p t h d", t=SB_TILES, h=2)).then_inc(S["v_sb"], 1)

            def normalise(u, b, G):
                dve.wait_ge(S["pv"], START + G + 1)
                pair = po[:, b // 2, 0:4 * VCOLS].rearrange("p (a d) -> p a d", a=4)
                ch.link(nc.vector.reciprocal(rs[:, :], pair[:, :, HD]))
                if b == 1:
                    dve.wait_ge(S["oT"], START + u + CHUNKS)
                nc.vector.tensor_tensor(
                    on[:, b - 1:b + 1, :].rearrange("p a (h d) -> p (a h) d", h=2),
                    pair[:, :, 0:HD],
                    rs[:, :].unsqueeze(2).to_broadcast([P, 4, HD]), ALU.mult).then_inc(S["norm"], 1)

            def add_out(sb):
                dve.wait_ge(S["out"], START + CHUNKS * sb + 1)
                own = s.padded[:, bass.ts(sb, SB_TILES), :]
                nc.vector.tensor_tensor(own, own, pout[:, :, :], ALU.add).then_inc(S["res"], 1)

            dve.wait_ge(s.s_rope, 32)
            ch.link(nc.vector.memset(on[:, :, :], 0.0))
            dve.sem_inc(S["v_sb"], CHUNKS)
            ch.link(nc.vector.tensor_copy(mask0[:, :], masks[:, 0, :]))
            for v in range(2):
                turn(v, 0, 0, "q_sb", v == 0)
                turn(v, 0, 1, "k_sb", v == 0)
                keep_v(v, v)
                if v == 0:
                    low(0, 0, 0)
                    low(0, 0, 1)
            maxima(0, 0, 0, first=True)
            maxima(0, 1, 1, first=True)
            start = ch.base + ch.n
            with dve.Fori(0, NSB) as sb:
                ch.enter(start, sb, 2 * CHUNKS + 1)
                for c in range(CHUNKS):
                    u, v, vc, vsb = units(sb, c)
                    for b in range(SB_TILES):
                        G = SB_TILES * u + b
                        if b == 2 and c == CHUNKS - 1:
                            ch.link(nc.vector.tensor_copy(mask0[:, :], masks[:, (sb + 1) % SB_PER_BATCH, :]))
                        maxima(c, (b + 2) % SB_TILES, G + 2)
                        if b == 1:
                            low(u + 1, (c + 1) % CHUNKS, 1)
                        if b == 0:
                            low(u + 1, (c + 1) % CHUNKS, 0)
                        if b == 2:
                            turn(v, vsb, 0, "q_sb", False)
                            turn(v, vsb, 1, "k_sb", False)
                        if b == 3:
                            keep_v(v, vc)
                        if b % 2 == 1:
                            normalise(u, b, G)
                        if c == 0 and b == 3:
                            add_out(sb)
            add_out(NSB)

        @block.sync
        def _(sp):
            sp.wait_ge(s.s_zero, 1)
            part = s.xg.rearrange("(n j) (r p) d -> n p (j r) d", n=ZERO_DMAS, p=P)
            for n in range(ZERO_DMAS):
                sp.dma_start(part[n], s.zeros[:, :].unsqueeze(1).to_broadcast(
                    [P, XBLOCKS // ZERO_DMAS * GROUP // P, HID])).then_inc(s.s_zeroed, 16)
            sp.wait_ge(s.s_zeroed, 16 * ZERO_DMAS)

        @block.gpsimd
        def _(pool):
            ch = Chain(pool, S["pool"])
            pool.sem_inc(S["k_rdy"], CHUNKS)
            def low_x(sb):
                pool.wait_ge(S["xh"], START + sb + 1)
                stand_alone(pool, s)
                half = [x[:, bass.ds(sb % 2, 1), :].rearrange("p o t -> p (o t)") for x in (xh, xl)]
                nc.gpsimd.tensor_tensor(half[1], s.xT[:, bass.ts(sb % NSB, SB)], half[0].bitcast(F32),
                                        ALU.subtract).then_inc(S["xl"], 1)

            pool.wait_ge(s.s_rope, 32)
            nc.gpsimd.tensor_copy(xs[:, :], s.xT[:, 0:SB]).then_inc(S["xs"], 1)

            def rotate(v, c, sb, which):
                pool.wait_ge(S["q_sh" if which == 0 else "k_sh"], START + v + 1)
                stand_alone(pool, s)
                nc.gpsimd.tensor_tensor(rot[:, which, :], rot[:, which, :], s.sin[:, pos(sb)], ALU.mult).then_inc(S["pool"], 1)
                ch.n += 1
                ch.wait()
                pool.wait_ge(S["q_cos" if which == 0 else "k_cos"], START + v + 1)
                pool.wait_ge(S["k_rdy" if which else "q_rdy"], START + v + (CHUNKS if which else 0))
                stand_alone(pool, s)
                nc.gpsimd.tensor_tensor(sums[:, which, :], lin[:, which, :], rot[:, which, :], ALU.add).then_inc(
                    S["k_sum" if which else "q_sum"], 1)

            def unit(v, c, sb):
                pool.wait_ge(S["oT"], START + v + 1)
                pool.wait_ge(S["k_rdy"], START + v + CHUNKS)
                stand_alone(pool, s)
                nc.gpsimd.tensor_copy(K[0][:, c, 0:P], K[0][:, c, SB:])
                nc.gpsimd.tensor_copy(K[1][:, c, 0:P], K[1][:, c, SB:]).then_inc(S["k_prev"], 1)
                pool.wait_ge(S["v_sb"], START + v + CHUNKS)
                stand_alone(pool, s)
                nc.gpsimd.tensor_copy(V[:, c, 0, :, :], V[:, c, SB_TILES, :, :]).then_inc(S["v_prev"], 1)
                rotate(v, c, sb, 0)
                rotate(v, c, sb, 1)

            low_x(0)
            for v in range(2):
                unit(v, v, 0)
            start = ch.base + ch.n
            with pool.Fori(0, NSB) as sb:
                ch.enter(start, sb, 2 * CHUNKS)
                for c in range(CHUNKS):
                    u, v, vc, vsb = units(sb, c)
                    if vc == 0:
                        pool.wait_ge(S["v_ps"], START + CHUNKS * (sb + 1))
                        stand_alone(pool, s)
                        nc.gpsimd.tensor_copy(xs[:, :], s.xT[:, bass.ts((sb + 1) % NSB, SB)]).then_inc(S["xs"], 1)
                    if c == 3:
                        low_x(sb + 1)
                    unit(v, vc, vsb)


def expert_stage(nc, sems, tag, s):
    with ExitStack() as ctx:
        m = Memory(nc, ctx)
        xt = m.sb(f"xt{tag}", [P, 4, GROUP // P, P])
        xh, xl = (m.sb(f"{n}{tag}", [P, 2, GROUP], F32R) for n in ("xh", "xl"))
        w1s = m.sb(f"w1s{tag}", [P, 2, 2, FFN], F32R)
        w2s = m.sb(f"w2s{tag}", [P, 2, HCHUNKS, P])
        hT = m.sb(f"hT{tag}", [P, 2, HCHUNKS, GROUP])
        yT = m.sb(f"yT{tag}", [P, 2, GROUP])
        yo = m.sb(f"yo{tag}", [P, 2, GROUP // P, P])
        px = m.psum(f"px{tag}", [P, SB])
        ph = m.psum(f"ph{tag}", [P, 2, HCHUNKS, GROUP])
        py = m.psum(f"py{tag}", [P, 2, SB])
        pz = m.psum(f"pz{tag}", [P, SB])
        S = s.signals[f"experts{tag}"]
        load = [sems.sem(f"e_load{k}{tag}") for k in range(4)]
        stored = [sems.sem(f"e_stored{k}{tag}") for k in range(2)]
        block = ctx.enter_context(nc.Block())
        STEP = 4
        ROUNDS = GROUPS // STEP

        def steps(eng, body, ahead=None):
            def turn(jj):
                es = []
                if ahead is not None:
                    es = [expert(eng, STEP * jj + a) for a in range(STEP + ahead)
                          if not isinstance(jj, int) or STEP * jj + a < GROUPS]
                for k in range(STEP):
                    body(jj, k, *([es[k:]] if es else []))

            rounds(eng, turn)

        def rounds(eng, turn):
            turn(0)
            with eng.Fori(0, ROUNDS - 2) as i:
                turn(i + 1)
            turn(ROUNDS - 1)

        def turns(eng, body):
            def turn(jj):
                gs = [place(eng, STEP * jj + a) if not isinstance(jj, int) or 0 <= STEP * jj + a < GROUPS else None
                      for a in range(2 * STEP)]
                for k in range(STEP):
                    body(jj, k, gs[k:])

            rounds(eng, turn)

        def outside(jj, k, ahead):
            return isinstance(jj, int) and not 0 <= STEP * jj + k + ahead < GROUPS

        def expert(eng, j):
            return eng.value_load(s.emap[0:1, bass.ds(j, 1)], min_val=0, max_val=EXPERTS - 1)

        def place(eng, j):
            return eng.value_load(s.gmap[0:1, bass.ds(j, 1)], min_val=0, max_val=XBLOCKS - 1)

        def rows(dram, j):
            return dram[bass.ds(j, 1), :, :].rearrange("o (p r) d -> p (o r) d", r=GROUP // P)

        @block.sync
        def _(sp):
            def fetch(g, k):
                sp.dma_start(xt[:, k, :, :], rows(s.xg, g)).then_inc(load[k], 16)

            def body(jj, k, gs):
                j = STEP * jj + k
                if not outside(jj, k, STEP):
                    sp.wait_ge(S["t"], START + j + 1)
                    fetch(gs[STEP], k)
                if not outside(jj, k, -1):
                    sp.wait_ge(S["yo"], START + j)
                    store(j - 1, k + 1)

            def store(j, k):
                sp.dma_start(rows(s.yg, j), yo[:, k % 2, :, :]).then_inc(stored[k % 2], 16)

            for k in range(STEP):
                fetch(place(sp, k), k)
            turns(sp, body)
            sp.wait_ge(S["yo"], START + GROUPS)
            store(GROUPS - 1, GROUPS - 1)
            for k in range(2):
                sp.wait_ge(stored[k], 16 * (GROUPS // 2))

        @block.tensor
        def _(pe):
            def turn(j, k, nth):
                pe.wait_ge(load[k % STEP], 16 * nth)
                for r in range(GROUP // P):
                    ins = nc.tensor.transpose(px[:, r * P:(r + 1) * P], xt[:, k % STEP, r, :], s.ident[:, :])
                ins.then_inc(S["t"], 1)

            def hidden(j, k):
                pe.wait_ge(S["xl"], START + j + 1)
                pe.wait_ge(S["w1"], START + j + 1)
                for i in range(HCHUNKS):
                    w = [w1s[:, k % 2, a, i * P:(i + 1) * P] for a in range(2)]
                    for n, (a, x) in enumerate(((0, xh), (0, xl), (1, xh))):
                        ins = nc.tensor.matmul(ph[:, k % 2, i, :], w[a], x[:, k % 2, :], start=(n == 0), stop=(n == 2))
                ins.then_inc(S["h"], 1)

            def turn_back(j, k):
                pe.wait_ge(S["yT"], START + j + 1)
                for r in range(GROUP // P):
                    ins = nc.tensor.transpose(pz[:, r * P:(r + 1) * P], yT[:, k % 2, r * P:(r + 1) * P], s.ident[:, :])
                ins.then_inc(S["z"], 1)

            def body(jj, k):
                j = STEP * jj + k
                if not outside(jj, k, 2):
                    pe.wait_ge(S["xl"], START + j + 2)
                    turn(j + 2, k + 2, jj + 1 + (k + 2) // STEP)
                if not outside(jj, k, 1):
                    if not outside(jj, k, -1):
                        pe.wait_ge(S["gelu"], START + HCHUNKS * j)
                    hidden(j + 1, k + 1)
                if not outside(jj, k, -1):
                    if not outside(jj, k, -2):
                        pe.wait_ge(S["yo"], START + j - 1)
                    turn_back(j - 1, k + 1)
                pe.wait_ge(S["gelu"], START + HCHUNKS * (j + 1))
                pe.wait_ge(S["w2"], START + j + 1)
                if not outside(jj, k, -2):
                    pe.wait_ge(S["yT"], START + j - 1)
                for i in range(HCHUNKS):
                    ins = nc.tensor.matmul(py[:, k % 2, 0:GROUP], w2s[:, k % 2, i, :], hT[:, k % 2, i, :],
                                           start=(i == 0), stop=(i == HCHUNKS - 1))
                ins.then_inc(S["y"], 1)

            turn(0, 0, 1)
            pe.wait_ge(S["xl"], START + 1)
            turn(1, 1, 1)
            hidden(0, 0)
            steps(pe, body)
            pe.wait_ge(S["yo"], START + GROUPS - 1)
            turn_back(GROUPS - 1, GROUPS - 1)

        @block.scalar
        def _(act):
            def read(j, k):
                act.wait_ge(S["t"], START + j + 1)
                nc.scalar.copy(xh[:, k % 2, :], px[:, 0:GROUP]).then_inc(S["xT"], 1)

            def gelu(j, k, e):
                act.wait_ge(S["h"], START + j + 1)
                for i in range(HCHUNKS):
                    nc.scalar.activation(hT[:, k % 2, i, :], ph[:, k % 2, i, :], ACT.Gelu_apprx_tanh,
                                         bias=s.b1[:, bass.ds(e * HCHUNKS + i, 1)]).then_inc(S["gelu"], 1)

            def body(jj, k, es):
                j = STEP * jj + k
                if not outside(jj, k, 2):
                    act.wait_ge(S["h"], START + j + 1)
                    read(j + 2, k + 2)
                if not outside(jj, k, 1):
                    if not outside(jj, k, -1):
                        act.wait_ge(S["y"], START + j)
                    gelu(j + 1, k + 1, es[1])
                if not outside(jj, k, -2):
                    act.wait_ge(S["z"], START + j - 1)
                act.wait_ge(S["y"], START + j + 1)
                nc.scalar.activation(yT[:, k % 2, :], py[:, k % 2, 0:GROUP], ACT.Identity,
                                     bias=s.b2[:, bass.ds(es[0], 1)]).then_inc(S["yT"], 1)

            e = expert(act, 0)
            read(0, 0)
            read(1, 1)
            gelu(0, 0, e)
            steps(act, body, 1)

        @block.vector
        def _(dve):
            def first_weights(j, k, e):
                nc.vector.tensor_copy(w1s[:, k % 2, 0, :], s.w1h[:, e, :])
                nc.vector.tensor_copy(w1s[:, k % 2, 1, :], s.w1[:, e, :].bitcast(F32R)).then_inc(S["w1"], 1)

            def low_x(j, k):
                dve.wait_ge(S["xT"], START + j + 1)
                nc.vector.tensor_tensor(xl[:, k % 2, :], px[:, 0:GROUP], xh[:, k % 2, :].bitcast(F32),
                                        ALU.subtract).then_inc(S["xl"], 1)

            def second_weights(j, k, e):
                nc.vector.tensor_copy(w2s[:, k % 2, :, :], s.w2[:, e, :, :]).then_inc(S["w2"], 1)

            def keep(j, k):
                dve.wait_ge(S["z"], START + j + 1)
                nc.vector.tensor_copy(yo[:, k % 2, :, :], pz[:, 0:GROUP].rearrange("p (r d) -> p r d", d=P)).then_inc(
                    S["yo"], 1)

            def body(jj, k, es):
                j = STEP * jj + k
                if not outside(jj, k, 2):
                    dve.wait_ge(S["h"], START + j + 1)
                    first_weights(j + 2, k + 2, es[2])
                    low_x(j + 2, k + 2)
                if not outside(jj, k, -1):
                    if not outside(jj, k, -3):
                        dve.wait_ge(stored[(k + 1) % 2], 16 * (2 * jj + (k - 1) // 2))
                    keep(j - 1, k + 1)
                if not outside(jj, k, 1):
                    if not outside(jj, k, -1):
                        dve.wait_ge(S["y"], START + j)
                    second_weights(j + 1, k + 1, es[1])

            e0, e1 = expert(dve, 0), expert(dve, 1)
            first_weights(0, 0, e0)
            first_weights(1, 1, e1)
            low_x(0, 0)
            low_x(1, 1)
            second_weights(0, 0, e0)
            steps(dve, body, 2)
            dve.wait_ge(stored[1], 16 * (GROUPS // 2 - 1))
            keep(GROUPS - 1, GROUPS - 1)


def full_stage(nc, sems, s):
    AHEAD = 7
    UBUF = AHEAD + 3
    with ExitStack() as ctx:
        m = Memory(nc, ctx)
        xs = m.sb("bxs", [P, SEQ])
        qT = m.sb("qT", [P, SEQ])
        kT = m.sb("kT", [P, SEQ])
        V = m.sb("bV", [P, BTILES, HID + 1])
        U = m.sb("U", [P, UBUF, SB])
        tri = m.sb("tri", [P, P])
        mn = m.sb("mn", [P, UBUF, BTILES // 4])
        st = m.sb("st", [P, UBUF, 4])
        pT = m.sb("bpT", [P, 2, 4, P])
        pre = m.sb("pre", [P, HID + 1])
        oo = m.sb("oo", [P, HID + 1])
        pp = m.psum("pp", [P, 2, SB])
        ps = m.psum("bps", [P, 2, SB])
        pt = m.psum("bpt", [P, 2, 4, P])
        po = m.psum("bpo", [P, 2, SB])
        S = s.signals["full"]
        block = ctx.enter_context(nc.Block())
        chunks = [[(k, min(4, BTILES - k)) for k in range(i, BTILES, 4)] for i in range(BTILES)]
        first = [sum(len(c) for c in chunks[:i]) for i in range(BTILES + 1)]
        NCH = first[-1]
        MARKS = 4 * BTILES + NCH
        chunk = [(i, c, k0, n) for i in range(BTILES) for c, (k0, n) in enumerate(chunks[i])]

        @block.tensor
        def _(pe):
            pe.wait_ge(s.s_late, 48)
            with pe.Fori(0, BATCH) as b:
                pe.wait_ge(S["xs"], START + b + 1)
                for a in range(12):
                    if a >= 2:
                        k = min(a - 1, 8)
                        pe.wait_ge(S["qk"], START + 8 * b + k)
                        if a - 1 > 8:
                            pe.wait_ge(S["v"], START + 4 * b + a - 9)
                    if a < 2:
                        pe.wait_ge(S["pre_sb"], START + (BTILES - 1) * b)
                    sl = slice(a % 4 * SB, (a % 4 + 1) * SB)
                    if a < 8:
                        w = s.wb[:, HID:2 * HID] if a < 4 else s.wb[:, 0:HID]
                        ins = nc.tensor.matmul(pp[:, a % 2, :], w, xs[:, sl], start=True, stop=True)
                    else:
                        for t in range(SB_TILES):
                            g = a % 4 * SB_TILES + t
                            ins = nc.tensor.matmul(pp[:, a % 2, t * P:(t + 1) * P], xs[:, g * P:(g + 1) * P],
                                                   s.wb[:, 2 * HID:], start=True, stop=True)
                    ins.then_inc(S["proj"], 1)
                pe.wait_ge(S["qk"], START + 8 * (b + 1))

                def scores(g):
                    i, c, k0, n = chunk[g]
                    if g >= 2:
                        pe.wait_ge(S["copy"], START + NCH * b + g - 1)
                    nc.tensor.matmul(ps[:, g % 2, 0:n * P], qT[:, i * P:(i + 1) * P], kT[:, k0 * P:(k0 + n) * P],
                                     start=True, stop=True).then_inc(S["s"], 1)

                def turn(g):
                    i, c, k0, n = chunk[g]
                    pe.wait_ge(S["p"], START + NCH * b + g + 1)
                    pe.wait_ge(S["pt"], START + NCH * b + max(g - 1, 0))
                    for t in range(n):
                        ins = nc.tensor.transpose(pt[:, g % 2, t, :], U[:, g % UBUF, t * P:(t + 1) * P], s.ident[:, :])
                    ins.then_inc(S["t"], 1)

                def values(g):
                    i, c, k0, n = chunk[g]
                    pe.wait_ge(S["pt"], START + NCH * b + g + 1)
                    if c == 0:
                        pe.wait_ge(S["o"], START + BTILES * b + max(i - 1, 0))
                    for t in range(n):
                        ins = nc.tensor.matmul(po[:, i % 2, 0:HID + 1], pT[:, g % 2, t, :], V[:, k0 + t, :],
                                               start=(c == 0 and t == 0), stop=(k0 + t == BTILES - 1))
                    ins.then_inc(S["pv"], 1)

                for g in range(AHEAD):
                    scores(g)
                pe.wait_ge(S["v"], START + 4 * (b + 1))
                for g in range(NCH):
                    turn(g)
                    if g + AHEAD < NCH:
                        scores(g + AHEAD)
                    if g > 0:
                        values(g - 1)
                    i, c, _, _ = chunk[g]
                    if c == 0 and i > 0:
                        pe.wait_ge(S["pre_sb"], START + (BTILES - 1) * b + max(i - 2, 0))
                        nc.tensor.matmul(pp[:, i % 2, 0:HID + 1], s.ones[:, :], V[:, i - 1, :], start=True,
                                         stop=True).then_inc(S["pre"], 1)
                values(NCH - 1)

        @block.scalar
        def _(act):
            with act.Fori(0, BATCH) as b:
                for a in range(8):
                    act.wait_ge(S["proj"], START + 12 * b + a + 1)
                    if a == 0:
                        act.wait_ge(S["pv"], START + NCH * b)
                    sl = slice(a % 4 * SB, (a % 4 + 1) * SB)
                    if a < 4:
                        ins = nc.scalar.copy(kT[:, sl], pp[:, a % 2, :])
                    else:
                        ins = nc.scalar.mul(qT[:, sl], pp[:, a % 2, :], float(HID) ** -0.5 / MASKED)
                    ins.then_inc(S["qk"], 1)

                def copy(g):
                    i, c, k0, n = chunk[g]
                    act.wait_ge(S["s"], START + NCH * b + g + 1)
                    if g >= UBUF:
                        act.wait_ge(S["t"], START + NCH * b + g - UBUF + 1)
                    nc.scalar.copy(U[:, g % UBUF, 0:n * P], ps[:, g % 2, 0:n * P]).then_inc(S["copy"], 1)

                def exponentials(g):
                    i, c, k0, n = chunk[g]
                    bias = st[:, i % UBUF, 1:2]
                    if c == 0:
                        act.wait_ge(S["bias"], START + BTILES * b + i + 1)
                        nc.scalar.activation(st[:, i % UBUF, 2:3], s.ones[:, 0:1], ACT.Exp, scale=-MASKED,
                                             bias=bias).then_inc(S["w0"], 1)
                    sl = U[:, g % UBUF, 0:n * P]
                    nc.scalar.activation(sl, sl, ACT.Exp, scale=-MASKED, bias=bias).then_inc(S["p"], 1)

                def read(g):
                    n = chunk[g][3]
                    act.wait_ge(S["t"], START + NCH * b + g + 1)
                    if g >= 2:
                        act.wait_ge(S["pv"], START + NCH * b + g - 1)
                    nc.scalar.copy(pT[:, g % 2, 0:n, :], pt[:, g % 2, 0:n, :]).then_inc(S["pt"], 1)

                for g in range(AHEAD - 1):
                    copy(g)
                exponentials(0)
                for g in range(NCH):
                    if g + AHEAD - 1 < NCH:
                        copy(g + AHEAD - 1)
                    if g + 1 < NCH:
                        exponentials(g + 1)
                    read(g)

        @block.vector
        def _(dve):
            ch = Chain(dve, S["chain"])
            nc.vector.memset(V[:, :, HID:], 1.0)
            dve.wait_ge(S["tri"], START + 2)
            with dve.Fori(0, BATCH) as b:
                ch.enter(0, b, MARKS)
                dve.wait_ge(S["proj"], START + 12 * b)
                nc.vector.tensor_copy(xs[:, :], s.xT[:, bass.ts(b, SEQ)]).then_inc(S["xs"], 1)
                for a in range(8, 12):
                    dve.wait_ge(S["proj"], START + 12 * b + a + 1)
                    if a == 8:
                        dve.wait_ge(S["pv"], START + NCH * b)
                        dve.wait_ge(S["pre"], START + (BTILES - 1) * b)
                    g = a % 4 * SB_TILES
                    nc.vector.tensor_copy(V[:, g:g + SB_TILES, 0:HID],
                                          pp[:, a % 2, :].rearrange("p (t d) -> p t d", t=SB_TILES)).then_inc(S["v"], 1)

                def take(g):
                    i, c, k0, n = chunk[g]
                    if c == 0 and i >= UBUF:
                        dve.wait_ge(S["p"], START + NCH * b + first[i - UBUF + 1])
                    dve.wait_ge(S["copy"], START + NCH * b + g + 1)
                    to = U[:, g % UBUF, 0:n * P]
                    if c == 0:
                        ch.link(nc.vector.tensor_tensor(to[:, 0:P], to[:, 0:P], tri[:, :], ALU.mult))
                    nc.vector.scalar_tensor_tensor(to, to, 0.0, to, ALU.is_equal, ALU.subtract).then_inc(S["u"], 1)
                    dve.wait_ge(S["u"], START + NCH * b + g + 1)
                    ch.mark(nc.vector.tensor_reduce(mn[:, i % UBUF, c:c + 1], to, AX_X, ALU.min))
                    if c == len(chunks[i]) - 1:
                        ch.wait()
                        ch.link(nc.vector.tensor_reduce(st[:, i % UBUF, 0:1], mn[:, i % UBUF, 0:c + 1], AX_X, ALU.min))
                        nc.vector.tensor_scalar(st[:, i % UBUF, 1:2], st[:, i % UBUF, 0:1], MASKED, None,
                                                ALU.mult).then_inc(S["bias"], 1)

                def finish(i):
                    if i > 0:
                        dve.wait_ge(S["pre"], START + (BTILES - 1) * b + i)
                        if i == 1:
                            nc.vector.tensor_copy(pre[:, :], pp[:, i % 2, 0:HID + 1]).then_inc(S["pre_sb"], 1)
                        else:
                            nc.vector.tensor_tensor(pre[:, :], pre[:, :], pp[:, i % 2, 0:HID + 1],
                                                    ALU.add).then_inc(S["pre_sb"], 1)
                        dve.wait_ge(S["pre_sb"], START + (BTILES - 1) * b + i)
                    dve.wait_ge(S["pv"], START + NCH * b + first[i + 1])
                    if i > 0:
                        dve.wait_ge(S["w0"], START + BTILES * b + i + 1)
                        ins = nc.vector.scalar_tensor_tensor(oo[:, :], pre[:, :], st[:, i % UBUF, 2:3],
                                                             po[:, i % 2, 0:HID + 1], ALU.mult, ALU.add)
                    else:
                        ins = nc.vector.tensor_copy(oo[:, :], po[:, 0, 0:HID + 1])
                    ins.then_inc(S["o"], 1)
                    dve.wait_ge(S["o"], START + BTILES * b + i + 1)
                    ch.link(nc.vector.reciprocal(st[:, i % UBUF, 3:4], oo[:, HID:]))
                    own = s.x[:, b * BTILES + i, :]
                    ch.mark(nc.vector.scalar_tensor_tensor(own, oo[:, 0:HID], st[:, i % UBUF, 3:4], own,
                                                           ALU.mult, ALU.add))

                for g in range(AHEAD - 1):
                    take(g)
                for g in range(NCH):
                    if g + AHEAD - 1 < NCH:
                        take(g + AHEAD - 1)
                    if g >= 2 and chunk[g - 2][0] != chunk[g - 1][0]:
                        finish(chunk[g - 2][0])
                for i in range(chunk[NCH - 2][0], BTILES):
                    finish(i)
                assert ch.n == MARKS

        @block.gpsimd
        def _(pool):
            nc.gpsimd.memset(tri[:, :], 1.0).then_inc(S["tri"], 1)
            pool.wait_ge(S["tri"], START + 1)
            nc.gpsimd.affine_select(out=tri[:, :], in_=tri[:, :], compare_op=ALU.is_ge, fill=0.0, base=0,
                                    pattern=[[1, P]], channel_multiplier=-1).then_inc(S["tri"], 1)


CONSTS = 2


class Shared:
    pass


def bass_hybrid(nc, hidden, wq, wk, wv, wo, bq, bk, bv, bo4, wb, w_router, w1, b1, w2, b2, cos, sin, out):
    with ExitStack() as ctx:
        m = Memory(nc, ctx)
        s = Shared()
        s.padded = m.sb("x", [P, SB_TILES + TILES, HID])
        s.x = s.padded[:, SB_TILES:, :]
        s.xT = m.sb("xT", [P, TILES * P])
        s.xn = s.xT[:, :].rearrange("p (t d) -> p t d", d=HID)
        s.pick = m.sb("pick", [P, TILES, TOPK])
        s.slot = m.sb("slot", [P, TOPK, TILES], U32)
        s.yslot = m.sb("yslot", [P, TOPK, TILES], U32)
        s.emap = m.sb("emap", [P, GROUPS], I32)
        s.gmap = m.sb("gmap", [P, GROUPS], I32)
        s.groupno = m.sb("groupno", [P, GROUPS])
        s.base = m.sb("base", [P, EXPERTS])
        s.before = m.sb("before", [P, P])
        s.xg = nc.dram_tensor("xg", [XBLOCKS, GROUP, HID], F32, kind="Internal").ap()
        s.yg = nc.dram_tensor("yg", [GROUPS, GROUP, HID], F32, kind="Internal").ap()
        s.split = False
        s.b1 = m.sb("b1", [P, EXPERTS * HCHUNKS])
        s.b2 = m.sb("b2", [P, EXPERTS])
        s.w_router = m.sb("w_router", [P, EXPERTS])
        s.wb = m.sb("wb", [P, 3 * HID])
        s.ident = m.sb("ident", [P, P])
        s.ones = m.sb("ones", [P, P])
        s.iota = m.sb("iota", [P, EXPERTS])
        s.bq, s.bk, s.bv = (m.sb(n, [P, CHUNKS]) for n in ("bq", "bk", "bv"))
        s.bo4 = m.sb("bo4", [1, SB])
        s.s_x = [m.sem(f"s_x{i}") for i in range(NSB // 2)]
        s.s_const, s.s_small, s.s_wqkvo, s.s_rope, s.s_late, s_out = (
            m.sem(n) for n in "s_const s_small s_wqkvo s_rope s_late s_out".split())
        s.s_passed = m.sem("s_passed")
        s.signals = {stage: {n: m.sem(f"{stage}_{n}") for n in names.split()} for stage, names in SIGNALS.items()}
        small = [(s.bq, bq), (s.bk, bk), (s.bv, bv), (s.bo4, bo4), (s.b1, b1), (s.b2, b2), (s.w_router, w_router)]
        s.n_small = len(small)
        s.s_zero, s.s_zeroed, s.s_count, s.s_mask = (m.sem(n) for n in ("s_zero", "s_zeroed", "s_count", "s_mask"))

        with ExitStack() as actx:
            a = Memory(nc, actx)
            s.wv, s.wo = (a.sb(n, [P, CHUNKS, P]) for n in ("wv", "wo"))
            s.wqh, s.wql, s.wkh, s.wkl = (a.sb(n, [P, CHUNKS, P], F32R) for n in ("wqh", "wql", "wkh", "wkl"))
            s.lin, s.rot = (a.sb(n, [P, 2, SB]) for n in ("lin", "rot"))
            s.wq, s.wk = (x[:, :, :].rearrange("p a (b c) -> p (a b) c", c=P) for x in (s.lin, s.rot))
            s.K = [a.sb(n, [P, CHUNKS, P + SB], F32R) for n in ("Kh", "Kl")]
            s.V = a.sb("V", [P, CHUNKS, 1 + SB_TILES, 2, VCOLS])
            s.mask = a.sb("mask", [P, 2 * P])
            s.masks = a.sb("masks", [P, SB_PER_BATCH, 2 * P])
            s.zeros = a.sb("zeros", [P, HID])
            number = a.sb("number", [P, GROUPS], I32)
            s.cos, s.sin = (a.sb(n, [P, SEQ]) for n in ("cos", "sin"))
            tokens = hidden.rearrange("b (t p) d -> p (b t) d", p=P)
            with nc.Block() as block:

                @block.sync
                def _(sp):
                    for i in range(NSB):
                        r = slice(i * SB_TILES, (i + 1) * SB_TILES)
                        sp.dma_start(s.x[:, r, :], tokens[:, r, :]).then_inc(s.s_x[i // 2], 16)
                    for to, of in ((s.cos, cos), (s.sin, sin)):
                        sp.dma_start(to[:, :], of).then_inc(s.s_rope, 16)
                    sp.dma_start(s.wb[:, :], wb).then_inc(s.s_late, 16)

                @block.tensor
                def _(pe):
                    for of_stage in s.signals.values():
                        for signal in of_stage.values():
                            pe.sem_inc(signal, START)

                @block.scalar
                def _(act):
                    for to, of in ((s.wq, wq), (s.wk, wk), (s.wv, wv), (s.wo, wo)):
                        act.dma_start(to[:, :, :], of).then_inc(s.s_wqkvo, 16)
                    for to, of in small:
                        act.dma_start(to[:, :], of).then_inc(s.s_small, 16)

                @block.gpsimd
                def _(pool):
                    nc.gpsimd.memset(s.ident[:, :], 0.0).then_inc(s.s_const, 1)
                    pool.wait_ge(s.s_const, 1)
                    nc.gpsimd.affine_select(out=s.ident[:, :], in_=s.ident[:, :], compare_op=ALU.not_equal,
                                            fill=1.0, base=0, pattern=[[-1, P]],
                                            channel_multiplier=1).then_inc(s.s_const, 1)
                    nc.gpsimd.memset(s.before[:, :], 1.0).then_inc(s.s_count, 1)
                    nc.gpsimd.iota(number[:, :], pattern=[[1, GROUPS]], base=0, channel_multiplier=0).then_inc(s.s_count, 1)
                    pool.wait_ge(s.s_count, 2)
                    nc.gpsimd.affine_select(out=s.before[:, :], in_=s.before[:, :], compare_op=ALU.is_gt, fill=0.0,
                                            base=0, pattern=[[1, P]], channel_multiplier=-1)
                    nc.gpsimd.tensor_copy(s.groupno[:, :], number[:, :])

                @block.vector
                def _(dve):
                    nc.vector.memset(s.zeros[:, :], 0.0).then_inc(s.s_zero, 1)
                    nc.vector.memset(s.ones[:, :], 1.0)
                    nc.vector.memset(s.padded[:, 0:SB_TILES, :], 0.0)
                    for e in range(EXPERTS):
                        nc.vector.memset(s.iota[:, e:e + 1], float(e))
                        nc.vector.memset(s.base[:, e:e + 1], float(e * BLOCKS * GROUP))
            norm_stage(nc, m, 0, s, first=True)
            window_stage(nc, m, s)
        s.w1 = m.sb("w1", [P, EXPERTS, FFN])
        s.w2 = m.sb("w2", [P, EXPERTS, HCHUNKS, HID])
        s.late = [(s.w1[:, :, :], w1.rearrange("e p f -> p e f")),
                  (s.w2[:, :, :, :], w2.rearrange("e (c p) d -> p e c d", p=P))]
        s.w1h = m.sb("w1h", [P, EXPERTS, FFN], F32R)
        norm_stage(nc, m, 1, s, router=True)
        s.split = True
        expert_stage(nc, m, 1, s)
        norm_stage(nc, m, 2, s, collect=True)
        full_stage(nc, m, s)
        norm_stage(nc, m, 3, s, router=True)
        expert_stage(nc, m, 3, s)
        last_stage(nc, m, s, out, s_out)


def last_stage(nc, sems, s, out, s_out):
    with ExitStack() as ctx:
        m = Memory(nc, ctx)
        got = m.sb("got", [P, TILES, TOPK, P])
        gathered = [sems.sem(f"l_got{i}") for i in range(TILES // PART)]
        S = s.signals["last"]
        tokens = out.rearrange("b (t p) d -> p (b t) d", p=P)
        block = ctx.enter_context(nc.Block())

        @block.gpsimd
        def _(pool):
            gather(nc, pool, s, got, gathered)

        @block.vector
        def _(dve):
            ch = Chain(dve, S["chain"])
            for i in range(NSB):
                combine(nc, ch, s, got, gathered, i)
                dve.sem_inc(S["sum"], 1)

        @block.sync
        def _(sp):
            for i in range(NSB):
                sp.wait_ge(S["sum"], START + i + 1)
                r = slice(i * SB_TILES, (i + 1) * SB_TILES)
                sp.dma_start(tokens[:, r, :], s.x[:, r, :]).then_inc(s_out, 16)
            sp.wait_ge(s_out, 16 * NSB)


def kernel(**inputs):
    import numpy as _np
    import concourse.bacc as _bacc
    from concourse import mybir as _mybir
    from concourse.bass_utils import run_bass_kernel_spmd as _run

    a = {k.removeprefix("L0_"): _np.asarray(v) for k, v in inputs.items()}
    w = _np.arange(P)
    feature = (w // HD) * HD + (w % HD) // 32 * 16 + _np.where(w % 32 < 16, w % 16, HD // 2 + w % 16)
    rows = (_np.arange(CHUNKS)[:, None] * P + feature[None, :]).reshape(-1)

    def transposed(x):
        return x.T.reshape(HID, CHUNKS, P)

    inv = (_np.float32(1.0) / _np.float32(10000.0) ** (_np.arange(0, HD, 2, dtype=_np.float32) / _np.float32(HD)))
    angle = (_np.arange(SEQ, dtype=_np.float32)[None, :] * inv.astype(_np.float32)[feature % 32][:, None])
    sign = _np.where(w % 32 < 16, -1.0, 1.0)[:, None]
    arrays = {
        "hidden": a["attn_a_hidden_states"],
        "wq": transposed(a["attn_a_Wq"][rows]), "wk": transposed(a["attn_a_Wk"][rows]),
        "wv": transposed(a["attn_a_Wv"]), "wo": a["attn_a_Wo"].T.reshape(CHUNKS, P, HID).transpose(1, 0, 2),
        "bq": a["attn_a_bq"][rows].reshape(CHUNKS, P).T, "bk": a["attn_a_bk"][rows].reshape(CHUNKS, P).T,
        "bv": a["attn_a_bv"].reshape(CHUNKS, P).T, "bo4": _np.tile(a["attn_a_bo"], SB_TILES)[None, :],
        "wb": a["attn_b_W"], "w_router": a["ffn_w_router"], "w1": a["ffn_w1"],
        "b1": a["ffn_b1"].reshape(EXPERTS * HCHUNKS, P).T, "w2": a["ffn_w2"], "b2": a["ffn_b2"].T,
        "cos": _np.cos(angle.astype(_np.float64)).astype(_np.float32),
        "sin": (sign * _np.sin(angle.astype(_np.float64))).astype(_np.float32),
    }
    arrays = {f"in_{k}": _np.ascontiguousarray(v) for k, v in arrays.items()}
    nc = _bacc.Bacc("TRN2", target_bir_lowering=False, num_devices=1)
    args = [nc.dram_tensor(k, v.shape, _mybir.dt.from_np(v.dtype), kind="ExternalInput").ap() for k, v in arrays.items()]
    out = nc.dram_tensor("out_x", (BATCH, SEQ, HID), F32, kind="ExternalOutput").ap()
    bass_hybrid(nc, *args, out)
    r = _run(nc, [arrays], core_ids=[0])
    return r.results[0]["out_x"]
```
